# Optimizing a Trainium2 kernel written in Bass

```python
import numpy as np
import jax
import jax.numpy as jnp

def _softmax(x, axis=-1):
    return jax.nn.softmax(x, axis=axis)

def _gelu(x):
    return jax.nn.gelu(x, approximate=True)

def _silu(x):
    return jax.nn.silu(x)

def _sigmoid(x):
    return jax.nn.sigmoid(x)

def _layernorm(x, axis=-1, eps=1e-05):
    m = jnp.mean(x, axis=axis, keepdims=True)
    v = jnp.var(x, axis=axis, keepdims=True)
    return (x - m) / jnp.sqrt(v + eps)

def _scatter_add(tgt, idx, src, axis=0):
    return tgt.at[idx].add(src)

def _segment_sum(src, seg, n):
    return jax.ops.segment_sum(src, seg, n)
kernel_name = 'mk_adaln_d2_jaxref_r8_ba4956'

def setup_inputs(seed: int=0):
    np.random.seed(seed)
    _w = jnp.asarray

    def _L0_attn_setup():
        import jax, jax.numpy as jnp
        import numpy as np
        THETA = 10000.0
        EPS = 1e-06
        N_HEADS = 16

        def apply_rope(x):
            b, h, l, d = x.shape
            inv_freq = 1.0 / THETA ** (jnp.arange(0, d, 2, dtype=jnp.float32) / d)
            t = jnp.arange(l, dtype=jnp.float32)
            freqs = t[:, None] * inv_freq[None, :]
            cos = jnp.cos(freqs)[None, None]
            sin = jnp.sin(freqs)[None, None]
            x1 = x[..., 0::2]
            x2 = x[..., 1::2]
            out = jnp.stack([x1 * cos - x2 * sin, x1 * sin + x2 * cos], axis=-1)
            return out.reshape(b, h, l, d)
        key = jax.random.key(seed)
        ks = jax.random.split(key, 5)
        dim = 128
        b, l = (1, 256)
        scale = 1.0 / np.sqrt(dim)
        return {'x': jax.random.normal(ks[0], (b, l, dim), dtype=jnp.float32), 'wq': jax.random.normal(ks[1], (dim, dim), dtype=jnp.float32) * scale, 'wk': jax.random.normal(ks[2], (dim, dim), dtype=jnp.float32) * scale, 'wv': jax.random.normal(ks[3], (dim, dim), dtype=jnp.float32) * scale, 'wo': jax.random.normal(ks[4], (dim, dim), dtype=jnp.float32) * scale}
    _L0_attn_in = _L0_attn_setup()

    def _L0_ffn_setup():
        import jax, jax.numpy as jnp
        import numpy as np
        S, B, D, H, DH = (512, 8, 128, 16, 64)

        def _forward(x, Wg, Wq, bq, Wkv, bkv, Wo, bo, ln_g, ln_b):
            s_len, bsz, d_model = x.shape
            n_head, _, d_head = Wq.shape
            cap = s_len // n_head
            scale = 1.0 / d_head ** 0.5
            h = jnp.transpose(x, (1, 0, 2))
            t = h
            probs = jax.nn.softmax(h @ Wg, axis=-1)
            scores = jnp.transpose(probs, (0, 2, 1))
            _, idx = jax.lax.top_k(scores, cap)
            idx = jnp.sort(idx, axis=-1)
            hg = jnp.take_along_axis(h[:, None, :, :], idx[..., None], axis=2)
            hg = jnp.transpose(hg, (1, 0, 2, 3))
            q = jnp.einsum('hbcd,hde->hbce', hg, Wq) + bq[:, None, None, :]
            kv = jnp.einsum('hbcd,hde->hbce', hg, Wkv) + bkv[:, None, None, :]
            k, v = jnp.split(kv, 2, axis=-1)
            att = jnp.einsum('hbid,hbjd->hbij', q, k) * scale
            p = jax.nn.softmax(att, axis=1)
            av = jnp.einsum('hbij,hbjd->hbid', p, v)
            ao = jnp.einsum('hbid,hde->hbie', av, Wo) + bo
            tok = jnp.transpose(idx, (1, 0, 2))
            b_ids = jnp.arange(bsz)[None, :, None]
            outs = jnp.zeros_like(t).at[b_ids, tok].add(ao)
            y = t + outs
            mu = jnp.mean(y, axis=-1, keepdims=True)
            var = jnp.var(y, axis=-1, keepdims=True)
            yn = (y - mu) * jax.lax.rsqrt(var + 1e-05) * ln_g + ln_b
            return jnp.transpose(yn, (1, 0, 2))
        key = jax.random.key(seed)
        ks = jax.random.split(key, 6)
        s = 0.02
        return {'x': jax.random.normal(ks[0], (S, B, D), jnp.float32), 'attn_mask': jnp.zeros((S, S), jnp.bool_), 'Wg': jax.random.normal(ks[1], (D, H), jnp.float32) * s, 'Wq': jax.random.normal(ks[2], (H, D, DH), jnp.float32) * s, 'bq': jnp.zeros((H, DH), jnp.float32), 'Wkv': jax.random.normal(ks[3], (H, D, 2 * DH), jnp.float32) * s, 'bkv': jnp.zeros((H, 2 * DH), jnp.float32), 'Wo': jax.random.normal(ks[4], (H, DH, D), jnp.float32) * s, 'bo': jnp.zeros((D,), jnp.float32), 'ln_g': jnp.ones((D,), jnp.float32), 'ln_b': jnp.zeros((D,), jnp.float32)}
    _L0_ffn_in = _L0_ffn_setup()
    _L0_c = _w((lambda *s: np.random.randn(*s).astype(np.float32) * 0.05)(8, 128))
    _L0_wmod = _w((lambda *s: np.random.randn(*s).astype(np.float32) * 0.05)(128, 6 * 128) * 128 ** (-0.5))

    def _L1_attn_setup():
        import jax, jax.numpy as jnp
        import numpy as np
        HEADS = 64
        DIM_HEAD = 64
        SCALE = DIM_HEAD ** (-0.5)
        EPS = 1e-06
        key = jax.random.key(seed)
        ks = jax.random.split(key, 6)
        b, s, dim = (2, 512, 128)
        inner = HEADS * DIM_HEAD
        std = 0.02
        return {'x': jax.random.normal(ks[0], (b, s, dim), dtype=jnp.float32), 'Wq': jax.random.normal(ks[1], (dim, inner), dtype=jnp.float32) * std, 'Wk': jax.random.normal(ks[2], (dim, inner), dtype=jnp.float32) * std, 'Wv': jax.random.normal(ks[3], (dim, inner), dtype=jnp.float32) * std, 'Wo': jax.random.normal(ks[4], (inner, dim), dtype=jnp.float32) * std, 'bo': jnp.zeros((dim,), dtype=jnp.float32)}
    _L1_attn_in = _L1_attn_setup()

    def _L1_ffn_setup():
        import jax, jax.numpy as jnp
        import numpy as np
        D = 128
        H = 4
        HD = D // H
        E = 8
        FF = 512
        CAP_FACTOR = 1.0

        def _ln(x, g, b, eps=1e-05):
            mu = jnp.mean(x, -1, keepdims=True)
            v = jnp.mean((x - mu) ** 2, -1, keepdims=True)
            return (x - mu) * jax.lax.rsqrt(v + eps) * g + b

        def _mha(x, w, b, ow, ob):
            L, N, _ = x.shape
            qkv = x @ w.T + b
            q, k, v = jnp.split(qkv, 3, axis=-1)
            rh = lambda t: t.reshape(L, N, H, HD).transpose(1, 2, 0, 3)
            q, k, v = (rh(q), rh(k), rh(v))
            scores = jnp.einsum('nhld,nhmd->nhlm', q, k) / np.float32(np.sqrt(HD))
            attn = jax.nn.softmax(scores, axis=-1)
            o = jnp.einsum('nhlm,nhmd->nhld', attn, v).transpose(2, 0, 1, 3).reshape(L, N, D)
            return o @ ow.T + ob

        def _moe(x, wg, w1, b1, w2, b2):
            L, N, _ = x.shape
            S = L * N
            cap = int(CAP_FACTOR * S) // E
            xf = x.reshape(S, D)
            gates = jax.nn.softmax(xf @ wg, axis=-1)
            idx = jnp.argmax(gates, axis=-1)
            mask1 = jax.nn.one_hot(idx, E, dtype=x.dtype)
            loc = jnp.sum((jnp.cumsum(mask1, 0) - 1.0) * mask1, -1).astype(jnp.int32)
            keep = loc < cap
            gate_val = jnp.take_along_axis(gates, idx[:, None], -1)[:, 0]
            slot = jnp.where(keep, idx.astype(jnp.int32) * cap + loc, E * cap)
            disp = jnp.zeros((E * cap, D), x.dtype).at[slot].set(xf, mode='drop')
            disp = disp.reshape(E, cap, D)
            h = jnp.einsum('ecd,edf->ecf', disp, w1) + b1[:, None, :]
            y = (jnp.einsum('ecf,efd->ecd', h, w2) + b2[:, None, :]).reshape(E * cap, D)
            out = jnp.where(keep[:, None], gate_val[:, None] * y[jnp.minimum(slot, E * cap - 1)], 0.0)
            return out.reshape(L, N, D)
        key = jax.random.key(seed)
        ks = jax.random.split(key, 8)
        L, N = (128, 16)
        s = 0.02
        return {'x': jax.random.normal(ks[0], (L, N, D), jnp.float32), 'in_proj_w': jax.random.normal(ks[1], (3 * D, D), jnp.float32) * s, 'in_proj_b': jnp.zeros((3 * D,), jnp.float32), 'out_proj_w': jax.random.normal(ks[2], (D, D), jnp.float32) * s, 'out_proj_b': jnp.zeros((D,), jnp.float32), 'ln1_g': jnp.ones((D,), jnp.float32), 'ln1_b': jnp.zeros((D,), jnp.float32), 'ln2_g': jnp.ones((D,), jnp.float32), 'ln2_b': jnp.zeros((D,), jnp.float32), 'wg': jax.random.normal(ks[3], (D, E), jnp.float32) * s, 'w1': jax.random.normal(ks[4], (E, D, FF), jnp.float32) * s, 'b1': jnp.zeros((E, FF), jnp.float32), 'w2': jax.random.normal(ks[5], (E, FF, D), jnp.float32) * s, 'b2': jnp.zeros((E, D), jnp.float32)}
    _L1_ffn_in = _L1_ffn_setup()
    _L1_c = _w((lambda *s: np.random.randn(*s).astype(np.float32) * 0.05)(8, 128))
    _L1_wmod = _w((lambda *s: np.random.randn(*s).astype(np.float32) * 0.05)(128, 6 * 128) * 128 ** (-0.5))
    _d = {'L0_attn_x': _L0_attn_in['x'], 'L0_attn_wq': _L0_attn_in['wq'], 'L0_attn_wk': _L0_attn_in['wk'], 'L0_attn_wv': _L0_attn_in['wv'], 'L0_attn_wo': _L0_attn_in['wo'], 'L0_ffn_attn_mask': _L0_ffn_in['attn_mask'], 'L0_ffn_Wg': _L0_ffn_in['Wg'], 'L0_ffn_Wq': _L0_ffn_in['Wq'], 'L0_ffn_bq': _L0_ffn_in['bq'], 'L0_ffn_Wkv': _L0_ffn_in['Wkv'], 'L0_ffn_bkv': _L0_ffn_in['bkv'], 'L0_ffn_Wo': _L0_ffn_in['Wo'], 'L0_ffn_bo': _L0_ffn_in['bo'], 'L0_ffn_ln_g': _L0_ffn_in['ln_g'], 'L0_ffn_ln_b': _L0_ffn_in['ln_b'], 'L0_c': _L0_c, 'L0_wmod': _L0_wmod, 'L1_attn_Wq': _L1_attn_in['Wq'], 'L1_attn_Wk': _L1_attn_in['Wk'], 'L1_attn_Wv': _L1_attn_in['Wv'], 'L1_attn_Wo': _L1_attn_in['Wo'], 'L1_attn_bo': _L1_attn_in['bo'], 'L1_ffn_in_proj_w': _L1_ffn_in['in_proj_w'], 'L1_ffn_in_proj_b': _L1_ffn_in['in_proj_b'], 'L1_ffn_out_proj_w': _L1_ffn_in['out_proj_w'], 'L1_ffn_out_proj_b': _L1_ffn_in['out_proj_b'], 'L1_ffn_ln1_g': _L1_ffn_in['ln1_g'], 'L1_ffn_ln1_b': _L1_ffn_in['ln1_b'], 'L1_ffn_ln2_g': _L1_ffn_in['ln2_g'], 'L1_ffn_ln2_b': _L1_ffn_in['ln2_b'], 'L1_ffn_wg': _L1_ffn_in['wg'], 'L1_ffn_w1': _L1_ffn_in['w1'], 'L1_ffn_b1': _L1_ffn_in['b1'], 'L1_ffn_w2': _L1_ffn_in['w2'], 'L1_ffn_b2': _L1_ffn_in['b2'], 'L1_c': _L1_c, 'L1_wmod': _L1_wmod}
    _x0 = _d['L0_attn_x']
    _d['L0_attn_x'] = jax.random.normal(jax.random.fold_in(jax.random.key(seed), 1), (8, 1024, 128), dtype=_x0.dtype)
    del _x0
    return _d

def reference(L0_attn_x, L0_attn_wq, L0_attn_wk, L0_attn_wv, L0_attn_wo, L0_ffn_attn_mask, L0_ffn_Wg, L0_ffn_Wq, L0_ffn_bq, L0_ffn_Wkv, L0_ffn_bkv, L0_ffn_Wo, L0_ffn_bo, L0_ffn_ln_g, L0_ffn_ln_b, L0_c, L0_wmod, L1_attn_Wq, L1_attn_Wk, L1_attn_Wv, L1_attn_Wo, L1_attn_bo, L1_ffn_in_proj_w, L1_ffn_in_proj_b, L1_ffn_out_proj_w, L1_ffn_out_proj_b, L1_ffn_ln1_g, L1_ffn_ln1_b, L1_ffn_ln2_g, L1_ffn_ln2_b, L1_ffn_wg, L1_ffn_w1, L1_ffn_b1, L1_ffn_w2, L1_ffn_b2, L1_c, L1_wmod):

    def _L0_attn_ref(x, wq, wk, wv, wo):
        import jax, jax.numpy as jnp
        import numpy as np
        THETA = 10000.0
        EPS = 1e-06
        N_HEADS = 16

        def apply_rope(x):
            b, h, l, d = x.shape
            inv_freq = 1.0 / THETA ** (jnp.arange(0, d, 2, dtype=jnp.float32) / d)
            t = jnp.arange(l, dtype=jnp.float32)
            freqs = t[:, None] * inv_freq[None, :]
            cos = jnp.cos(freqs)[None, None]
            sin = jnp.sin(freqs)[None, None]
            x1 = x[..., 0::2]
            x2 = x[..., 1::2]
            out = jnp.stack([x1 * cos - x2 * sin, x1 * sin + x2 * cos], axis=-1)
            return out.reshape(b, h, l, d)
        b, l, dim = x.shape
        h = N_HEADS
        d = dim // h
        q = (x @ wq).reshape(b, l, h, d)
        k = (x @ wk).reshape(b, l, h, d)
        v = (x @ wv).reshape(b, l, h, d)
        q = apply_rope(q.transpose(0, 2, 1, 3)).transpose(0, 2, 1, 3)
        k = apply_rope(k.transpose(0, 2, 1, 3)).transpose(0, 2, 1, 3)
        Q = jax.nn.relu(q)
        K = jax.nn.relu(k)
        kv_state = jnp.einsum('blhd,blhm->blhdm', K, v)
        kv_cumsum = jnp.cumsum(kv_state, axis=1)
        k_cumsum = jnp.cumsum(K, axis=1)
        numerator = jnp.einsum('blhd,blhdm->blhm', Q, kv_cumsum)
        denominator = jnp.einsum('blhd,blhd->blh', Q, k_cumsum)[..., None]
        out = numerator / (denominator + EPS)
        out = out.reshape(b, l, dim)
        return out @ wo

    def _L0_ffn_ref(x, attn_mask, Wg, Wq, bq, Wkv, bkv, Wo, bo, ln_g, ln_b):
        import jax, jax.numpy as jnp
        import numpy as np
        S, B, D, H, DH = (512, 8, 128, 16, 64)

        def _forward(x, Wg, Wq, bq, Wkv, bkv, Wo, bo, ln_g, ln_b):
            s_len, bsz, d_model = x.shape
            n_head, _, d_head = Wq.shape
            cap = s_len // n_head
            scale = 1.0 / d_head ** 0.5
            h = jnp.transpose(x, (1, 0, 2))
            t = h
            probs = jax.nn.softmax(h @ Wg, axis=-1)
            scores = jnp.transpose(probs, (0, 2, 1))
            _, idx = jax.lax.top_k(scores, cap)
            idx = jnp.sort(idx, axis=-1)
            hg = jnp.take_along_axis(h[:, None, :, :], idx[..., None], axis=2)
            hg = jnp.transpose(hg, (1, 0, 2, 3))
            q = jnp.einsum('hbcd,hde->hbce', hg, Wq) + bq[:, None, None, :]
            kv = jnp.einsum('hbcd,hde->hbce', hg, Wkv) + bkv[:, None, None, :]
            k, v = jnp.split(kv, 2, axis=-1)
            att = jnp.einsum('hbid,hbjd->hbij', q, k) * scale
            p = jax.nn.softmax(att, axis=1)
            av = jnp.einsum('hbij,hbjd->hbid', p, v)
            ao = jnp.einsum('hbid,hde->hbie', av, Wo) + bo
            tok = jnp.transpose(idx, (1, 0, 2))
            b_ids = jnp.arange(bsz)[None, :, None]
            outs = jnp.zeros_like(t).at[b_ids, tok].add(ao)
            y = t + outs
            mu = jnp.mean(y, axis=-1, keepdims=True)
            var = jnp.var(y, axis=-1, keepdims=True)
            yn = (y - mu) * jax.lax.rsqrt(var + 1e-05) * ln_g + ln_b
            return jnp.transpose(yn, (1, 0, 2))
        return _forward(x, Wg, Wq, bq, Wkv, bkv, Wo, bo, ln_g, ln_b)

    def _L1_attn_ref(x, Wq, Wk, Wv, Wo, bo):
        import jax, jax.numpy as jnp
        import numpy as np
        HEADS = 64
        DIM_HEAD = 64
        SCALE = DIM_HEAD ** (-0.5)
        EPS = 1e-06
        b, s, dim = x.shape
        h, dh = (HEADS, DIM_HEAD)
        q = (x @ Wq).reshape(b, s, h, dh)
        k = (x @ Wk).reshape(b, s, h, dh)
        v = (x @ Wv).reshape(b, s, h, dh)
        q = jax.nn.relu(q) * SCALE
        k = jax.nn.relu(k)
        kv = jnp.einsum('bsid,bsjd->bsdj', k, v)
        out = jnp.einsum('bsid,bsdj->bsij', q, kv)
        q_norm = jnp.einsum('bsid,bsd->bsi', q, k.sum(axis=2))
        out = out / (q_norm[..., None] + EPS)
        out = out.reshape(b, s, h * h)
        return out @ Wo + bo

    def _L1_ffn_ref(x, in_proj_w, in_proj_b, out_proj_w, out_proj_b, ln1_g, ln1_b, ln2_g, ln2_b, wg, w1, b1, w2, b2):
        import jax, jax.numpy as jnp
        import numpy as np
        D = 128
        H = 4
        HD = D // H
        E = 8
        FF = 512
        CAP_FACTOR = 1.0

        def _ln(x, g, b, eps=1e-05):
            mu = jnp.mean(x, -1, keepdims=True)
            v = jnp.mean((x - mu) ** 2, -1, keepdims=True)
            return (x - mu) * jax.lax.rsqrt(v + eps) * g + b

        def _mha(x, w, b, ow, ob):
            L, N, _ = x.shape
            qkv = x @ w.T + b
            q, k, v = jnp.split(qkv, 3, axis=-1)
            rh = lambda t: t.reshape(L, N, H, HD).transpose(1, 2, 0, 3)
            q, k, v = (rh(q), rh(k), rh(v))
            scores = jnp.einsum('nhld,nhmd->nhlm', q, k) / np.float32(np.sqrt(HD))
            attn = jax.nn.softmax(scores, axis=-1)
            o = jnp.einsum('nhlm,nhmd->nhld', attn, v).transpose(2, 0, 1, 3).reshape(L, N, D)
            return o @ ow.T + ob

        def _moe(x, wg, w1, b1, w2, b2):
            L, N, _ = x.shape
            S = L * N
            cap = int(CAP_FACTOR * S) // E
            xf = x.reshape(S, D)
            gates = jax.nn.softmax(xf @ wg, axis=-1)
            idx = jnp.argmax(gates, axis=-1)
            mask1 = jax.nn.one_hot(idx, E, dtype=x.dtype)
            loc = jnp.sum((jnp.cumsum(mask1, 0) - 1.0) * mask1, -1).astype(jnp.int32)
            keep = loc < cap
            gate_val = jnp.take_along_axis(gates, idx[:, None], -1)[:, 0]
            slot = jnp.where(keep, idx.astype(jnp.int32) * cap + loc, E * cap)
            disp = jnp.zeros((E * cap, D), x.dtype).at[slot].set(xf, mode='drop')
            disp = disp.reshape(E, cap, D)
            h = jnp.einsum('ecd,edf->ecf', disp, w1) + b1[:, None, :]
            y = (jnp.einsum('ecf,efd->ecd', h, w2) + b2[:, None, :]).reshape(E * cap, D)
            out = jnp.where(keep[:, None], gate_val[:, None] * y[jnp.minimum(slot, E * cap - 1)], 0.0)
            return out.reshape(L, N, D)
        y1 = _ln(x + _mha(x, in_proj_w, in_proj_b, out_proj_w, out_proj_b), ln1_g, ln1_b)
        y2 = _ln(y1 + _moe(y1, wg, w1, b1, w2, b2), ln2_g, ln2_b)
        return y2
    x = L0_attn_x
    mod = (_silu(L0_c) @ L0_wmod).reshape(L0_c.shape[0], 6, 1, -1)
    sa, ca, ga, sb, cb, gb = (mod[:, 0], mod[:, 1], mod[:, 2], mod[:, 3], mod[:, 4], mod[:, 5])
    ga = (2 * (ga >= 0) - 1) * jnp.maximum(jnp.abs(ga), 0.25)
    gb = (2 * (gb >= 0) - 1) * jnp.maximum(jnp.abs(gb), 0.25)
    h = _layernorm(x, axis=-1) * (1 + ca) + sa
    x = x + ga * _L0_attn_ref(h, L0_attn_wq, L0_attn_wk, L0_attn_wv, L0_attn_wo)
    h = _layernorm(x, axis=-1) * (1 + cb) + sb
    x = x + gb * _L0_ffn_ref(h, L0_ffn_attn_mask, L0_ffn_Wg, L0_ffn_Wq, L0_ffn_bq, L0_ffn_Wkv, L0_ffn_bkv, L0_ffn_Wo, L0_ffn_bo, L0_ffn_ln_g, L0_ffn_ln_b)
    mod = (_silu(L1_c) @ L1_wmod).reshape(L1_c.shape[0], 6, 1, -1)
    sa, ca, ga, sb, cb, gb = (mod[:, 0], mod[:, 1], mod[:, 2], mod[:, 3], mod[:, 4], mod[:, 5])
    ga = (2 * (ga >= 0) - 1) * jnp.maximum(jnp.abs(ga), 0.25)
    gb = (2 * (gb >= 0) - 1) * jnp.maximum(jnp.abs(gb), 0.25)
    h = _layernorm(x, axis=-1) * (1 + ca) + sa
    x = x + ga * _L1_attn_ref(h, L1_attn_Wq, L1_attn_Wk, L1_attn_Wv, L1_attn_Wo, L1_attn_bo)
    h = _layernorm(x, axis=-1) * (1 + cb) + sb
    x = x + gb * _L1_ffn_ref(h, L1_ffn_in_proj_w, L1_ffn_in_proj_b, L1_ffn_out_proj_w, L1_ffn_out_proj_b, L1_ffn_ln1_g, L1_ffn_ln1_b, L1_ffn_ln2_g, L1_ffn_ln2_b, L1_ffn_wg, L1_ffn_w1, L1_ffn_b1, L1_ffn_w2, L1_ffn_b2)
    return x

_drawn_inputs = setup_inputs


def setup_inputs(seed=0):
    import zlib

    import numpy as np

    out = dict(_drawn_inputs(seed))
    spreads = {'L0_ffn_bq': (0.0, 0.1),
     'L0_ffn_bkv': (0.0, 0.1),
     'L0_ffn_bo': (0.0, 0.1),
     'L0_ffn_ln_g': (1.0, 0.2),
     'L0_ffn_ln_b': (0.0, 0.353),
     'L1_attn_bo': (0.0, 0.348),
     'L1_ffn_in_proj_b': (0.0, 0.8),
     'L1_ffn_out_proj_b': (0.0, 0.332),
     'L1_ffn_ln1_g': (1.0, 0.2),
     'L1_ffn_ln1_b': (0.0, 0.332),
     'L1_ffn_ln2_g': (1.0, 0.2),
     'L1_ffn_ln2_b': (0.0, 0.32),
     'L1_ffn_b1': (0.0, 0.8),
     'L1_ffn_b2': (0.0, 2.0)}
    factors = {'L0_attn_wq': 3.353,
     'L0_attn_wk': 2.773,
     'L1_attn_Wq': 4.32,
     'L1_attn_Wk': 8.0,
     'L1_attn_Wv': 3.577,
     'L1_attn_Wo': 3.558,
     'L1_ffn_in_proj_w': 8.0,
     'L1_ffn_out_proj_w': 7.764,
     'L1_ffn_wg': 8.0,
     'L1_ffn_w1': 8.0,
     'L1_ffn_w2': 8.0}
    for name, (base, spread) in spreads.items():
        noise = np.random.default_rng([zlib.crc32(name.encode()), seed]).standard_normal(out[name].shape)
        drawn = base * np.exp(spread * noise) if base else spread * noise
        out[name] = jnp.asarray(drawn.astype(out[name].dtype))
    for name, factor in factors.items():
        out[name] = (out[name] * factor).astype(out[name].dtype)
    return out
```

```python
from contextlib import ExitStack

import numpy as np

import concourse.bass as bass
from concourse import mybir

F32 = mybir.dt.float32
F32R = mybir.dt.float32r
ALU = mybir.AluOpType
ACT = mybir.ActivationFunctionType
AX = mybir.AxisListType

P = 128
B, L, D = 8, 1024, 128
SEG = P // B
TILES = B * L // P
PAIRS = TILES // 2
EPS_LN = 1e-5
EPS_ATT = 1e-6

H0, D0 = 16, 8
V0 = D0 + 1
HEADS_OF_BANK = (6, 5, 5)

(M0_SHIFT, M0_SCALE, M0_GATE, M0_SHIFT2, M0_SCALE2, M0_GAIN2, M0_BIAS2, M1_SHIFT, M1_SCALE, M1_GATE,
 M1_BIAS, M1_SHIFT2, M1_SCALE2, M1_GAIN2, M1_BIAS2, M_COUNT) = range(16)

_row = np.arange(P)
_batch, _pos = _row // SEG, _row % SEG
_same = _batch[:, None] == _batch[None, :]
IDENT = np.eye(P, dtype=np.float32)
UPTO = (_same & (_pos[:, None] <= _pos[None, :])).astype(np.float32)
SAME_BATCH = _same.astype(np.float32)
LAST_OF_BATCH = (_same & (_pos[:, None] == SEG - 1)).astype(np.float32)
BATCH_BEFORE = (_batch[:, None] < _batch[None, :]).astype(np.float32)
FOLD = (_row[:, None] % 64 == _row[None, :] % 64).astype(np.float32)
OTHER_POSITION = np.where(_pos[:, None] == _pos[None, :], 0.0, -1e30).astype(np.float32)


def rope_tables():
    inv = (1.0 / np.float32(10000.0) ** (np.arange(0, D0, 2, dtype=np.float32) / np.float32(D0))).astype(np.float32)
    at = (np.arange(TILES)[None, :] * SEG + _pos[:, None]).astype(np.float32)
    angle = (at[:, :, None] * inv[None, None, :]).astype(np.float32)
    cos, sin = np.cos(angle).astype(np.float32), np.sin(angle).astype(np.float32)
    return np.repeat(cos, 2, axis=2), np.stack([-sin, sin], axis=3).reshape(P, TILES, D0)


def tiles_of(x):
    return x.rearrange("l (j n) d -> j l n d", n=SEG)


class Scope:

    def __init__(self, nc):
        self.nc, self.stack = nc, ExitStack()

    def sb(self, name, shape, dt=F32):
        return self.stack.enter_context(self.nc.sbuf_tensor(name, shape, dt))

    def psum(self, name, shape, dt=F32):
        return self.stack.enter_context(self.nc.psum_tensor(name, shape, dt))

    def sem(self, name):
        return self.stack.enter_context(self.nc.semaphore(name))


class Signal:

    def __init__(self, scope, name, ahead=0):
        self.sem, self.ahead = scope.sem(name), ahead

    def give_ahead(self, engine):
        engine.sem_inc(self.sem, self.ahead)

    def mark(self, instruction, by=1):
        instruction.then_inc(self.sem, by)

    def wait(self, engine, count):
        engine.wait_ge(self.sem, count + self.ahead)


def in_rounds(eng, ring, body):
    with eng.Fori(0, PAIRS // ring - 1) as i:
        for b in range(ring):
            body(i, b)
    for b in range(ring):
        body(PAIRS // ring - 1, b)


class Chain:

    def __init__(self, engine, sem, per_round):
        self.engine, self.sem, self.per_round, self.base, self.n = engine, sem, per_round, 0, 0

    def start(self, rnd, first=0):
        self.base, self.n = rnd * self.per_round + first, 0

    def then(self, instruction):
        self.n += 1
        instruction.then_inc(self.sem, 1)
        self.engine.wait_ge(self.sem, self.base + self.n)


def settle(engine, settled):
    engine.sem_inc(settled, 1)


def modulation(nc, L0_c, L0_wmod, L0_ln_g, L0_ln_b, L1_c, L1_wmod, L1_bo, L1_ln2_g, L1_ln2_b, mods):
    s = Scope(nc)
    with s.stack:
        cT = s.sb("mod_cT", [P, 2, B])
        wmod = s.sb("mod_w", [P, 2, 6 * D])
        rows = s.sb("mod_rows", [P, 5, D])
        cneg = s.sb("mod_exp", [P, 2, B])
        den = s.sb("mod_den", [P, 2, B])
        rden = s.sb("mod_rden", [P, 2, B])
        silu = s.sb("mod_silu", [P, 2, B])
        silu_rows = s.sb("mod_silu_rows", [P, 2, P])
        size = s.sb("mod_size", [P, 2, 2, D])
        sign = s.sb("mod_sign", [P, 2, 2, D])
        gate = s.sb("mod_gate", [P, 2, 2, D])
        tile = s.sb("mod_tiles", [P, M_COUNT, D])
        mod_ps = s.psum("mod_ps", [P, 4, 512])
        loaded, exp_done, silu_done, mod_done = s.sem("mod_loaded"), s.sem("mod_exp_done"), s.sem("mod_silu_done"), s.sem("mod_done")
        steps, tiles_done, stored = s.sem("mod_steps"), s.sem("mod_tiles_done"), s.sem("mod_stored")
        with nc.Block() as block:

            @block.sync
            def _(sp):
                for layer, (c, w) in enumerate(((L0_c, L0_wmod), (L1_c, L1_wmod))):
                    sp.dma_start(cT[:, layer, :], c).then_inc(loaded, 16)
                    sp.dma_start(wmod[:, layer, :], w).then_inc(loaded, 16)
                for n, row in enumerate((L0_ln_g, L0_ln_b, L1_bo, L1_ln2_g, L1_ln2_b)):
                    sp.dma_start(rows[:, n, :], row.rearrange("(a d) -> a d", a=1).to_broadcast([P, D])).then_inc(loaded, 16)
                sp.wait_ge(tiles_done, 1)
                sp.dma_start(mods.rearrange("m p d -> p m d"), tile[:, 0:M_COUNT, :]).then_inc(stored, 16)
                sp.wait_ge(stored, 16)

            @block.scalar
            def _(act):
                act.wait_ge(loaded, 9 * 16)
                act.activation(cneg[:, :, :], cT[:, :, :], ACT.Exp, scale=-1.0).then_inc(exp_done, 1)

            @block.tensor
            def _(pe):
                pe.wait_ge(silu_done, 1)
                for layer in range(2):
                    for half, width in ((0, 512), (1, 256)):
                        last = pe.matmul(mod_ps[:, 2 * layer + half, 0:width], silu_rows[:, layer, :],
                                         wmod[:, layer, 512 * half:512 * half + width], start=True, stop=True)
                last.then_inc(mod_done, 1)

            @block.vector
            def _(dve):
                link = Chain(dve, steps, 5)
                link.start(0)
                dve.wait_ge(exp_done, 1)
                link.then(dve.tensor_scalar(den[:, :, :], cneg[:, :, :], 1.0, None, ALU.add))
                link.then(dve.reciprocal(rden[:, :, :], den[:, :, :]))
                link.then(dve.tensor_tensor(silu[:, :, :], cT[:, :, :], rden[:, :, :], ALU.mult))
                for layer in range(2):
                    last = dve.tensor_copy(silu_rows[:, layer, :].rearrange("p (l n) -> p l n", n=SEG),
                                           silu[:, layer, :].unsqueeze(2).to_broadcast([P, B, SEG]))
                last.then_inc(silu_done, 1)
                dve.wait_ge(mod_done, 1)

                def part(layer, k):
                    return mod_ps[:, 2 * layer + k // 4, (k % 4) * D:(k % 4) * D + D]

                for layer, (shift, scale, shift2, scale2) in enumerate(
                        ((M0_SHIFT, M0_SCALE, M0_SHIFT2, M0_SCALE2), (M1_SHIFT, M1_SCALE, M1_SHIFT2, M1_SCALE2))):
                    dve.tensor_copy(tile[:, shift, :], part(layer, 0))
                    dve.tensor_scalar(tile[:, scale, :], part(layer, 1), 1.0, None, ALU.add)
                    dve.tensor_copy(tile[:, shift2, :], part(layer, 3))
                    dve.tensor_scalar(tile[:, scale2, :], part(layer, 4), 1.0, None, ALU.add)
                    for g, k in enumerate((2, 5)):
                        last = dve.tensor_scalar(sign[:, layer, g, :], part(layer, k), 0.0, 2.0, ALU.is_ge, ALU.mult)
                link.then(last)
                link.then(dve.tensor_scalar(sign[:, :, :, :], sign[:, :, :, :], -1.0, None, ALU.add))
                for layer in range(2):
                    for g, k in enumerate((2, 5)):
                        last = dve.tensor_tensor(size[:, layer, g, :], sign[:, layer, g, :], part(layer, k), ALU.mult)
                link.then(last)
                link.then(dve.scalar_tensor_tensor(gate[:, :, :, :], size[:, :, :, :], 0.25, sign[:, :, :, :], ALU.max, ALU.mult))
                dve.tensor_copy(tile[:, M0_GATE, :], gate[:, 0, 0, :])
                dve.tensor_copy(tile[:, M1_GATE, :], gate[:, 1, 0, :])
                dve.tensor_tensor(tile[:, M0_GAIN2, :], gate[:, 0, 1, :], rows[:, 0, :], ALU.mult)
                dve.tensor_tensor(tile[:, M0_BIAS2, :], gate[:, 0, 1, :], rows[:, 1, :], ALU.mult)
                dve.tensor_tensor(tile[:, M1_BIAS, :], gate[:, 1, 0, :], rows[:, 2, :], ALU.mult)
                dve.tensor_tensor(tile[:, M1_GAIN2, :], gate[:, 1, 1, :], rows[:, 3, :], ALU.mult)
                dve.tensor_tensor(tile[:, M1_BIAS2, :], gate[:, 1, 1, :], rows[:, 4, :],
                                  ALU.mult).then_inc(tiles_done, 1)


def layer0(nc, x, wqkv, wo, mods, ident, upto, last_of_batch, cos2, sin2, out):
    s = Scope(nc)
    x_t, out_t = tiles_of(x), tiles_of(out)
    RING = 4
    with s.stack:
        sb = s.sb
        consts = sb("l0_mods", [P, 7, D])
        wqkv_sb, wo_sb = sb("l0_wqkv", [P, 3 * D]), sb("l0_wo", [P, D])
        ident_sb, upto_sb, last_sb = sb("l0_ident", [P, P]), sb("l0_upto", [P, P]), sb("l0_last", [P, P])
        cos_sb, sin_sb = sb("l0_cos", [P, TILES, D0]), sb("l0_sin", [P, TILES, D0])
        eps = sb("l0_eps", [P, 1])
        xin = sb("l0_x", [P, RING, 2, D])
        x1, normed, y = sb("l0_x1", [P, 2, D]), sb("l0_normed", [P, 2, D]), sb("l0_y", [P, 2, 2, D])
        stats, mv = sb("l0_stats", [P, 2, 6]), sb("l0_mean_var", [P, 3, 2, 2])
        std, rstd = sb("l0_std", [P, 3, 2]), sb("l0_rstd", [P, 2])
        h, hT = sb("l0_h", [P, 2, D]), sb("l0_hT", [P, 2, P])
        raw = sb("l0_raw", [P, 2, 2 * D])
        straight, turned = sb("l0_straight", [P, 2, 2 * D]), sb("l0_turned", [P, 2, 2 * D])
        rotated = sb("l0_rotated", [P, 2, 2 * D])
        qk = sb("l0_qk", [P, 2, 2, 2 * D])
        v1 = sb("l0_v1", [P, 2, H0, V0])
        kv = sb("l0_kv", [P, 2, H0, D0, V0])
        cum = sb("l0_cum", [P, 2, H0, D0, V0])
        prod = sb("l0_prod", [P, H0, D0, V0])
        nd = sb("l0_numden", [P, 2, H0, V0])
        den, rden = sb("l0_den", [P, 2, H0]), sb("l0_rden", [P, 2, H0])
        o, oT = sb("l0_o", [P, 2, D]), sb("l0_oT", [P, 2, P])
        hT_ps, oT_ps, y_ps = s.psum("l0_hT_ps", [P, 2, 256]), s.psum("l0_oT_ps", [P, 2, 256]), s.psum("l0_y_ps", [P, 2, 256])
        proj_ps, cum_ps = s.psum("l0_proj_ps", [P, 2, 512]), s.psum("l0_cum_ps", [P, 3, 512])

        loaded, ready = s.sem("l0_loaded"), s.sem("l0_ready")
        settled = s.sem("l0_settled")
        x_in = [Signal(s, f"l0_x_in{k}") for k in range(RING)]
        y_stored = [Signal(s, f"l0_y_stored{k}", 32) for k in range(2)]
        dve_steps = s.sem("l0_dve_steps")
        mv_done = [Signal(s, f"l0_mv_done{k}") for k in range(3)]
        std_done = [Signal(s, f"l0_std_done{k}") for k in range(3)]
        h_done, hT_ps_done, hT_done = Signal(s, "l0_h_done"), Signal(s, "l0_hT_ps_done", 1), Signal(s, "l0_hT_done")
        proj_done, raw_done = Signal(s, "l0_proj_done", 1), Signal(s, "l0_raw_done", 1)
        straight_done, rotated_done, qk_done = Signal(s, "l0_straight_done"), Signal(s, "l0_rotated_done", 1), Signal(s, "l0_qk_done", 1)
        kv_done, cum_ps_done, cum_done, cum_read = (Signal(s, "l0_kv_done", 2), Signal(s, "l0_cum_ps_done", 6),
                                                    Signal(s, "l0_cum_done", 3), Signal(s, "l0_cum_read", 2))
        o_done, oT_ps_done, oT_done = Signal(s, "l0_o_done"), Signal(s, "l0_oT_ps_done", 1), Signal(s, "l0_oT_done")
        y_ps_done, x1_done, y_done = Signal(s, "l0_y_ps_done", 1), Signal(s, "l0_x1_done", 2), Signal(s, "l0_y_done")

        LOADS = 8
        BANKS = len(HEADS_OF_BANK)
        first = [sum(HEADS_OF_BANK[:k]) for k in range(BANKS)]

        def bank(k):
            return slice(first[k], first[k] + HEADS_OF_BANK[k]), HEADS_OF_BANK[k] * D0 * V0

        def mod(k):
            return consts[:, k, :].unsqueeze(1).to_broadcast([P, 2, D])

        def is_pair(i, b):
            return not isinstance(i, int) or i * RING + b < PAIRS

        with nc.Block() as block:

            @block.sync
            def _(sp):
                for dst, src in ((consts[:, :, :], mods[0:7].rearrange("m p d -> p m d")),
                                 (wqkv_sb[:, :], wqkv), (wo_sb[:, :], wo), (ident_sb[:, :], ident),
                                 (upto_sb[:, :], upto), (last_sb[:, :], last_of_batch), (cos_sb[:, :, :], cos2),
                                 (sin_sb[:, :, :], sin2)):
                    sp.dma_start(dst, src).then_inc(loaded, 16)
                for k in range(2):
                    y_stored[k].give_ahead(sp)

                def load(n, slot):
                    for t in range(2):
                        x_in[slot].mark(sp.dma_start(xin[:, slot, t, :], x_t[n * 2 + t]), 16)

                load(0, 0)
                load(1, 1)

                def body(i, b):
                    n = i * RING + b
                    if is_pair(i, b + 2):
                        x1_done.wait(sp, n - 1)
                        load(n + 2, (b + 2) % RING)
                    y_done.wait(sp, n + 1)
                    for t in range(2):
                        y_stored[b % 2].mark(sp.dma_start(out_t[n * 2 + t], y[:, b % 2, t, :]), 16)

                in_rounds(sp, RING, body)
                for k in range(2):
                    y_stored[k].wait(sp, PAIRS // 2 * 32)

            @block.gpsimd
            def _(pool):
                pool.memset(eps[:, :], EPS_LN)
                pool.memset(v1[:, :, :, :], 1.0)
                pool.memset(cum[:, 1], 0.0).then_inc(ready, 1)
                qk_done.give_ahead(pool)
                cum_ps_done.give_ahead(pool)
                rotated_done.give_ahead(pool)
                pool.wait_ge(loaded, LOADS * 16)

                def b1(n, par):
                    raw_done.wait(pool, n + 1)
                    rotated_done.wait(pool, n)
                    last = pool.tensor_tensor(
                        straight[:, :, :].rearrange("p t (g d) -> p t g d", d=D0),
                        raw[:, :, :].rearrange("p t (g d) -> p t g d", d=D0),
                        cos_sb[:, bass.ds(n * 2, 2), :].unsqueeze(2).to_broadcast([P, 2, 2 * H0, D0]), ALU.mult)
                    straight_done.mark(last)
                    qk_done.wait(pool, n + 1)
                    for t in range(2):
                        cum_ps_done.wait(pool, 6 * (n - 1) + 3 * t + 3)
                        k = qk[:, par, t, D:2 * D].rearrange("p (h d) -> p h d", d=D0)
                        kv_done.mark(pool.tensor_tensor(
                            kv[:, t], k.unsqueeze(3).to_broadcast([P, H0, D0, V0]),
                            v1[:, t].unsqueeze(2).to_broadcast([P, H0, D0, V0]), ALU.mult))

                b1(0, 0)
                in_rounds(pool, RING, lambda i, b: b1(i * RING + b + 1, (b + 1) % 2) if is_pair(i, b + 1) else None)

            @block.scalar
            def _(act):
                act.wait_ge(ready, 1)
                kv_done.give_ahead(act)
                cum_read.give_ahead(act)
                y_ps_done.give_ahead(act)

                def root(k, n):
                    mv_done[k].wait(act, n + 1)
                    std_done[k].mark(act.activation(std[:, k, :], mv[:, k, :, 1], ACT.Sqrt, bias=eps[:, 0:1]))

                def a(n):
                    root(0, n)
                    hT_ps_done.wait(act, n + 1)
                    proj_done.wait(act, n)
                    hT_done.mark(act.copy(hT[:, :, :], hT_ps[:, :, 0:P]))

                def b1(n, par):
                    proj_done.wait(act, n + 1)
                    rotated_done.wait(act, n)
                    kv_done.wait(act, 2 * n)
                    act.copy(raw[:, :, :], proj_ps[:, :, 0:2 * D])
                    raw_done.mark(act.copy(v1[:, :, :, 0:D0],
                                           proj_ps[:, :, 2 * D:3 * D].rearrange("p t (h d) -> p t h d", d=D0)))
                    rotated_done.wait(act, n + 1)
                    cum_read.wait(act, 2 * (n - 1))
                    qk_done.mark(act.activation(qk[:, par, :, :], rotated[:, :, :], ACT.Relu))

                def b2(n):
                    for t in range(2):
                        cum_read.wait(act, 2 * n + t - 1)
                        for k in range(BANKS):
                            heads, width = bank(k)
                            cum_ps_done.wait(act, 6 * n + 3 * t + k + 1)
                            cum_done.mark(act.copy(cum[:, t, heads].rearrange("p h d m -> p (h d m)"),
                                                   cum_ps[:, k, 0:width]))
                    oT_ps_done.wait(act, n + 1)
                    y_ps_done.wait(act, n)
                    oT_done.mark(act.copy(oT[:, :, :], oT_ps[:, :, 0:P]))

                a(0)
                a(1)
                b1(0, 0)

                def body(i, b):
                    n = i * RING + b
                    if is_pair(i, b + 1):
                        b1(n + 1, (b + 1) % 2)
                    b2(n)
                    if is_pair(i, b + 2):
                        a(n + 2)
                    root(1, n)
                    root(2, n)

                in_rounds(act, RING, body)

            @block.tensor
            def _(pe):
                pe.wait_ge(loaded, LOADS * 16)
                pe.wait_ge(ready, 1)
                cum_done.give_ahead(pe)
                raw_done.give_ahead(pe)
                x1_done.give_ahead(pe)
                oT_ps_done.give_ahead(pe)
                proj_done.give_ahead(pe)

                def turn(n):
                    h_done.wait(pe, n + 1)
                    if not isinstance(n, int) or n:
                        hT_done.wait(pe, n)
                    for t in range(2):
                        last = pe.transpose(hT_ps[:, t, 0:P], h[:, t, :], ident_sb[:, :])
                    hT_ps_done.mark(last)

                def project(n):
                    hT_done.wait(pe, n + 1)
                    raw_done.wait(pe, n)
                    for t in range(2):
                        last = pe.matmul(proj_ps[:, t, 0:3 * D], hT[:, t, :], wqkv_sb[:, :], start=True, stop=True)
                    proj_done.mark(last)

                for n in range(2):
                    turn(n)
                    project(n)

                def body(i, b):
                    n = i * RING + b
                    for t in range(2):
                        kv_done.wait(pe, 2 * n + t + 1)
                        for k in range(BANKS):
                            heads, width = bank(k)
                            cum_done.wait(pe, 6 * n + 3 * t + k - 3 + 1)
                            pe.matmul(cum_ps[:, k, 0:width], upto_sb[:, :],
                                      kv[:, t, heads].rearrange("p h d m -> p (h d m)"), start=True, stop=False)
                            cum_ps_done.mark(pe.matmul(
                                cum_ps[:, k, 0:width], last_sb[:, :],
                                cum[:, 1 - t, heads].rearrange("p h d m -> p (h d m)"), start=False, stop=True))
                    o_done.wait(pe, n + 1)
                    for t in range(2):
                        last = pe.transpose(oT_ps[:, t, 0:P], o[:, t, :], ident_sb[:, :])
                    oT_ps_done.mark(last)
                    if is_pair(i, b + 2):
                        turn(n + 2)
                    oT_done.wait(pe, n + 1)
                    x1_done.wait(pe, n)
                    for t in range(2):
                        last = pe.matmul(y_ps[:, t, 0:D], oT[:, t, :], wo_sb[:, :], start=True, stop=True)
                    y_ps_done.mark(last)
                    if is_pair(i, b + 2):
                        project(n + 2)

                in_rounds(pe, RING, body)

            @block.vector
            def _(dve):
                dve.wait_ge(loaded, LOADS * 16)
                hT_ps_done.give_ahead(dve)
                link = Chain(dve, dve_steps, 0)

                step = link.then

                def stats_of(k, src):
                    for t in range(2):
                        last = dve.bn_stats(stats[:, t, :], src[:, t, :])
                    step(last)
                    settle(dve, settled)
                    for t in range(2):
                        last = dve.bn_aggr(mv[:, k, t, :], stats[:, t, :])
                    mv_done[k].mark(last)

                def normalise(k, n, dst, src):
                    std_done[k].wait(dve, n + 1)
                    step(dve.reciprocal(rstd[:, :], std[:, k, :]))
                    for t in range(2):
                        last = dve.tensor_scalar(dst[:, t, :], src[:, t, :], mv[:, k, t, 0:1], rstd[:, t:t + 1],
                                                 ALU.subtract, ALU.mult)
                    step(last)

                def a(n, cycle, ring):
                    x_in[ring].wait(dve, 32 * cycle + 32)
                    stats_of(0, xin[:, ring])
                    hT_ps_done.wait(dve, n)
                    normalise(0, n, h, xin[:, ring])
                    step(dve.tensor_tensor(h[:, :, :], h[:, :, :], mod(M0_SCALE), ALU.mult))
                    h_done.mark(dve.tensor_tensor(h[:, :, :], h[:, :, :], mod(M0_SHIFT), ALU.add))

                def b1(n):
                    raw_done.wait(dve, n + 1)
                    qk_done.wait(dve, n)
                    pairs = [a[:, :, :].rearrange("p t (g f e) -> p t g f e", f=D0 // 2, e=2) for a in (raw, turned)]
                    for t in range(2):
                        sin = sin_sb[:, bass.ds(n * 2 + t, 1), :].rearrange("p a (f e) -> p a f e", e=2)
                        for e in range(2):
                            last = dve.tensor_tensor(pairs[1][:, t, :, :, e], pairs[0][:, t, :, :, 1 - e],
                                                     sin[:, :, :, e].to_broadcast([P, 2 * H0, D0 // 2]), ALU.mult)
                    step(last)
                    straight_done.wait(dve, n + 1)
                    rotated_done.mark(dve.tensor_tensor(rotated[:, :, :], straight[:, :, :], turned[:, :, :], ALU.add))

                def b2(n, par):
                    for t in range(2):
                        cum_done.wait(dve, 6 * n + 3 * t + 3)
                        q = qk[:, par, t, 0:D].unsqueeze(2).to_broadcast([P, D, V0])
                        ins = dve.tensor_tensor(prod[:, :, :, :].rearrange("p h d m -> p (h d) m"),
                                                cum[:, t].rearrange("p h d m -> p (h d) m"), q, ALU.mult)
                        cum_read.mark(ins)
                        cum_read.wait(dve, 2 * n + t + 1)
                        step(dve.tensor_reduce(nd[:, t], prod[:, :, :, :].rearrange("p h d m -> p h m d"), AX.X, ALU.add))
                    step(dve.tensor_scalar(den[:, :, :], nd[:, :, :, D0], EPS_ATT, None, ALU.add))
                    step(dve.reciprocal(rden[:, :, :], den[:, :, :]))
                    oT_ps_done.wait(dve, n)
                    o_done.mark(dve.tensor_tensor(o[:, :, :].rearrange("p t (h d) -> p t h d", d=D0), nd[:, :, :, 0:D0],
                                                  rden[:, :, :].unsqueeze(3).to_broadcast([P, 2, H0, D0]), ALU.mult))

                def c(n, ring, uses):
                    y_ps_done.wait(dve, n + 1)
                    step(dve.tensor_tensor(x1[:, :, :], y_ps[:, :, 0:D], mod(M0_GATE), ALU.mult))
                    ins = dve.tensor_tensor(x1[:, :, :], x1[:, :, :], xin[:, ring], ALU.add)
                    x1_done.mark(ins)
                    x1_done.wait(dve, n + 1)
                    stats_of(1, x1)
                    normalise(1, n, normed, x1)
                    step(dve.tensor_tensor(normed[:, :, :], normed[:, :, :], mod(M0_SCALE2), ALU.mult))
                    step(dve.tensor_tensor(normed[:, :, :], normed[:, :, :], mod(M0_SHIFT2), ALU.add))
                    stats_of(2, normed)
                    normalise(2, n, normed, normed)
                    step(dve.tensor_tensor(normed[:, :, :], normed[:, :, :], mod(M0_GAIN2), ALU.mult))
                    step(dve.tensor_tensor(normed[:, :, :], normed[:, :, :], mod(M0_BIAS2), ALU.add))
                    y_stored[ring % 2].wait(dve, 32 * uses)
                    y_done.mark(dve.tensor_tensor(y[:, ring % 2], normed[:, :, :], x1[:, :, :], ALU.add))

                sizes = dict(a=4, b1=1, b2=4, c=11)
                per_round = sum(sizes.values())

                def stage(fn, at, *args):
                    link.base, link.n = at, 0
                    fn(*args)
                    assert link.n == sizes[fn.__name__], (fn.__name__, link.n)
                    return at + link.n

                head = stage(a, 0, 0, 0, 0)
                head = stage(a, head, 1, 0, 1)
                head = stage(b1, head, 0)
                at = head

                def body(i, b):
                    nonlocal at
                    n = i * RING + b
                    if b == 0:
                        at = n * per_round + head
                    if is_pair(i, b + 1):
                        at = stage(b1, at, n + 1)
                    at = stage(b2, at, n, b % 2)
                    if is_pair(i, b + 2):
                        at = stage(a, at, n + 2, i + (b + 2) // RING, (b + 2) % RING)
                    at = stage(c, at, n, b, i * (RING // 2) + b // 2)

                in_rounds(dve, RING, body)


def layer1_attention(nc, x, wq, wk, wv, wo, mods, ident, fold, out):
    s = Scope(nc)
    x_t, out_t = tiles_of(x), tiles_of(out)
    HEADS, DH = 64, 64
    HALF = P // 2
    TOK = 2 * P
    CHUNKS = HEADS * DH // P
    UNIT = 4
    UNITS = CHUNKS // UNIT
    SCALE = DH ** -0.5
    BATCHES = [7] * 4 + [6] * 6
    assert sum(BATCHES) == HALF
    NB = len(BATCHES)
    W = DH + 1
    PROJ = 2 * NB
    ORDER = [(w, u) for u in range(UNITS) for w in "kq"] + [("v", u) for u in range(UNITS)]
    ROUND = PROJ + len(ORDER)
    V_BY_DVE = [u for u in range(UNITS) if u % 2]
    V_BY_ACT = [u for u in range(UNITS) if u % 2 == 0]
    FOLD_AFTER = len(ORDER) - UNITS + 1

    def evacuates(engine, place):
        if place < PROJ:
            return True
        w, u = ORDER[place - PROJ]
        return (w == "q" or (w == "v" and u in V_BY_ACT)) == (engine == "act")

    def evacuated(engine, g, place):
        of = [evacuates(engine, p) for p in range(ROUND)]
        return g * sum(of) + sum(of[PROJ:]) + sum(of[:place + 1])

    with s.stack:
        sb = s.sb
        consts = sb("l1_mods", [P, 4, D])
        ident_sb, fold_sb = sb("l1_ident", [P, P]), sb("l1_fold", [P, P])
        w_hi = {w: sb(f"l1_w{w}_hi", [P, HEADS * DH], F32R) for w in "qkv"}
        w_lo = {w: sb(f"l1_w{w}_lo", [P, HEADS * DH], F32R) for w in "qkv"}
        wo_sb = sb("l1_wo", [P, CHUNKS, D])
        q = sb("l1_q", [P, P, HEADS])
        v = sb("l1_v", [P, P, W])
        att = sb("l1_att", [P, CHUNKS, P])
        ksum = sb("l1_ksum", [P, UNIT, TOK])
        ks = sb("l1_ks", [P, P])
        den_a, rden_a = sb("l1_den_a", [HALF, 8]), sb("l1_rden_a", [HALF, 8])
        den_b, rden_b = sb("l1_den_b", [P, 2, HALF]), sb("l1_rden_b", [P, 2, HALF])
        eps, eps_att = sb("l1_eps", [P, 1]), sb("l1_eps_att", [P, 1])
        xin, h = sb("l1_x", [P, 2, D]), sb("l1_h", [P, 2, D])
        xres, y = sb("l1_xres", [P, 2, D]), sb("l1_y", [P, 2, D])
        stats, mv = sb("l1_stats", [P, 2, 6]), sb("l1_mean_var", [P, 2, 2])
        std, rstd = sb("l1_std", [P, 2]), sb("l1_rstd", [P, 2])
        hT_hi, hT_lo = sb("l1_hT_hi", [P, 2, 2, HALF], F32R), sb("l1_hT_lo", [P, 2, 2, HALF], F32R)
        ring = s.psum("l1_ring", [P, 3, 2, 512])
        o_ps = s.psum("l1_o_ps", [P, 512])
        misc_ps = s.psum("l1_misc_ps", [P, 512])
        hT_ps, ks_ps = misc_ps[:, 0:TOK], misc_ps[:, TOK:2 * TOK]

        loaded, split_done, ready = s.sem("l1_loaded"), s.sem("l1_split_done"), s.sem("l1_ready")
        dve_steps = s.sem("l1_dve_steps")
        settled, pe_settled = s.sem("l1_settled"), s.sem("l1_pe_settled")
        x_in = Signal(s, "l1_x_in")
        y_stored = [Signal(s, f"l1_y_stored{k}", 16) for k in range(2)]
        unit_done = Signal(s, "l1_unit_done")
        evac = {"act": Signal(s, "l1_act_evac"), "dve": Signal(s, "l1_dve_evac")}
        mv_done, std_done, h_done = Signal(s, "l1_mv_done"), Signal(s, "l1_std_done"), Signal(s, "l1_h_done")
        hT_ps_done, hT_hi_done, hT_done = Signal(s, "l1_hT_ps_done", 1), Signal(s, "l1_hT_hi_done"), Signal(s, "l1_hT_done")
        ks_ps_done, ks_done = Signal(s, "l1_ks_ps_done"), Signal(s, "l1_ks_done")
        v_pool_done, rden_b_done, att_pool_done = Signal(s, "l1_v_pool_done"), Signal(s, "l1_rden_b_done"), Signal(s, "l1_att_pool_done")
        o_ps_done, y_done, xres_done = Signal(s, "l1_o_ps_done"), Signal(s, "l1_y_done", 2), Signal(s, "l1_xres_done")

        LOADS = 8

        def buffer(place):
            return ring[:, place % 3]

        def index(g, place):
            return g * ROUND + place + (ROUND - PROJ)

        def unit_ready(eng, g, place):
            unit_done.wait(eng, index(g, place) + 1)

        def wait_evacuated(eng, by, g, place):
            evac[by].wait(eng, evacuated(by, g, place))

        def place_of(w, u):
            return PROJ + ORDER.index((w, u))

        def rounds(eng, body, last):
            with eng.Fori(0, PAIRS - 1) as g:
                body(g)
            last(PAIRS - 1)

        def pieces(place):
            ps = buffer(place).rearrange("p a b -> p (a b)").rearrange("p (c t) -> p c t", t=TOK)
            for par in range(2):
                for ab in range(2):
                    yield par, ab, ps[HALF * par:HALF * par + HALF, :, P * ab:P * ab + P]

        def half(ab):
            return slice(HALF * ab, HALF * ab + HALF)

        def v_piece(u, par, ab):
            first = 32 * par + UNIT * u
            return v[half(ab), :, first:first + UNIT].rearrange("p t c -> p c t")

        def batch(k):
            return sum(BATCHES[:k]), BATCHES[k]

        def products(place, ab, m):
            return buffer(place)[half(ab), ab, 0:m * W].rearrange("p (t j) -> p t j", j=W)

        with nc.Block() as block:

            @block.sync
            def _(sp):
                sp.dma_start(q[:, 0:HALF, :].rearrange("p a b -> p (a b)"), wq).then_inc(loaded, 16)
                sp.dma_start(q[:, HALF:P, :].rearrange("p a b -> p (a b)"), wk).then_inc(loaded, 16)
                sp.dma_start(att[:, :, :].rearrange("p a b -> p (a b)"), wv).then_inc(loaded, 16)
                sp.dma_start(consts[:, :, :], mods[M1_SHIFT:M1_BIAS + 1].rearrange("m p d -> p m d")).then_inc(loaded, 16)
                sp.dma_start(ident_sb[:, :], ident).then_inc(loaded, 16)
                sp.dma_start(fold_sb[:, :], fold).then_inc(loaded, 16)
                for par in range(2):
                    sp.dma_start(wo_sb[half(par), :, :],
                                 wo.rearrange("(i c q) e -> q i c e", i=HEADS, q=2)[par]).then_inc(loaded, 16)

                def load(g):
                    for t in range(2):
                        x_in.mark(sp.dma_start(xin[:, t, :], x_t[g * 2 + t]), 16)

                for k in range(2):
                    y_stored[k].give_ahead(sp)

                def store(g):
                    for t in range(2):
                        y_done.wait(sp, 2 * g + t + 1)
                        y_stored[t].mark(sp.dma_start(out_t[g * 2 + t], y[:, t, :]), 16)

                load(0)

                def body(g):
                    xres_done.wait(sp, g + 1)
                    load(g + 1)
                    store(g)

                rounds(sp, body, store)
                for k in range(2):
                    y_stored[k].wait(sp, PAIRS * 16)

            @block.gpsimd
            def _(pool):
                pool.memset(eps[:, :], EPS_LN)
                pool.memset(eps_att[:, :], EPS_ATT).then_inc(ready, 1)
                y_done.give_ahead(pool)
                hT_ps_done.give_ahead(pool)
                pool.wait_ge(loaded, LOADS * 16)

                def scale_v(g):
                    ks_done.wait(pool, g + 2)
                    for u in V_BY_ACT:
                        wait_evacuated(pool, "act", g, place_of("v", u))
                        part = v[:, :, 0:DH].rearrange("p t (q c) -> p t q c", q=2)[:, :, :, UNIT * u:UNIT * u + UNIT]
                        last = pool.tensor_tensor(part, part, ks[:, :].unsqueeze(2).unsqueeze(3).to_broadcast([P, P, 2, UNIT]), ALU.mult)
                    v_pool_done.mark(last)

                def residual(g):
                    x_in.wait(pool, 32 * g + 32)
                    h_done.wait(pool, g + 1)
                    y_done.wait(pool, 2 * g)
                    xres_done.mark(pool.tensor_tensor(
                        xres[:, :, :], xin[:, :, :], consts[:, 3, :].unsqueeze(1).to_broadcast([P, 2, D]), ALU.add))

                def scale_att(g, sub):
                    for k in range(NB):
                        t0, m = batch(k)
                        rden_b_done.wait(pool, NB * (2 * g + sub) + k + 1)
                        part = att[:, :, HALF + t0:HALF + t0 + m].rearrange("p c t -> p t c")
                        last = pool.tensor_tensor(
                            part, part, rden_b[:, sub, t0:t0 + m].unsqueeze(2).to_broadcast([P, m, CHUNKS]), ALU.mult)
                    att_pool_done.mark(last)

                def body(g):
                    residual(g)
                    scale_att(g, 0)
                    scale_att(g, 1)

                def loop(g):
                    body(g)
                    scale_v(g)

                scale_v(-1)
                rounds(pool, loop, body)

            @block.scalar
            def _(act):
                act.wait_ge(ready, 1)
                act.wait_ge(split_done, 2)

                def prepare(g):
                    mv_done.wait(act, g + 1)
                    std_done.mark(act.activation(std[:, :], mv[:, :, 1], ACT.Sqrt, bias=eps[:, 0:1]))
                    hT_ps_done.wait(act, g + 1)
                    hT_hi_done.mark(act.copy(hT_hi[:, :, :, :].rearrange("p a s t -> p s a t"),
                                             hT_ps.rearrange("p (s a t) -> p s a t", s=2, a=2)))

                def project(g):
                    for n, (w, u) in enumerate(ORDER):
                        place = PROJ + n
                        if w == "q":
                            unit_ready(act, g, place)
                            for par, ab, ps in pieces(place):
                                dst = q[half(ab), :, 2 * UNIT * u + par:2 * UNIT * (u + 1):2].rearrange("p t c -> p c t")
                                last = act.activation(dst, ps, ACT.Relu, scale=SCALE)
                            evac["act"].mark(last)
                        elif w == "v":
                            if u in V_BY_ACT:
                                unit_ready(act, g, place)
                                for par, ab, ps in pieces(place):
                                    last = act.copy(v_piece(u, par, ab), ps)
                                evac["act"].mark(last)
                            if u == V_BY_ACT[0]:
                                ks_ps_done.wait(act, g + 2)
                                for ab in range(2):
                                    src = ks_ps[half(ab), P * ab:P * ab + P]
                                    act.copy(v[half(ab), :, DH], src)
                                    last = act.copy(ks[half(ab), :], src)
                                ks_done.mark(last)

                def attend(g, sub):
                    for k in range(NB):
                        t0, m = batch(k)
                        place = NB * sub + k
                        unit_ready(act, g, place)
                        ps = products(place, 1, m)
                        for par in range(2):
                            act.activation(den_b[half(par), sub, t0:t0 + m], ps[:, :, DH], ACT.Identity,
                                           bias=eps_att[half(1), 0:1])
                            last = act.copy(att[half(par), :, HALF + t0:HALF + t0 + m].rearrange("p c t -> p t c"),
                                            ps[:, :, CHUNKS * par:CHUNKS * par + CHUNKS])
                        evac["act"].mark(last)

                prepare(0)
                project(-1)

                def body(g):
                    attend(g, 0)
                    prepare(g + 1)
                    attend(g, 1)
                    project(g)

                def last(g):
                    attend(g, 0)
                    attend(g, 1)

                rounds(act, body, last)

            @block.tensor
            def _(pe):
                pe.wait_ge(loaded, LOADS * 16)
                pe.wait_ge(split_done, 2)

                def acquire(g, place):
                    if isinstance(g, int) and g == -1 and place - 3 < PROJ:
                        return
                    if place >= 3:
                        user = place - 3
                    else:
                        user = max(p for p in range(ROUND) if p % 3 == place)
                        g = g - 1
                    for by in evac:
                        if evacuates(by, user):
                            wait_evacuated(pe, by, g, user)

                def turn(g):
                    h_done.wait(pe, g + 1)
                    if not isinstance(g, int) or g:
                        hT_done.wait(pe, g)
                    for t in range(2):
                        last = pe.transpose(hT_ps[:, t * P:t * P + P], h[:, t, :], ident_sb[:, :])
                    hT_ps_done.mark(last)

                def project(g):
                    hT_done.wait(pe, g + 2)
                    hi, lo = (a[:, :, :, :].rearrange("p a s t -> p (a s t)") for a in (hT_hi, hT_lo))
                    for n, (w, u) in enumerate(ORDER):
                        if n == FOLD_AFTER:
                            wait_evacuated(pe, "dve", g, place_of("k", UNITS - 1))
                            for k in range(UNIT):
                                last = pe.matmul(ks_ps, fold_sb[:, :], ksum[:, k, :], start=k == 0, stop=k == UNIT - 1)
                            ks_ps_done.mark(last)
                        place = PROJ + n
                        acquire(g, place)
                        ps = buffer(place).rearrange("p a b -> p (a b)").rearrange("p (c t) -> p c t", t=TOK)
                        for c in range(UNIT):
                            cols = slice((UNIT * u + c) * P, (UNIT * u + c) * P + P)
                            pe.matmul(ps[:, c], w_hi[w][:, cols], hi, start=True, stop=False)
                            pe.matmul(ps[:, c], w_hi[w][:, cols], lo, start=False, stop=False)
                            last = pe.matmul(ps[:, c], w_lo[w][:, cols], hi, start=False, stop=True)
                        unit_done.mark(last)

                def attend(g, sub):
                    if sub == 0:
                        v_pool_done.wait(pe, g + 1)
                        wait_evacuated(pe, "dve", g - 1, place_of("v", V_BY_DVE[-1]))
                    for k in range(NB):
                        t0, m = batch(k)
                        place = NB * sub + k
                        acquire(g, place)
                        settle(pe, pe_settled)
                        for t in range(m):
                            tok = HALF * sub + t0 + t
                            for ab in range(2):
                                last = pe.matmul(products(place, ab, m)[:, t], q[half(ab), tok, :], v[half(ab), tok, :],
                                                 start=True, stop=True)
                        unit_done.mark(last)

                def output(g, sub):
                    wait_evacuated(pe, "dve", g, NB * sub + NB - 1)
                    att_pool_done.wait(pe, 2 * g + sub + 1)
                    y_done.wait(pe, 2 * g + sub)
                    for c in range(CHUNKS):
                        last = pe.matmul(o_ps[:, 0:D], att[:, c, :], wo_sb[:, c, :], start=c == 0, stop=c == CHUNKS - 1)
                    o_ps_done.mark(last)

                turn(0)
                project(-1)

                def body(g):
                    attend(g, 0)
                    output(g, 0)
                    turn(g + 1)
                    attend(g, 1)
                    project(g)
                    output(g, 1)

                def last(g):
                    for sub in range(2):
                        attend(g, sub)
                        output(g, sub)

                rounds(pe, body, last)

            @block.vector
            def _(dve):
                dve.wait_ge(loaded, LOADS * 16)
                for w, src in (("q", q[:, 0:HALF, :]), ("k", q[:, HALF:P, :]), ("v", att[:, :, :])):
                    src = src.rearrange("p a b -> p (a b)")
                    last = dve.tensor_copy(w_hi[w][:, :], src)
                last.then_inc(split_done, 1)
                dve.wait_ge(split_done, 1)
                for w, src in (("q", q[:, 0:HALF, :]), ("k", q[:, HALF:P, :]), ("v", att[:, :, :])):
                    src = src.rearrange("p a b -> p (a b)")
                    last = dve.tensor_tensor(w_lo[w][:, :], src, w_hi[w][:, :].bitcast(F32), ALU.subtract)
                last.then_inc(split_done, 1)
                link = Chain(dve, dve_steps, 0)
                step = link.then

                def mod(k):
                    return consts[:, k, :].unsqueeze(1).to_broadcast([P, 2, D])

                def prepare(g):
                    x_in.wait(dve, 32 * g + 32)
                    for t in range(2):
                        last = dve.bn_stats(stats[:, t, :], xin[:, t, :])
                    step(last)
                    settle(dve, settled)
                    for t in range(2):
                        last = dve.bn_aggr(mv[:, t, :], stats[:, t, :])
                    mv_done.mark(last)
                    std_done.wait(dve, g + 1)
                    step(dve.reciprocal(rstd[:, :], std[:, :]))
                    hT_ps_done.wait(dve, g)
                    for t in range(2):
                        last = dve.tensor_scalar(h[:, t, :], xin[:, t, :], mv[:, t, 0:1], rstd[:, t:t + 1],
                                                 ALU.subtract, ALU.mult)
                    step(last)
                    step(dve.tensor_tensor(h[:, :, :], h[:, :, :], mod(1), ALU.mult))
                    h_done.mark(dve.tensor_tensor(h[:, :, :], h[:, :, :], mod(0), ALU.add))

                def rest(g):
                    hT_hi_done.wait(dve, g + 1)
                    hT_done.mark(dve.tensor_tensor(hT_lo[:, :, :, :].rearrange("p a s t -> p s a t"),
                                                   hT_ps.rearrange("p (s a t) -> p s a t", s=2, a=2),
                                                   hT_hi[:, :, :, :].bitcast(F32).rearrange("p a s t -> p s a t"), ALU.subtract))

                def project(g):
                    for n, (w, u) in enumerate(ORDER):
                        place = PROJ + n
                        if w == "k":
                            unit_ready(dve, g, place)
                            ps = buffer(place).rearrange("p a b -> p (a b)")
                            acc = ksum[:, :, :].rearrange("p c t -> p (c t)")
                            if u == 0:
                                last = dve.tensor_scalar(acc, ps, 0.0, None, ALU.max)
                            else:
                                wait_evacuated(dve, "dve", g, place_of("k", u - 1))
                                last = dve.scalar_tensor_tensor(acc, ps, 0.0, acc, ALU.max, ALU.add)
                            evac["dve"].mark(last)
                        elif w == "v" and u in V_BY_DVE:
                            if u == V_BY_DVE[0]:
                                ks_done.wait(dve, g + 2)
                            unit_ready(dve, g, place)
                            for par, ab, ps in pieces(place):
                                last = dve.tensor_tensor(v_piece(u, par, ab), ps,
                                                         ks[half(ab), :].unsqueeze(1).to_broadcast([HALF, UNIT, P]), ALU.mult)
                            evac["dve"].mark(last)

                def attend(g, sub):
                    for k in range(NB):
                        t0, m = batch(k)
                        place = NB * sub + k
                        unit_ready(dve, g, place)
                        ps = products(place, 0, m)
                        step(dve.tensor_scalar(den_a[:, 0:m], ps[:, :, DH], EPS_ATT, None, ALU.add))
                        step(dve.reciprocal(rden_a[:, 0:m], den_a[:, 0:m]))
                        for par in range(2):
                            last = dve.tensor_tensor(
                                att[half(par), :, t0:t0 + m].rearrange("p c t -> p t c"),
                                ps[:, :, CHUNKS * par:CHUNKS * par + CHUNKS],
                                rden_a[:, 0:m].unsqueeze(2).to_broadcast([HALF, m, CHUNKS]), ALU.mult)
                        evac["dve"].mark(last)
                        wait_evacuated(dve, "act", g, place)
                        rden_b_done.mark(dve.reciprocal(rden_b[:, sub, t0:t0 + m], den_b[:, sub, t0:t0 + m]))

                def residual(g, sub):
                    o_ps_done.wait(dve, 2 * g + sub + 1)
                    xres_done.wait(dve, g + 1)
                    y_stored[sub].wait(dve, 16 * g)
                    step(dve.tensor_tensor(y[:, sub, :], o_ps[:, 0:D], consts[:, 2, :], ALU.mult))
                    y_done.mark(dve.tensor_tensor(y[:, sub, :], y[:, sub, :], xres[:, sub, :], ALU.add))

                sizes = dict(prepare=4, rest=0, project=0, attend=2 * NB, residual=1)

                def stage(fn, at, *args):
                    link.base, link.n = at, 0
                    fn(*args)
                    assert link.n == sizes[fn.__name__], (fn.__name__, link.n)
                    return at + link.n

                head = stage(prepare, 0, 0)
                stage(rest, head, 0)
                head = stage(project, head, -1)
                per_round = sizes["prepare"] + sizes["project"] + 2 * (sizes["attend"] + sizes["residual"])

                def body(g):
                    at = stage(attend, head + g * per_round, g, 0)
                    at = stage(prepare, at, g + 1)
                    at = stage(residual, at, g, 0)
                    stage(rest, at, g + 1)
                    at = stage(attend, at, g, 1)
                    at = stage(project, at, g)
                    stage(residual, at, g, 1)

                def last(g):
                    at = head + g * per_round
                    for sub in range(2):
                        at = stage(attend, at, g, sub)
                        at = stage(residual, at, g, sub)

                rounds(dve, body, last)


def layer1_ffn(nc, x, in_w, in_b, out_w, out_b, ln1_g, ln1_b, wg, w1, b1, w2, b2, mods, ident, upto, same_batch,
               batch_before, other_position, tile_mask, falling, y1_dram, y1T_dram, out):
    s = Scope(nc)
    x_t, out_t = tiles_of(x), tiles_of(out)
    NH, DH = 4, 32
    E, FF = 8, 512
    FC = FF // P
    CAP = B * L // E
    SCALE = DH ** -0.5
    W = DH + 1
    RING = 2
    BLOCK = P // E
    with s.stack:
        sb = s.sb
        consts = sb("f_mods", [P, 4, D])
        rows = sb("f_rows", [P, 4, D])
        in_w_sb, in_b_sb, out_w_sb = sb("f_in_w", [P, 3 * D]), sb("f_in_b", [P, 2]), sb("f_out_w", [P, D])
        wg_sb, ident_sb = sb("f_wg", [P, E]), sb("f_ident", [P, P])
        upto_sb, same_sb, before_sb = sb("f_upto", [P, P]), sb("f_same", [P, P]), sb("f_before", [P, P])
        other_sb = sb("f_other", [P, P])
        eps, power = sb("f_eps", [P, 2]), sb("f_power", [P, 2])
        logits = sb("f_logits", [P, TILES, E])
        w12 = sb("f_w12", [P, E, D])
        bias = sb("f_bias", [P, TILES, D])
        coef = sb("f_coef", [P, TILES, E])

        with ExitStack() as part:
            def sb1(name, shape, dt=F32):
                return part.enter_context(nc.sbuf_tensor(name, shape, dt))

            def ps1(name, shape):
                return part.enter_context(nc.psum_tensor(name, shape, F32))

            xin, h = sb1("fa_x", [P, RING, 2, D]), sb1("fa_h", [P, RING, 2, D])
            stats, mv = sb1("fa_stats", [P, 2, 6]), sb1("fa_mean_var", [P, 2, 2, 2])
            shifted, rstd = sb1("fa_shifted", [P, 2, 2]), sb1("fa_rstd", [P, 2, 2])
            hT = sb1("fa_hT", [P, 2, P])
            qT, kT = sb1("fa_qT", [P, 2, P]), sb1("fa_kT", [P, 2, P])
            v1 = sb1("fa_v1", [P, RING, 2, NH, W])
            score, top = sb1("fa_score", [P, NH, 2, P]), sb1("fa_top", [P, NH, 2])
            prob, probT = sb1("fa_prob", [P, NH, 2, P]), sb1("fa_probT", [P, NH, 2, P])
            rden, o, oT = sb1("fa_rden", [P, 2, NH]), sb1("fa_o", [P, 2, D]), sb1("fa_oT", [P, 2, P])
            z, y1, y1T = sb1("fa_z", [P, 2, D]), sb1("fa_y1", [P, 2, D]), sb1("fa_y1T", [P, 2, P])
            s_ps, t_ps, qk_ps = ps1("fa_s_ps", [P, NH, 512]), ps1("fa_t_ps", [P, 512]), ps1("fa_qk_ps", [P, 512])
            r1_ps, r2_ps = ps1("fa_r1_ps", [P, 512]), ps1("fa_r2_ps", [P, 512])
            turned_ps = t_ps[:, 0:2 * P].rearrange("p (t k) -> p t k", t=2)
            v_ps = mha_ps = r1_ps[:, 0:2 * D].rearrange("p (t d) -> p t d", t=2)
            o_ps = r2_ps[:, 0:2 * NH * W].rearrange("p (t h d) -> p t h d", t=2, h=NH)
            logit_ps = r2_ps[:, 2 * NH * W:2 * NH * W + 2 * E].rearrange("p (t e) -> p t e", t=2)

            def sig(name, ahead=0):
                return Signal(s, "fa_" + name, ahead)

            loaded, ready, dve_steps, pool_steps = s.sem("fa_loaded"), s.sem("fa_ready"), s.sem("fa_dve_steps"), s.sem("fa_pool_steps")
            settled = s.sem("fa_settled")
            x_in = [sig(f"x_in{k}") for k in range(RING)]
            mv_done, rstd_done = [sig(f"mv_done{k}") for k in range(2)], [sig(f"rstd_done{k}") for k in range(2)]
            h_done, hT_ps_done, hT_done = sig("h_done"), sig("hT_ps_done"), sig("hT_done")
            qk_ps_done, v_ps_done, qk_done, v_done = sig("qk_ps_done", 1), sig("v_ps_done"), sig("qk_done", 1), sig("v_done", 1)
            s_ps_done, masked, shifted_done, prob_done = sig("s_ps_done", 1), sig("masked"), sig("shifted_done"), sig("prob_done", 1)
            probT_ps_done, probT_done, o_ps_done, o_done = sig("probT_ps_done", 1), sig("probT_done", 1), sig("o_ps_done", 1), sig("o_done", 1)
            oT_ps_done, oT_done, mha_ps_done, z_done = sig("oT_ps_done", 1), sig("oT_done", 1), sig("mha_ps_done", 1), sig("z_done", 2)
            y1_done, y1T_ps_done, y1T_done = sig("y1_done"), sig("y1T_ps_done", 1), sig("y1T_done", 2)
            logit_ps_done, logit_done = sig("logit_ps_done", 1), sig("logit_done", 1)
            y1_stored, y1T_stored = sig("y1_stored", 16), sig("y1T_stored", 16)
            LOADS = 15

            def is_pair(i, b):
                return not isinstance(i, int) or 0 <= i * RING + b < PAIRS

            def rounds(eng, body):
                for b in range(RING):
                    body(0, b)
                with eng.Fori(1, PAIRS // RING - 1) as i:
                    for b in range(RING):
                        body(i, b)
                for b in range(RING):
                    body(PAIRS // RING - 1, b)

            def two(row):
                return row.unsqueeze(1).to_broadcast([P, 2, D])

            with nc.Block() as block:

                @block.sync
                def _(sp):
                    for dst, src in ((consts[:, :, :], mods[M1_SHIFT2:M1_BIAS2 + 1].rearrange("m p d -> p m d")),
                                     (in_w_sb[:, :], in_w), (out_w_sb[:, :], out_w), (wg_sb[:, :], wg),
                                     (in_b_sb[:, 0:1], in_b[0:D].rearrange("(p a) -> p a", a=1)),
                                     (in_b_sb[:, 1:2], in_b[D:2 * D].rearrange("(p a) -> p a", a=1)),
                                     (ident_sb[:, :], ident), (upto_sb[:, :], upto), (same_sb[:, :], same_batch),
                                     (before_sb[:, :], batch_before), (other_sb[:, :], other_position),
                                     (rows[:, 0, :], in_b[2 * D:3 * D].rearrange("(a d) -> a d", a=1).to_broadcast([P, D])),
                                     (rows[:, 1, :], out_b.rearrange("(a d) -> a d", a=1).to_broadcast([P, D])),
                                     (rows[:, 2, :], ln1_g.rearrange("(a d) -> a d", a=1).to_broadcast([P, D])),
                                     (rows[:, 3, :], ln1_b.rearrange("(a d) -> a d", a=1).to_broadcast([P, D]))):
                        sp.dma_start(dst, src).then_inc(loaded, 16)

                    def load(n, slot):
                        for t in range(2):
                            x_in[slot].mark(sp.dma_start(xin[:, slot, t, :], x_t[n * 2 + t]), 16)

                    load(0, 0)

                    def body(i, b):
                        n = i * RING + b
                        if is_pair(i, b + 1):
                            if is_pair(i, b - 1):
                                h_done.wait(sp, n)
                            load(n + 1, (b + 1) % RING)
                        y1_done.wait(sp, n + 1)
                        y1_stored.mark(sp.dma_start(y1_dram[n], y1[:, :, :]), 16)
                        y1T_done.wait(sp, n + 1)
                        y1T_stored.mark(sp.dma_start(y1T_dram[n], y1T[:, :, :]), 16)

                    y1_stored.give_ahead(sp)
                    y1T_stored.give_ahead(sp)
                    rounds(sp, body)
                    y1_stored.wait(sp, PAIRS * 16)
                    y1T_stored.wait(sp, PAIRS * 16)

                @block.gpsimd
                def _(pool):
                    pool.memset(eps[:, :], EPS_LN)
                    pool.memset(power[:, :], -0.5)
                    pool.memset(v1[:, :, :, :, :], 1.0).then_inc(ready, 1)
                    pool.wait_ge(ready, 1)
                    link = Chain(pool, pool_steps, 0)

                    def root(k, n, at):
                        link.base, link.n = at, 0
                        mv_done[k].wait(pool, n + 1)
                        link.then(pool.tensor_tensor(shifted[:, k, :], mv[:, k, :, 1], eps[:, :], ALU.add))
                        rstd_done[k].mark(pool.tensor_tensor(rstd[:, k, :], shifted[:, k, :], power[:, :], ALU.pow))

                    root(0, 0, 0)

                    def body(i, b):
                        n = i * RING + b
                        if is_pair(i, b + 1):
                            root(0, n + 1, 2 * n + 1)
                            root(1, n, 2 * n + 2)
                        else:
                            root(1, n, 2 * n + 1)

                    rounds(pool, body)

                @block.scalar
                def _(act):
                    act.wait_ge(loaded, LOADS * 16)
                    prob_done.give_ahead(act)
                    qk_ps_done.give_ahead(act)
                    s_ps_done.give_ahead(act)
                    probT_ps_done.give_ahead(act)
                    o_ps_done.give_ahead(act)
                    mha_ps_done.give_ahead(act)
                    logit_ps_done.give_ahead(act)

                    def project(n):
                        v_ps_done.wait(act, n + 1)
                        s_ps_done.wait(act, n)
                        for k, dst in enumerate((qT, kT)):
                            last = act.activation(dst[:, :, :].rearrange("p t k -> p (t k)"), qk_ps[:, k * 2 * P:(k + 1) * 2 * P],
                                                  ACT.Identity, bias=in_b_sb[:, k:k + 1])
                        qk_done.mark(last)

                    def a(n):
                        hT_ps_done.wait(act, n + 1)
                        qk_ps_done.wait(act, n)
                        hT_done.mark(act.copy(hT[:, :, :], turned_ps))

                    def d(n):
                        y1T_ps_done.wait(act, n + 1)
                        logit_ps_done.wait(act, n)
                        y1T_stored.wait(act, 16 * n)
                        y1T_done.mark(act.copy(y1T[:, :, :], turned_ps))
                        logit_ps_done.wait(act, n + 1)
                        logit_done.mark(act.copy(logits[:, bass.ds(n * 2, 2), :], logit_ps))

                    a(0)
                    project(0)

                    def body(i, b):
                        n = i * RING + b
                        shifted_done.wait(act, n + 1)
                        probT_ps_done.wait(act, n)
                        prob_done.mark(act.activation(prob[:, :, :, :], score[:, :, :, :], ACT.Exp, scale=SCALE))
                        if is_pair(i, b - 1):
                            d(n - 1)
                        if is_pair(i, b + 1):
                            a(n + 1)
                        probT_ps_done.wait(act, n + 1)
                        o_ps_done.wait(act, n)
                        probT_done.mark(act.copy(probT[:, :, :, :].rearrange("p h t k -> p h (t k)"), s_ps[:, :, 0:2 * P]))
                        if is_pair(i, b + 1):
                            project(n + 1)
                        oT_ps_done.wait(act, n + 1)
                        mha_ps_done.wait(act, n)
                        oT_done.mark(act.copy(oT[:, :, :], turned_ps))

                    rounds(act, body)
                    d(PAIRS - 1)

                @block.tensor
                def _(pe):
                    pe.wait_ge(loaded, LOADS * 16)
                    for given in (qk_done, v_done, probT_done, o_done, oT_done, z_done, y1T_done, logit_done):
                        given.give_ahead(pe)

                    def turn(src, done):
                        for t in range(2):
                            last = pe.transpose(turned_ps[:, t, :], src[:, t, :], ident_sb[:, :])
                        done.mark(last)

                    def a(n, slot):
                        h_done.wait(pe, n + 1)
                        y1T_done.wait(pe, n - 1)
                        turn(h[:, slot], hT_ps_done)

                    def project(n):
                        hT_done.wait(pe, n + 1)
                        qk_done.wait(pe, n)
                        z_done.wait(pe, n - 1)
                        for k in range(2):
                            last = pe.matmul(qk_ps[:, k * 2 * P:(k + 1) * 2 * P], in_w_sb[:, k * D:(k + 1) * D],
                                             hT[:, :, :].rearrange("p t k -> p (t k)"), start=True, stop=True)
                        qk_ps_done.mark(last)
                        for t in range(2):
                            last = pe.matmul(v_ps[:, t, :], hT[:, t, :], in_w_sb[:, 2 * D:3 * D], start=True, stop=True)
                        v_ps_done.mark(last)

                    def d(n):
                        y1_done.wait(pe, n + 1)
                        oT_done.wait(pe, n + 1)
                        turn(y1, y1T_ps_done)
                        y1T_done.wait(pe, n + 1)
                        o_done.wait(pe, n + 1)
                        for t in range(2):
                            last = pe.matmul(logit_ps[:, t, :], y1T[:, t, :], wg_sb[:, :], start=True, stop=True)
                        logit_ps_done.mark(last)

                    a(0, 0)
                    project(0)

                    def body(i, b):
                        n = i * RING + b
                        qk_done.wait(pe, n + 1)
                        probT_done.wait(pe, n)
                        for t in range(2):
                            for hd in range(NH):
                                last = pe.matmul(s_ps[:, hd, t * P:t * P + P], qT[DH * hd:DH * hd + DH, t, :],
                                                 kT[DH * hd:DH * hd + DH, t, :], start=True, stop=True)
                        s_ps_done.mark(last)
                        if is_pair(i, b - 1):
                            d(n - 1)
                        if is_pair(i, b + 1):
                            a(n + 1, (b + 1) % RING)
                        prob_done.wait(pe, n + 1)
                        masked.wait(pe, n + 1)
                        for t in range(2):
                            for hd in range(NH):
                                last = pe.transpose(s_ps[:, hd, t * P:t * P + P], prob[:, hd, t, :], ident_sb[:, :])
                        probT_ps_done.mark(last)
                        probT_done.wait(pe, n + 1)
                        v_done.wait(pe, n + 1)
                        logit_done.wait(pe, n)
                        for t in range(2):
                            for hd in range(NH):
                                last = pe.matmul(o_ps[:, t, hd, :], probT[:, hd, t, :], v1[:, b, t, hd, :], start=True, stop=True)
                        o_ps_done.mark(last)
                        if is_pair(i, b + 1):
                            project(n + 1)
                        o_done.wait(pe, n + 1)
                        if is_pair(i, b + 1):
                            hT_done.wait(pe, n + 2)
                        turn(o, oT_ps_done)
                        oT_done.wait(pe, n + 1)
                        if is_pair(i, b + 1):
                            v_done.wait(pe, n + 2)
                        for t in range(2):
                            last = pe.matmul(mha_ps[:, t, :], oT[:, t, :], out_w_sb[:, :], start=True, stop=True)
                        mha_ps_done.mark(last)

                    rounds(pe, body)
                    d(PAIRS - 1)

                @block.vector
                def _(dve):
                    dve.wait_ge(loaded, LOADS * 16)
                    dve.wait_ge(ready, 1)
                    oT_ps_done.give_ahead(dve)
                    y1T_ps_done.give_ahead(dve)
                    link = Chain(dve, dve_steps, 0)
                    step = link.then

                    def stats_of(k, src):
                        for t in range(2):
                            last = dve.bn_stats(stats[:, t, :], src[:, t, :])
                        step(last)
                        settle(dve, settled)
                        for t in range(2):
                            last = dve.bn_aggr(mv[:, k, t, :], stats[:, t, :])
                        mv_done[k].mark(last)

                    def normalise(k, n, dst, src, gain, shift, done):
                        rstd_done[k].wait(dve, n + 1)
                        for t in range(2):
                            last = dve.tensor_scalar(dst[:, t, :], src[:, t, :], mv[:, k, t, 0:1], rstd[:, k, t:t + 1],
                                                     ALU.subtract, ALU.mult)
                        step(last)
                        step(dve.tensor_tensor(dst, dst, two(gain), ALU.mult))
                        done.mark(dve.tensor_tensor(dst, dst, two(shift), ALU.add))

                    def start(n, cycle, slot):
                        x_in[slot].wait(dve, 32 * cycle + 32)
                        stats_of(0, xin[:, slot])

                    def a(n, slot):
                        normalise(0, n, h[:, slot], xin[:, slot], consts[:, 1, :], consts[:, 0, :], h_done)

                    def values(n, slot):
                        v_ps_done.wait(dve, n + 1)
                        v_done.mark(dve.tensor_tensor(
                            v1[:, slot, :, :, 0:DH], v_ps.rearrange("p t (h d) -> p t h d", h=NH),
                            two(rows[:, 0, :]).rearrange("p t (h d) -> p t h d", h=NH), ALU.add))

                    def scores(n):
                        s_ps_done.wait(dve, n + 1)
                        prob_done.wait(dve, n)
                        for t in range(2):
                            last = dve.tensor_tensor(score[:, :, t, :], s_ps[:, :, t * P:t * P + P],
                                                     other_sb[:, :].unsqueeze(1).to_broadcast([P, NH, P]), ALU.add)
                        masked.mark(last)
                        masked.wait(dve, n + 1)
                        step(dve.tensor_reduce(top[:, :, :], score[:, :, :, :], AX.X, ALU.max))
                        shifted_done.mark(dve.tensor_tensor(
                            score[:, :, :, :], score[:, :, :, :], top[:, :, :].unsqueeze(3).to_broadcast([P, NH, 2, P]),
                            ALU.subtract))

                    def attended(n):
                        o_ps_done.wait(dve, n + 1)
                        step(dve.reciprocal(rden[:, :, :], o_ps[:, :, :, DH]))
                        oT_ps_done.wait(dve, n)
                        o_done.mark(dve.tensor_tensor(o[:, :, :].rearrange("p t (h d) -> p t h d", h=NH), o_ps[:, :, :, 0:DH],
                                                      rden[:, :, :].unsqueeze(3).to_broadcast([P, 2, NH, DH]), ALU.mult))

                    def residual(n, slot):
                        mha_ps_done.wait(dve, n + 1)
                        ins = dve.tensor_tensor(z[:, :, :], mha_ps, two(rows[:, 1, :]), ALU.add)
                        z_done.mark(ins)
                        z_done.wait(dve, n + 1)
                        step(dve.tensor_tensor(z[:, :, :], z[:, :, :], h[:, slot], ALU.add))
                        stats_of(1, z)
                        y1T_ps_done.wait(dve, n)
                        y1_stored.wait(dve, 16 * n)
                        normalise(1, n, y1[:, :, :], z, rows[:, 2, :], rows[:, 3, :], y1_done)

                    sizes = dict(start=1, a=2, values=0, scores=1, attended=1, residual=4)

                    def stage(fn, at, *args):
                        link.base, link.n = at, 0
                        fn(*args)
                        assert link.n == sizes[fn.__name__], (fn.__name__, link.n)
                        return at + link.n

                    at = stage(start, 0, 0, 0, 0)
                    head = stage(a, at, 0, 0)
                    values(0, 0)
                    per_round = sum(sizes.values())

                    def body(i, b):
                        n = i * RING + b
                        at = head + n * per_round
                        more = is_pair(i, b + 1)
                        at = stage(scores, at, n)
                        if more:
                            at = stage(start, at, n + 1, i + (b + 1) // RING, (b + 1) % RING)
                            at = stage(a, at, n + 1, (b + 1) % RING)
                        at = stage(attended, at, n)
                        if more:
                            values(n + 1, (b + 1) % RING)
                        stage(residual, at, n, b)

                    rounds(dve, body)

        with ExitStack() as part:
            def sb2(name, shape, dt=F32):
                return part.enter_context(nc.sbuf_tensor(name, shape, dt))

            def ps2(name, shape):
                return part.enter_context(nc.psum_tensor(name, shape, F32))

            w1_sb, w2_sb = sb2("fb_w1", [P, E, FC, D]), sb2("fb_w2", [P, E, FC, D])
            b1_sb, b2_rows, b12 = sb2("fb_b1", [P, E, FC]), sb2("fb_b2", [P, D]), sb2("fb_b12", [P, D])
            b1_of = sb2("fb_b1_of", [P, E, FC, BLOCK, E])
            mask_sb, falling_sb = sb2("fb_mask", [P, BLOCK]), sb2("fb_falling", [P, E])
            b12_of = sb2("fb_b12_of", [P, BLOCK, D])
            top, ex, total = sb2("fb_top", [P, TILES]), sb2("fb_exp", [P, TILES, E]), sb2("fb_sum", [P, TILES])
            rtotal, gates, gate = sb2("fb_rsum", [P, TILES]), sb2("fb_gates", [P, TILES, E]), sb2("fb_gate", [P, TILES])
            rank, first = sb2("fb_rank", [P, TILES, E]), sb2("fb_first", [P, TILES])
            chosen, of_batch = sb2("fb_chosen", [P, TILES, E]), sb2("fb_of_batch", [P, E])
            tile_counts, running = sb2("fb_tile_counts", [P, TILES, E]), sb2("fb_running", [P, TILES, E])
            zero, place, kept = sb2("fb_zero", [P, TILES]), sb2("fb_place", [P, TILES, E]), sb2("fb_kept", [P, TILES, E])
            coefT = sb2("fb_coefT", [P, TILES // BLOCK, P])
            w_ps, within_ps, tile_ps, before_ps = ps2("fb_w_ps", [P, 2, 512]), ps2("fb_within_ps", [P, 512]), ps2("fb_tile_ps", [P, 512]), ps2("fb_before_ps", [P, 512])
            b_ps, bias_ps = ps2("fb_b_ps", [P, 512]), ps2("fb_bias_ps", [P, 2, 512])
            loaded, ready, dve_steps = s.sem("fb_loaded"), s.sem("fb_ready"), s.sem("fb_dve_steps")
            shifted_done, exp_done, chosen_done, of_batch_done = s.sem("fb_shifted_done"), s.sem("fb_exp_done"), s.sem("fb_chosen_done"), s.sem("fb_of_batch_done")
            counts_done, b1_of_done, w12_ps_done, b12_ps_done = s.sem("fb_counts_done"), s.sem("fb_b1_of_done"), s.sem("fb_w12_ps_done"), s.sem("fb_b12_ps_done")
            b12_of_done, coef_done, coefT_ps_done, coefT_done = s.sem("fb_b12_of_done"), s.sem("fb_coef_done"), s.sem("fb_coefT_ps_done"), s.sem("fb_coefT_done")
            bias_ps_done, bias_done = s.sem("fb_bias_ps_done"), s.sem("fb_bias_done")
            with nc.Block() as block:

                @block.sync
                def _(sp):
                    sp.dma_start(w1_sb[:, :, :, :], w1.rearrange("e (c p) d -> p e c d", p=P)).then_inc(loaded, 16)
                    sp.dma_start(w2_sb[:, :, :, :], w2.rearrange("e (c p) d -> p e c d", p=P)).then_inc(loaded, 16)
                    sp.dma_start(b1_sb[:, :, :].rearrange("p e c -> p (e c)"), b1).then_inc(loaded, 16)
                    sp.dma_start(b2_rows[:, :], b2.unsqueeze(0).to_broadcast([BLOCK, E, D])).then_inc(loaded, 16)
                    sp.dma_start(mask_sb[:, :], tile_mask).then_inc(loaded, 16)
                    sp.dma_start(falling_sb[:, :], falling).then_inc(loaded, 16)

                @block.gpsimd
                def _(pool):
                    pool.memset(zero[:, :], 0.0)
                    pool.memset(b1_of[:, :, :, :, :], 0.0).then_inc(ready, 1)
                    pool.wait_ge(ready, 1)
                    pool.wait_ge(loaded, 6 * 16)
                    for e in range(E):
                        last = pool.tensor_copy(b1_of[:, e, :, :, e], b1_sb[:, e, :].unsqueeze(2).to_broadcast([P, FC, BLOCK]))
                    last.then_inc(b1_of_done, 1)

                @block.scalar
                def _(act):
                    act.wait_ge(shifted_done, 1)
                    act.activation(ex[:, :, :], ex[:, :, :], ACT.Exp).then_inc(exp_done, 1)
                    act.wait_ge(w12_ps_done, 1)
                    act.copy(w12[:, :, :].rearrange("p (a e) d -> p a (e d)", a=2), w_ps[:, :, :])
                    act.wait_ge(coefT_ps_done, 1)
                    act.copy(coefT[:, :, :].rearrange("p a b -> p (a b)"), within_ps[:, :]).then_inc(coefT_done, 1)
                    for k in range(TILES // 4):
                        act.wait_ge(bias_ps_done, k + 1)
                        act.copy(bias[:, 4 * k:4 * k + 4, :].rearrange("p t d -> p (t d)"),
                                 bias_ps[:, k % 2, :]).then_inc(bias_done, 1)

                @block.tensor
                def _(pe):
                    pe.wait_ge(loaded, 6 * 16)
                    for e in range(E):
                        for c in range(FC):
                            last = pe.matmul(w_ps[:, e // 4, (e % 4) * D:(e % 4) * D + D], w1_sb[:, e, c, :], w2_sb[:, e, c, :],
                                             start=c == 0, stop=c == FC - 1)
                    last.then_inc(w12_ps_done, 1)
                    pe.wait_ge(b1_of_done, 1)
                    for e in range(E):
                        for c in range(FC):
                            last = pe.matmul(b_ps[:, 0:D], b1_of[:, e, c].rearrange("p a b -> p (a b)"), w2_sb[:, e, c, :],
                                             start=e == c == 0, stop=(e, c) == (E - 1, FC - 1))
                    last.then_inc(b12_ps_done, 1)
                    pe.wait_ge(chosen_done, 1)
                    flat = chosen[:, :, :].rearrange("p t e -> p (t e)")
                    pe.matmul(within_ps[:, :], upto_sb[:, :], flat, start=True, stop=True)
                    pe.matmul(tile_ps[:, :], same_sb[:, :], flat, start=True, stop=True)
                    pe.wait_ge(of_batch_done, 1)
                    pe.matmul(before_ps[:, 0:E], before_sb[:, :], of_batch[:, :], start=True, stop=True).then_inc(counts_done, 1)
                    pe.wait_ge(coef_done, 1)
                    for k in range(TILES // BLOCK):
                        last = pe.transpose(within_ps[:, k * P:k * P + P],
                                            coef[:, k * BLOCK:(k + 1) * BLOCK, :].rearrange("p t e -> p (t e)"), ident_sb[:, :])
                    last.then_inc(coefT_ps_done, 1)
                    pe.wait_ge(coefT_done, 1)
                    pe.wait_ge(b12_of_done, 1)
                    for j in range(TILES):
                        k = j // 4
                        if j % 4 == 0 and k >= 2:
                            pe.wait_ge(bias_done, k - 1)
                        last = pe.matmul(bias_ps[:, k % 2, (j % 4) * D:(j % 4) * D + D], coefT[:, j // BLOCK, :],
                                         b12_of[:, j % BLOCK, :], start=True, stop=True)
                        if j % 4 == 3:
                            last.then_inc(bias_ps_done, 1)

                @block.vector
                def _(dve):
                    link = Chain(dve, dve_steps, 0)
                    step = link.then

                    def each(a):
                        return a.unsqueeze(2).to_broadcast([P, TILES, E])

                    step(dve.tensor_reduce(top[:, :], logits[:, :, :], AX.X, ALU.max))
                    dve.tensor_tensor(ex[:, :, :], logits[:, :, :], each(top[:, :]), ALU.subtract).then_inc(shifted_done, 1)
                    dve.wait_ge(exp_done, 1)
                    step(dve.tensor_reduce(total[:, :], ex[:, :, :], AX.X, ALU.add))
                    step(dve.reciprocal(rtotal[:, :], total[:, :]))
                    step(dve.tensor_tensor(gates[:, :, :], ex[:, :, :], each(rtotal[:, :]), ALU.mult))
                    step(dve.tensor_reduce(gate[:, :], gates[:, :, :], AX.X, ALU.max))
                    step(dve.tensor_tensor(rank[:, :, :], gates[:, :, :], each(gate[:, :]), ALU.is_equal))
                    dve.wait_ge(loaded, 6 * 16)
                    step(dve.tensor_tensor(rank[:, :, :], rank[:, :, :],
                                           falling_sb[:, :].unsqueeze(1).to_broadcast([P, TILES, E]), ALU.mult))
                    step(dve.tensor_reduce(first[:, :], rank[:, :, :], AX.X, ALU.max))
                    ins = dve.tensor_tensor(chosen[:, :, :], rank[:, :, :], each(first[:, :]), ALU.is_equal)
                    ins.then_inc(chosen_done, 1)
                    dve.wait_ge(chosen_done, 1)
                    dve.tensor_reduce(of_batch[:, :], chosen[:, :, :].rearrange("p t e -> p e t"), AX.X, ALU.add).then_inc(of_batch_done, 1)
                    dve.wait_ge(b12_ps_done, 1)
                    step(dve.tensor_tensor(b12[:, :], b_ps[:, 0:D], b2_rows[:, :], ALU.add))
                    dve.tensor_tensor(b12_of[:, :, :], b12[:, :].unsqueeze(1).to_broadcast([P, BLOCK, D]),
                                      mask_sb[:, :].unsqueeze(2).to_broadcast([P, BLOCK, D]), ALU.mult).then_inc(b12_of_done, 1)
                    dve.wait_ge(counts_done, 1)
                    dve.wait_ge(ready, 1)
                    step(dve.tensor_copy(tile_counts[:, :, :].rearrange("p t e -> p (t e)"), tile_ps[:, :]))
                    for e in range(E):
                        last = dve.tensor_tensor_scan(running[:, :, e], tile_counts[:, :, e], zero[:, :], 0.0, ALU.add, ALU.add)
                    step(last)
                    step(dve.tensor_tensor(running[:, :, :], running[:, :, :], tile_counts[:, :, :], ALU.subtract))
                    step(dve.tensor_tensor(place[:, :, :].rearrange("p t e -> p (t e)"), within_ps[:, :],
                                           running[:, :, :].rearrange("p t e -> p (t e)"), ALU.add))
                    step(dve.tensor_copy(of_batch[:, :], before_ps[:, 0:E]))
                    step(dve.tensor_tensor(place[:, :, :], place[:, :, :], of_batch[:, :].unsqueeze(1).to_broadcast([P, TILES, E]), ALU.add))
                    step(dve.scalar_tensor_tensor(kept[:, :, :].rearrange("p t e -> p (t e)"),
                                                  place[:, :, :].rearrange("p t e -> p (t e)"), float(CAP),
                                                  chosen[:, :, :].rearrange("p t e -> p (t e)"), ALU.is_le, ALU.mult))
                    dve.tensor_tensor(coef[:, :, :], kept[:, :, :], each(gate[:, :]), ALU.mult).then_inc(coef_done, 1)

        with ExitStack() as part:
            def sb3(name, shape, dt=F32):
                return part.enter_context(nc.sbuf_tensor(name, shape, dt))

            xin, y1, y1T = sb3("fc_x", [P, 2, 2, D]), sb3("fc_y1", [P, 2, 2, D]), sb3("fc_y1T", [P, 2, 2, P])
            acc, y = sb3("fc_acc", [P, 2, D]), sb3("fc_y", [P, 2, 2, D])
            stats, mv = sb3("fc_stats", [P, 2, 6]), sb3("fc_mean_var", [P, 2, 2])
            std, rstd = sb3("fc_std", [P, 2]), sb3("fc_rstd", [P, 2])
            e_ps = part.enter_context(nc.psum_tensor("fc_e_ps", [P, 4, 2, 512], F32))
            ins_done = [Signal(s, f"fc_in{k}") for k in range(2)]
            y_stored = [Signal(s, f"fc_y_stored{k}", 32) for k in range(2)]
            e_done, e_read = Signal(s, "fc_e_done", 4), Signal(s, "fc_e_read", 4)
            mv_done, std_done, y_done = Signal(s, "fc_mv_done"), Signal(s, "fc_std_done"), Signal(s, "fc_y_done", 2)
            dve_steps, settled = s.sem("fc_dve_steps"), s.sem("fc_settled")
            with nc.Block() as block:

                @block.sync
                def _(sp):
                    for k in range(2):
                        y_stored[k].give_ahead(sp)
                    y_done.give_ahead(sp)

                    def load(n, slot):
                        ins_done[slot].mark(sp.dma_start(y1T[:, slot], y1T_dram[n]), 16)
                        ins_done[slot].mark(sp.dma_start(y1[:, slot], y1_dram[n]), 16)
                        for t in range(2):
                            ins_done[slot].mark(sp.dma_start(xin[:, slot, t, :], x_t[n * 2 + t]), 16)

                    load(0, 0)

                    def body(i, b):
                        n = i * 2 + b
                        if not isinstance(i, int) or n + 1 < PAIRS:
                            y_done.wait(sp, n)
                            load(n + 1, 1 - b)
                        y_done.wait(sp, n + 1)
                        for t in range(2):
                            y_stored[b].mark(sp.dma_start(out_t[n * 2 + t], y[:, b, t, :]), 16)

                    in_rounds(sp, 2, body)
                    for k in range(2):
                        y_stored[k].wait(sp, PAIRS // 2 * 32)

                @block.scalar
                def _(act):
                    def body(i, b):
                        n = i * 2 + b
                        mv_done.wait(act, n + 1)
                        std_done.mark(act.activation(std[:, :], mv[:, :, 1], ACT.Sqrt, bias=eps[:, 0:1]))

                    in_rounds(act, 2, body)

                @block.tensor
                def _(pe):
                    e_read.give_ahead(pe)

                    def body(i, b):
                        n = i * 2 + b
                        ins_done[b].wait(pe, 64 * i + 64)
                        for t in range(2):
                            e_read.wait(pe, 2 * n + t - 3)
                            for k in range(2):
                                last = pe.matmul(e_ps[:, (2 * b + t) % 4, k, :], y1T[:, b, t, :],
                                                 w12[:, 4 * k:4 * k + 4, :].rearrange("p e d -> p (e d)"), start=True, stop=True)
                            e_done.mark(last)

                    in_rounds(pe, 2, body)

                @block.vector
                def _(dve):
                    e_done.give_ahead(dve)
                    link = Chain(dve, dve_steps, 1 + (E - 1) + 5)
                    step = link.then

                    def body(i, b):
                        n = i * 2 + b
                        link.start(n)
                        ins_done[b].wait(dve, 64 * i + 64)
                        y_done.wait(dve, n)
                        step(dve.tensor_tensor(acc[:, :, :], y1[:, b], bias[:, bass.ds(n * 2, 2), :], ALU.add))
                        for e in range(E):
                            for t in range(2):
                                if e == 0:
                                    e_done.wait(dve, 2 * n + t + 1)
                                last = dve.scalar_tensor_tensor(
                                    acc[:, t, :], e_ps[:, 2 * b + t, e // 4, (e % 4) * D:(e % 4) * D + D],
                                    coef[:, bass.ds(n * 2 + t, 1), e], acc[:, t, :], ALU.mult, ALU.add)
                                if e == E - 1:
                                    e_read.mark(last)
                                elif t == 1:
                                    step(last)
                        e_read.wait(dve, 2 * n + 2)
                        for t in range(2):
                            last = dve.bn_stats(stats[:, t, :], acc[:, t, :])
                        step(last)
                        settle(dve, settled)
                        for t in range(2):
                            last = dve.bn_aggr(mv[:, t, :], stats[:, t, :])
                        mv_done.mark(last)
                        std_done.wait(dve, n + 1)
                        step(dve.reciprocal(rstd[:, :], std[:, :]))
                        for t in range(2):
                            last = dve.tensor_scalar(acc[:, t, :], acc[:, t, :], mv[:, t, 0:1], rstd[:, t:t + 1],
                                                     ALU.subtract, ALU.mult)
                        step(last)
                        step(dve.tensor_tensor(acc[:, :, :], acc[:, :, :], consts[:, 2, :].unsqueeze(1).to_broadcast([P, 2, D]), ALU.mult))
                        step(dve.tensor_tensor(acc[:, :, :], acc[:, :, :], consts[:, 3, :].unsqueeze(1).to_broadcast([P, 2, D]), ALU.add))
                        y_stored[b].wait(dve, 32 * i)
                        y_done.mark(dve.tensor_tensor(y[:, b], acc[:, :, :], xin[:, b], ALU.add))
                        assert link.n == link.per_round

                    in_rounds(dve, 2, body)


def adaln_two_layers(nc, x, L0_wqkv, L0_wo, L0_ln_g, L0_ln_b, L0_c, L0_wmod, L1_wq, L1_wk, L1_wv, L1_wo, L1_bo,
                     in_w, in_b, out_w, out_b, ln1_g, ln1_b, ln2_g, ln2_b, wg, w1, b1, w2, b2, L1_c, L1_wmod,
                     ident, upto, same_batch, last_of_batch, batch_before, fold, other_position, cos, sin,
                     tile_mask, falling, out):
    def scratch(name, shape):
        return nc.dram_tensor(name, shape, F32, kind="Internal").ap()

    mods = scratch("mods", (M_COUNT, P, D))
    x1, x2 = scratch("x1", (B, L, D)), scratch("x2", (B, L, D))
    y1, y1T = scratch("y1", (PAIRS, P, 2, D)), scratch("y1T", (PAIRS, D, 2, P))
    modulation(nc, L0_c, L0_wmod, L0_ln_g, L0_ln_b, L1_c, L1_wmod, L1_bo, ln2_g, ln2_b, mods)
    layer0(nc, x, L0_wqkv, L0_wo, mods, ident, upto, last_of_batch, cos, sin, x1)
    layer1_attention(nc, x1, L1_wq, L1_wk, L1_wv, L1_wo, mods, ident, fold, x2)
    layer1_ffn(nc, x2, in_w, in_b, out_w, out_b, ln1_g, ln1_b, wg, w1, b1, w2, b2, mods, ident, upto, same_batch,
               batch_before, other_position, tile_mask, falling, y1, y1T, out)




def kernel(**inputs):
    import numpy as _np
    import concourse.bacc as _bacc
    from concourse import mybir as _mybir
    from concourse.bass_utils import run_bass_kernel_spmd as _run

    a = {name: _np.asarray(value) for name, value in inputs.items()}
    experts, hidden = a["L1_ffn_b1"].shape
    cos, sin = rope_tables()
    arrays = {
        "x": a["L0_attn_x"],
        "L0_wqkv": _np.concatenate([a["L0_attn_wq"], a["L0_attn_wk"], a["L0_attn_wv"]], axis=1),
        "L0_wo": a["L0_attn_wo"],
        "L0_ln_g": a["L0_ffn_ln_g"],
        "L0_ln_b": a["L0_ffn_ln_b"],
        "L0_c": a["L0_c"].T,
        "L0_wmod": a["L0_wmod"],
        "L1_wq": a["L1_attn_Wq"],
        "L1_wk": a["L1_attn_Wk"],
        "L1_wv": a["L1_attn_Wv"],
        "L1_wo": a["L1_attn_Wo"],
        "L1_bo": a["L1_attn_bo"],
        "in_w": a["L1_ffn_in_proj_w"].T,
        "in_b": a["L1_ffn_in_proj_b"],
        "out_w": a["L1_ffn_out_proj_w"].T,
        "out_b": a["L1_ffn_out_proj_b"],
        "ln1_g": a["L1_ffn_ln1_g"],
        "ln1_b": a["L1_ffn_ln1_b"],
        "ln2_g": a["L1_ffn_ln2_g"],
        "ln2_b": a["L1_ffn_ln2_b"],
        "wg": a["L1_ffn_wg"],
        "w1": a["L1_ffn_w1"].transpose(0, 2, 1),
        "b1": a["L1_ffn_b1"].reshape(experts, hidden // P, P).transpose(2, 0, 1).reshape(P, -1),
        "w2": a["L1_ffn_w2"],
        "b2": a["L1_ffn_b2"],
        "L1_c": a["L1_c"].T,
        "L1_wmod": a["L1_wmod"],
        "ident": IDENT,
        "upto": UPTO,
        "same_batch": SAME_BATCH,
        "last_of_batch": LAST_OF_BATCH,
        "batch_before": BATCH_BEFORE,
        "fold": FOLD,
        "other_position": OTHER_POSITION,
        "cos": cos,
        "sin": sin,
        "tile_mask": (_np.arange(P)[:, None] // experts == _np.arange(P // experts)[None, :]).astype(_np.float32),
        "falling": _np.tile(_np.arange(experts, 0, -1).astype(_np.float32), (P, 1)),
    }
    arrays = {name: _np.ascontiguousarray(value) for name, value in arrays.items()}
    nc = _bacc.Bacc("TRN2", target_bir_lowering=False, num_devices=1)
    args = {name: nc.dram_tensor(name, value.shape, _mybir.dt.from_np(value.dtype), kind="ExternalInput").ap()
            for name, value in arrays.items()}
    out = nc.dram_tensor("out", (B, L, D), F32, kind="ExternalOutput").ap()
    adaln_two_layers(nc, out=out, **args)
    r = _run(nc, [arrays], core_ids=[0])
    return r.results[0]["out"]
```

```python
from contextlib import ExitStack

import numpy as np

import concourse.bass as bass
from concourse import mybir

F32 = mybir.dt.float32
F32R = mybir.dt.float32r
ALU = mybir.AluOpType
ACT = mybir.ActivationFunctionType
AX = mybir.AxisListType

P = 128
B, L, D = 8, 1024, 128
SEG = P // B
TILES = B * L // P
PAIRS = TILES // 2
EPS_LN = 1e-5
EPS_ATT = 1e-6

H0, D0 = 16, 8
V0 = D0 + 1
HEADS_OF_BANK = (6, 5, 5)

(M0_SHIFT, M0_SCALE, M0_GATE, M0_SHIFT2, M0_SCALE2, M0_GAIN2, M0_BIAS2, M1_SHIFT, M1_SCALE, M1_GATE,
 M1_BIAS, M1_SHIFT2, M1_SCALE2, M1_GAIN2, M1_BIAS2, M_COUNT) = range(16)

_row = np.arange(P)
_batch, _pos = _row // SEG, _row % SEG
_same = _batch[:, None] == _batch[None, :]
IDENT = np.eye(P, dtype=np.float32)
UPTO = (_same & (_pos[:, None] <= _pos[None, :])).astype(np.float32)
SAME_BATCH = _same.astype(np.float32)
LAST_OF_BATCH = (_same & (_pos[:, None] == SEG - 1)).astype(np.float32)
BATCH_BEFORE = (_batch[:, None] < _batch[None, :]).astype(np.float32)
FOLD = (_row[:, None] % 64 == _row[None, :] % 64).astype(np.float32)
OTHER_POSITION = np.where(_pos[:, None] == _pos[None, :], 0.0, -1e30).astype(np.float32)


def rope_tables():
    inv = (1.0 / np.float32(10000.0) ** (np.arange(0, D0, 2, dtype=np.float32) / np.float32(D0))).astype(np.float32)
    at = (np.arange(TILES)[None, :] * SEG + _pos[:, None]).astype(np.float32)
    angle = (at[:, :, None] * inv[None, None, :]).astype(np.float32)
    cos, sin = np.cos(angle).astype(np.float32), np.sin(angle).astype(np.float32)
    return np.repeat(cos, 2, axis=2), np.stack([-sin, sin], axis=3).reshape(P, TILES, D0)


def tiles_of(x):
    return x.rearrange("l (j n) d -> j l n d", n=SEG)


class Scope:

    def __init__(self, nc):
        self.nc, self.stack = nc, ExitStack()

    def sb(self, name, shape, dt=F32):
        return self.stack.enter_context(self.nc.sbuf_tensor(name, shape, dt))

    def psum(self, name, shape, dt=F32):
        return self.stack.enter_context(self.nc.psum_tensor(name, shape, dt))

    def sem(self, name):
        return self.stack.enter_context(self.nc.semaphore(name))


class Signal:

    def __init__(self, scope, name, ahead=0):
        self.sem, self.ahead = scope.sem(name), ahead

    def give_ahead(self, engine):
        engine.sem_inc(self.sem, self.ahead)

    def mark(self, instruction, by=1):
        instruction.then_inc(self.sem, by)

    def wait(self, engine, count):
        if not isinstance(count, int) or count + self.ahead > 0:
            engine.wait_ge(self.sem, count + self.ahead)


def in_rounds(eng, ring, body):
    with eng.Fori(0, PAIRS // ring - 1) as i:
        for b in range(ring):
            body(i, b)
    for b in range(ring):
        body(PAIRS // ring - 1, b)


def in_range(i, b, ring):
    return not isinstance(i, int) or 0 <= i * ring + b < PAIRS


def pairs_done(n):
    return min(max(n, 0), PAIRS) if isinstance(n, int) else n


def two(row):
    return row.unsqueeze(1).to_broadcast([P, 2, D])


def all_rounds(eng, ring, body, more=0):
    for n in range(-more, ring):
        body(n // ring, n % ring)
    with eng.Fori(1, PAIRS // ring - 1) as i:
        for b in range(ring):
            body(i, b)
    for n in range(PAIRS - ring, PAIRS + more):
        body(n // ring, n % ring)


class Steps:

    def __init__(self, engine, sem):
        self.engine, self.sem, self.base, self.n = engine, sem, 0, 0

    def start(self, base):
        self.base, self.n = base, 0

    def mark(self, instruction):
        self.n += 1
        instruction.then_inc(self.sem, 1)
        return self.base + self.n

    def wait(self, count):
        self.engine.wait_ge(self.sem, count)


class Chain:

    def __init__(self, engine, sem, per_round):
        self.engine, self.sem, self.per_round, self.base, self.n = engine, sem, per_round, 0, 0

    def start(self, rnd, first=0):
        self.base, self.n = rnd * self.per_round + first, 0

    def then(self, instruction):
        self.n += 1
        instruction.then_inc(self.sem, 1)
        self.engine.wait_ge(self.sem, self.base + self.n)


def settle(engine, settled):
    engine.sem_inc(settled, 1)


def modulation(nc, L0_c, L0_wmod, L0_ln_g, L0_ln_b, L1_c, L1_wmod, L1_bo, L1_ln2_g, L1_ln2_b, mods):
    s = Scope(nc)
    with s.stack:
        cT = s.sb("mod_cT", [P, 2, B])
        wmod = s.sb("mod_w", [P, 2, 6 * D])
        rows = s.sb("mod_rows", [P, 5, D])
        cneg = s.sb("mod_exp", [P, 2, B])
        den = s.sb("mod_den", [P, 2, B])
        rden = s.sb("mod_rden", [P, 2, B])
        silu = s.sb("mod_silu", [P, 2, B])
        silu_rows = s.sb("mod_silu_rows", [P, 2, P])
        size = s.sb("mod_size", [P, 2, 2, D])
        sign = s.sb("mod_sign", [P, 2, 2, D])
        gate = s.sb("mod_gate", [P, 2, 2, D])
        tile = s.sb("mod_tiles", [P, M_COUNT, D])
        mod_ps = s.psum("mod_ps", [P, 4, 512])
        loaded, exp_done, silu_done, mod_done = s.sem("mod_loaded"), s.sem("mod_exp_done"), s.sem("mod_silu_done"), s.sem("mod_done")
        steps, tiles_done, stored = s.sem("mod_steps"), s.sem("mod_tiles_done"), s.sem("mod_stored")
        with nc.Block() as block:

            @block.sync
            def _(sp):
                for layer, (c, w) in enumerate(((L0_c, L0_wmod), (L1_c, L1_wmod))):
                    sp.dma_start(cT[:, layer, :], c).then_inc(loaded, 16)
                    sp.dma_start(wmod[:, layer, :], w).then_inc(loaded, 16)
                for n, row in enumerate((L0_ln_g, L0_ln_b, L1_bo, L1_ln2_g, L1_ln2_b)):
                    sp.dma_start(rows[:, n, :], row.rearrange("(a d) -> a d", a=1).to_broadcast([P, D])).then_inc(loaded, 16)
                sp.wait_ge(tiles_done, 1)
                sp.dma_start(mods.rearrange("m p d -> p m d"), tile[:, 0:M_COUNT, :]).then_inc(stored, 16)
                sp.wait_ge(stored, 16)

            @block.scalar
            def _(act):
                act.wait_ge(loaded, 9 * 16)
                act.activation(cneg[:, :, :], cT[:, :, :], ACT.Exp, scale=-1.0).then_inc(exp_done, 1)

            @block.tensor
            def _(pe):
                pe.wait_ge(silu_done, 1)
                for layer in range(2):
                    for half, width in ((0, 512), (1, 256)):
                        last = pe.matmul(mod_ps[:, 2 * layer + half, 0:width], silu_rows[:, layer, :],
                                         wmod[:, layer, 512 * half:512 * half + width], start=True, stop=True)
                last.then_inc(mod_done, 1)

            @block.vector
            def _(dve):
                link = Chain(dve, steps, 5)
                link.start(0)
                dve.wait_ge(exp_done, 1)
                link.then(dve.tensor_scalar(den[:, :, :], cneg[:, :, :], 1.0, None, ALU.add))
                link.then(dve.reciprocal(rden[:, :, :], den[:, :, :]))
                link.then(dve.tensor_tensor(silu[:, :, :], cT[:, :, :], rden[:, :, :], ALU.mult))
                for layer in range(2):
                    last = dve.tensor_copy(silu_rows[:, layer, :].rearrange("p (l n) -> p l n", n=SEG),
                                           silu[:, layer, :].unsqueeze(2).to_broadcast([P, B, SEG]))
                last.then_inc(silu_done, 1)
                dve.wait_ge(mod_done, 1)

                def part(layer, k):
                    return mod_ps[:, 2 * layer + k // 4, (k % 4) * D:(k % 4) * D + D]

                for layer, (shift, scale, shift2, scale2) in enumerate(
                        ((M0_SHIFT, M0_SCALE, M0_SHIFT2, M0_SCALE2), (M1_SHIFT, M1_SCALE, M1_SHIFT2, M1_SCALE2))):
                    dve.tensor_copy(tile[:, shift, :], part(layer, 0))
                    dve.tensor_scalar(tile[:, scale, :], part(layer, 1), 1.0, None, ALU.add)
                    dve.tensor_copy(tile[:, shift2, :], part(layer, 3))
                    dve.tensor_scalar(tile[:, scale2, :], part(layer, 4), 1.0, None, ALU.add)
                    for g, k in enumerate((2, 5)):
                        last = dve.tensor_scalar(sign[:, layer, g, :], part(layer, k), 0.0, 2.0, ALU.is_ge, ALU.mult)
                link.then(last)
                link.then(dve.tensor_scalar(sign[:, :, :, :], sign[:, :, :, :], -1.0, None, ALU.add))
                for layer in range(2):
                    for g, k in enumerate((2, 5)):
                        last = dve.tensor_tensor(size[:, layer, g, :], sign[:, layer, g, :], part(layer, k), ALU.mult)
                link.then(last)
                link.then(dve.scalar_tensor_tensor(gate[:, :, :, :], size[:, :, :, :], 0.25, sign[:, :, :, :], ALU.max, ALU.mult))
                dve.tensor_copy(tile[:, M0_GATE, :], gate[:, 0, 0, :])
                dve.tensor_copy(tile[:, M1_GATE, :], gate[:, 1, 0, :])
                dve.tensor_tensor(tile[:, M0_GAIN2, :], gate[:, 0, 1, :], rows[:, 0, :], ALU.mult)
                dve.tensor_tensor(tile[:, M0_BIAS2, :], gate[:, 0, 1, :], rows[:, 1, :], ALU.mult)
                dve.tensor_tensor(tile[:, M1_BIAS, :], gate[:, 1, 0, :], rows[:, 2, :], ALU.mult)
                dve.tensor_tensor(tile[:, M1_GAIN2, :], gate[:, 1, 1, :], rows[:, 3, :], ALU.mult)
                dve.tensor_tensor(tile[:, M1_BIAS2, :], gate[:, 1, 1, :], rows[:, 4, :],
                                  ALU.mult).then_inc(tiles_done, 1)


def layer0(nc, x, wqkv, wo, mods, ident, upto, last_of_batch, cos2, sin2, out):
    s = Scope(nc)
    x_t, out_t = tiles_of(x), tiles_of(out)
    RING = 4
    with s.stack:
        sb = s.sb
        consts = sb("l0_mods", [P, 7, D])
        wqkv_sb, wo_sb = sb("l0_wqkv", [P, 3 * D]), sb("l0_wo", [P, D])
        ident_sb, upto_sb, last_sb = sb("l0_ident", [P, P]), sb("l0_upto", [P, P]), sb("l0_last", [P, P])
        cos_sb, sin_sb = sb("l0_cos", [P, TILES, D0]), sb("l0_sin", [P, TILES, D0])
        eps = sb("l0_eps", [P, 1])
        xin = sb("l0_x", [P, RING, 2, D])
        x1, biased, y = sb("l0_x1", [P, 2, D]), sb("l0_biased", [P, 2, D]), sb("l0_y", [P, 2, 2, D])
        scaled, normed = sb("l0_scaled", [P, 3, 2, D]), sb("l0_normed", [P, 2, D])
        stats, mv = sb("l0_stats", [P, 3, 2, 6]), sb("l0_mean_var", [P, 3, 2, 2])
        std, rstd = sb("l0_std", [P, 3, 2]), sb("l0_rstd", [P, 3, 2])
        h, hT = sb("l0_h", [P, 2, D]), sb("l0_hT", [P, 2, P])
        raw = sb("l0_raw", [P, 2, 2, 2 * D])
        straight, turned = sb("l0_straight", [P, 2, 2 * D]), sb("l0_turned", [P, 2, 2 * D])
        rotated = sb("l0_rotated", [P, 2, 2 * D])
        qk = sb("l0_qk", [P, 2, 2, 2 * D])
        v1 = sb("l0_v1", [P, 2, 2, H0, V0])
        kv = sb("l0_kv", [P, 2, 2, H0, D0, V0])
        cum = sb("l0_cum", [P, 2, H0, D0, V0])
        prod = sb("l0_prod", [P, 2, H0, D0, V0])
        nd = sb("l0_numden", [P, 2, H0, V0])
        den, rden = sb("l0_den", [P, 2, H0]), sb("l0_rden", [P, 2, H0])
        o, oT = sb("l0_o", [P, 2, D]), sb("l0_oT", [P, 2, P])
        hT_ps, oT_ps, y_ps = s.psum("l0_hT_ps", [P, 2, 256]), s.psum("l0_oT_ps", [P, 2, 256]), s.psum("l0_y_ps", [P, 2, 256])
        proj_ps, cum_ps = s.psum("l0_proj_ps", [P, 2, 512]), s.psum("l0_cum_ps", [P, 3, 512])

        loaded, ready, settled = s.sem("l0_loaded"), s.sem("l0_ready"), s.sem("l0_settled")
        x_in = [Signal(s, f"l0_x_in{k}") for k in range(RING)]
        y_stored = [Signal(s, f"l0_y_stored{k}", 32) for k in range(2)]
        dve_steps = s.sem("l0_dve_steps")
        mv_done = [Signal(s, f"l0_mv_done{k}") for k in range(3)]
        std_done = [Signal(s, f"l0_std_done{k}") for k in range(3)]
        h_done, hT_ps_done, hT_done = Signal(s, "l0_h_done"), Signal(s, "l0_hT_ps_done", 1), Signal(s, "l0_hT_done", 1)
        proj_done, raw_done = Signal(s, "l0_proj_done", 1), Signal(s, "l0_raw_done", 1)
        straight_done, rotated_done, qk_done = Signal(s, "l0_straight_done"), Signal(s, "l0_rotated_done", 1), Signal(s, "l0_qk_done", 1)
        kv_done, cum_ps_done, cum_done = Signal(s, "l0_kv_done", 2), Signal(s, "l0_cum_ps_done", 6), Signal(s, "l0_cum_done", 3)
        prod_done = [Signal(s, f"l0_prod_done{t}", 1) for t in range(2)]
        sums_done = Signal(s, "l0_sums_done", 2)
        o_done, oT_ps_done, oT_done = Signal(s, "l0_o_done"), Signal(s, "l0_oT_ps_done", 1), Signal(s, "l0_oT_done", 1)
        y_ps_done, x1_done, biased_done, y_done = (Signal(s, "l0_y_ps_done", 1), Signal(s, "l0_x1_done", 2),
                                                   Signal(s, "l0_biased_done"), Signal(s, "l0_y_done", 1))

        LOADS = 8
        BANKS = len(HEADS_OF_BANK)
        first = [sum(HEADS_OF_BANK[:k]) for k in range(BANKS)]

        def bank(k):
            return slice(first[k], first[k] + HEADS_OF_BANK[k]), HEADS_OF_BANK[k] * D0 * V0

        def products(t, par):
            flat = "p h d m -> p (h d) m"
            return (prod[:, t].rearrange(flat), cum[:, t].rearrange(flat), qk[:, par, t, 0:D].unsqueeze(2).to_broadcast([P, D, V0]))

        with nc.Block() as block:

            @block.sync
            def _(sp):
                for dst, src in ((consts[:, :, :], mods[0:7].rearrange("m p d -> p m d")),
                                 (wqkv_sb[:, :], wqkv), (wo_sb[:, :], wo), (ident_sb[:, :], ident),
                                 (upto_sb[:, :], upto), (last_sb[:, :], last_of_batch), (cos_sb[:, :, :], cos2),
                                 (sin_sb[:, :, :], sin2)):
                    sp.dma_start(dst, src).then_inc(loaded, 16)
                for k in range(2):
                    y_stored[k].give_ahead(sp)

                def load(n, slot):
                    for t in range(2):
                        x_in[slot].mark(sp.dma_start(xin[:, slot, t, :], x_t[n * 2 + t]), 16)

                def store(n, par):
                    y_done.wait(sp, n + 1)
                    for t in range(2):
                        y_stored[par].mark(sp.dma_start(out_t[n * 2 + t], y[:, par, t, :]), 16)

                for n in range(3):
                    load(n, n)

                def body(i, b):
                    n = i * RING + b
                    if in_range(i, b + 3, RING):
                        x1_done.wait(sp, n)
                        load(n + 3, (b + 3) % RING)
                    if in_range(i, b - 1, RING):
                        store(n - 1, (b - 1) % 2)

                all_rounds(sp, RING, body)
                store(PAIRS - 1, (PAIRS - 1) % 2)
                for k in range(2):
                    y_stored[k].wait(sp, PAIRS // 2 * 32)

            @block.gpsimd
            def _(pool):
                pool.memset(eps[:, :], EPS_LN)
                pool.memset(v1[:, :, :, :, :], 1.0)
                pool.memset(cum[:, 1], 0.0).then_inc(ready, 1)
                qk_done.give_ahead(pool)
                cum_ps_done.give_ahead(pool)
                rotated_done.give_ahead(pool)
                sums_done.give_ahead(pool)
                y_done.give_ahead(pool)
                pool.wait_ge(loaded, LOADS * 16)

                def rotate(n, par):
                    raw_done.wait(pool, n + 1)
                    rotated_done.wait(pool, n)
                    straight_done.mark(pool.tensor_tensor(
                        straight[:, :, :].rearrange("p t (g d) -> p t g d", d=D0),
                        raw[:, par].rearrange("p t (g d) -> p t g d", d=D0),
                        cos_sb[:, bass.ds(n * 2, 2), :].unsqueeze(2).to_broadcast([P, 2, 2 * H0, D0]), ALU.mult))

                def multiply(n, par):
                    qk_done.wait(pool, n + 1)
                    cum_ps_done.wait(pool, 6 * (n - 1))
                    for t in range(2):
                        k = qk[:, par, t, D:2 * D].rearrange("p (h d) -> p h d", d=D0)
                        kv_done.mark(pool.tensor_tensor(
                            kv[:, par, t], k.unsqueeze(3).to_broadcast([P, H0, D0, V0]),
                            v1[:, par, t].unsqueeze(2).to_broadcast([P, H0, D0, V0]), ALU.mult))

                def attend(n, par):
                    cum_done.wait(pool, 6 * n + 6)
                    sums_done.wait(pool, 2 * n)
                    dst, sums, q = products(1, par)
                    prod_done[1].mark(pool.tensor_tensor(dst, sums, q, ALU.mult))

                def bias(n):
                    x1_done.wait(pool, n + 1)
                    y_done.wait(pool, n)
                    biased_done.mark(pool.tensor_tensor(
                        biased[:, :, :], x1[:, :, :], consts[:, M0_BIAS2, :].unsqueeze(1).to_broadcast([P, 2, D]), ALU.add))

                rotate(0, 0)
                multiply(0, 0)

                def body(i, b):
                    n = i * RING + b
                    if in_range(i, b + 1, RING):
                        rotate(n + 1, (b + 1) % 2)
                    attend(n, b % 2)
                    if in_range(i, b + 1, RING):
                        multiply(n + 1, (b + 1) % 2)
                    if in_range(i, b - 1, RING):
                        bias(n - 1)

                all_rounds(pool, RING, body)
                bias(PAIRS - 1)

            @block.scalar
            def _(act):
                act.wait_ge(ready, 1)
                kv_done.give_ahead(act)
                y_ps_done.give_ahead(act)
                for t in range(2):
                    prod_done[t].give_ahead(act)

                def root(k, n):
                    mv_done[k].wait(act, n + 1)
                    std_done[k].mark(act.activation(std[:, k, :], mv[:, k, :, 1], ACT.Sqrt, bias=eps[:, 0:1]))

                def turn(n):
                    hT_ps_done.wait(act, n + 1)
                    proj_done.wait(act, n)
                    hT_done.mark(act.copy(hT[:, :, :], hT_ps[:, :, 0:P]))

                def project(n, par):
                    proj_done.wait(act, n + 1)
                    rotated_done.wait(act, n - 1)
                    kv_done.wait(act, 2 * (n - 1))
                    act.copy(raw[:, par], proj_ps[:, :, 0:2 * D])
                    raw_done.mark(act.copy(v1[:, par, :, :, 0:D0],
                                           proj_ps[:, :, 2 * D:3 * D].rearrange("p t (h d) -> p t h d", d=D0)))

                def rectify(n, par):
                    rotated_done.wait(act, n + 1)
                    for t in range(2):
                        prod_done[t].wait(act, n - 1)
                    qk_done.mark(act.activation(qk[:, par, :, :], rotated[:, :, :], ACT.Relu))

                def sums(n, t):
                    prod_done[t].wait(act, n)
                    for k in range(BANKS):
                        heads, width = bank(k)
                        cum_ps_done.wait(act, 6 * n + 3 * t + k + 1)
                        cum_done.mark(act.copy(cum[:, t, heads].rearrange("p h d m -> p (h d m)"), cum_ps[:, k, 0:width]))

                def attended(n):
                    oT_ps_done.wait(act, n + 1)
                    y_ps_done.wait(act, n)
                    oT_done.mark(act.copy(oT[:, :, :], oT_ps[:, :, 0:P]))

                for n in range(2):
                    root(0, n)
                    turn(n)
                    if n == 0:
                        proj_done.wait(act, 1)
                        act.copy(raw[:, 0], proj_ps[:, :, 0:2 * D])
                        raw_done.mark(act.copy(v1[:, 0, :, :, 0:D0],
                                               proj_ps[:, :, 2 * D:3 * D].rearrange("p t (h d) -> p t h d", d=D0)))
                rotated_done.wait(act, 1)
                qk_done.mark(act.activation(qk[:, 0, :, :], rotated[:, :, :], ACT.Relu))
                project(1, 1)

                def body(i, b):
                    n = i * RING + b
                    sums(n, 0)
                    if in_range(i, b - 1, RING):
                        attended(n - 1)
                    if in_range(i, b + 2, RING):
                        root(0, n + 2)
                    sums(n, 1)
                    if in_range(i, b + 1, RING):
                        rectify(n + 1, (b + 1) % 2)
                    if in_range(i, b + 2, RING):
                        turn(n + 2)
                    if in_range(i, b - 1, RING):
                        root(1, n - 1)
                    if in_range(i, b + 2, RING):
                        project(n + 2, b % 2)
                    if in_range(i, b - 1, RING):
                        root(2, n - 1)

                all_rounds(act, RING, body)
                attended(PAIRS - 1)
                root(1, PAIRS - 1)
                root(2, PAIRS - 1)

            @block.tensor
            def _(pe):
                pe.wait_ge(loaded, LOADS * 16)
                pe.wait_ge(ready, 1)
                cum_done.give_ahead(pe)
                raw_done.give_ahead(pe)
                x1_done.give_ahead(pe)
                oT_ps_done.give_ahead(pe)
                proj_done.give_ahead(pe)
                hT_done.give_ahead(pe)
                oT_done.give_ahead(pe)

                def turn(n):
                    h_done.wait(pe, n + 1)
                    hT_done.wait(pe, n)
                    for t in range(2):
                        last = pe.transpose(hT_ps[:, t, 0:P], h[:, t, :], ident_sb[:, :])
                    hT_ps_done.mark(last)

                def project(n):
                    hT_done.wait(pe, n + 1)
                    raw_done.wait(pe, n)
                    for t in range(2):
                        last = pe.matmul(proj_ps[:, t, 0:3 * D], hT[:, t, :], wqkv_sb[:, :], start=True, stop=True)
                    proj_done.mark(last)

                def sums(n, t, par):
                    kv_done.wait(pe, 2 * n + t + 1)
                    for k in range(BANKS):
                        heads, width = bank(k)
                        cum_done.wait(pe, 6 * n + 3 * t + k - 3 + 1)
                        pe.matmul(cum_ps[:, k, 0:width], upto_sb[:, :],
                                  kv[:, par, t, heads].rearrange("p h d m -> p (h d m)"), start=True, stop=False)
                        cum_ps_done.mark(pe.matmul(
                            cum_ps[:, k, 0:width], last_sb[:, :],
                            cum[:, 1 - t, heads].rearrange("p h d m -> p (h d m)"), start=False, stop=True))

                def attended(n):
                    o_done.wait(pe, n + 1)
                    oT_done.wait(pe, n)
                    for t in range(2):
                        last = pe.transpose(oT_ps[:, t, 0:P], o[:, t, :], ident_sb[:, :])
                    oT_ps_done.mark(last)

                def output(n):
                    oT_done.wait(pe, n + 1)
                    x1_done.wait(pe, n)
                    for t in range(2):
                        last = pe.matmul(y_ps[:, t, 0:D], oT[:, t, :], wo_sb[:, :], start=True, stop=True)
                    y_ps_done.mark(last)

                for n in range(2):
                    turn(n)
                    project(n)

                def body(i, b):
                    n = i * RING + b
                    sums(n, 0, b % 2)
                    if in_range(i, b - 1, RING):
                        attended(n - 1)
                    sums(n, 1, b % 2)
                    if in_range(i, b - 1, RING):
                        output(n - 1)
                    if in_range(i, b + 2, RING):
                        turn(n + 2)
                        project(n + 2)

                all_rounds(pe, RING, body)
                attended(PAIRS - 1)
                output(PAIRS - 1)

            @block.vector
            def _(dve):
                dve.wait_ge(loaded, LOADS * 16)
                hT_ps_done.give_ahead(dve)
                steps = Steps(dve, dve_steps)

                def mod(k):
                    return consts[:, k, :]

                class Norm:

                    def __init__(self, k, n, src, gain):
                        self.k, self.n, self.src, self.gain = k, n, src, gain

                    def stats(self):
                        for t in range(2):
                            last = dve.bn_stats(stats[:, self.k, t, :], self.src[:, t, :])
                        self.had = steps.mark(last)

                    def mean(self):
                        steps.wait(self.had)
                        settle(dve, settled)
                        for t in range(2):
                            last = dve.bn_aggr(mv[:, self.k, t, :], stats[:, self.k, t, :])
                        mv_done[self.k].mark(last)

                    def scale(self):
                        mv_done[self.k].wait(dve, self.n + 1)
                        for t in range(2):
                            last = dve.scalar_tensor_tensor(scaled[:, self.k, t, :], self.src[:, t, :], mv[:, self.k, t, 0:1],
                                                            mod(self.gain), ALU.subtract, ALU.mult)
                        self.had = steps.mark(last)

                    def invert(self):
                        std_done[self.k].wait(dve, self.n + 1)
                        self.had = steps.mark(dve.reciprocal(rstd[:, self.k, :], std[:, self.k, :]))

                    def finish(self, dst, shift):
                        steps.wait(self.had)
                        for t in range(2):
                            last = dve.scalar_tensor_tensor(dst[:, t, :], scaled[:, self.k, t, :], rstd[:, self.k, t:t + 1],
                                                            mod(shift) if isinstance(shift, int) else shift[:, t, :],
                                                            ALU.mult, ALU.add)
                        return last

                def add_x(n, slot, had):
                    steps.wait(had)
                    x1_done.mark(dve.tensor_tensor(x1[:, :, :], x1[:, :, :], xin[:, slot], ALU.add))
                    x1_done.wait(dve, n + 1)

                def finish(n, par, uses, norm):
                    norm.invert()
                    biased_done.wait(dve, n + 1)
                    y_stored[par].wait(dve, 32 * uses)
                    y_done.mark(norm.finish(y[:, par], biased))

                def turn(n, par):
                    raw_done.wait(dve, n + 1)
                    pairs = [a.rearrange("p t (g f e) -> p t g f e", f=D0 // 2, e=2) for a in (raw[:, par], turned[:, :, :])]
                    for t in range(2):
                        sin = sin_sb[:, bass.ds(n * 2 + t, 1), :].rearrange("p a (f e) -> p a f e", e=2)
                        for e in range(2):
                            last = dve.tensor_tensor(pairs[1][:, t, :, :, e], pairs[0][:, t, :, :, 1 - e],
                                                     sin[:, :, :, e].to_broadcast([P, 2 * H0, D0 // 2]), ALU.mult)
                    return steps.mark(last)

                def rotate(n, had):
                    steps.wait(had)
                    straight_done.wait(dve, n + 1)
                    qk_done.wait(dve, n)
                    rotated_done.mark(dve.tensor_tensor(rotated[:, :, :], straight[:, :, :], turned[:, :, :], ALU.add))

                def product(n, par):
                    cum_done.wait(dve, 6 * n + 3)
                    dst, sums, q = products(0, par)
                    prod_done[0].mark(dve.tensor_tensor(dst, sums, q, ALU.mult))

                def reduce(n, t):
                    prod_done[t].wait(dve, n + 1)
                    sums_done.mark(dve.tensor_reduce(nd[:, t], prod[:, t].rearrange("p h d m -> p h m d"), AX.X, ALU.add))

                A, B1, B2, C = 3, 1, 2, 8

                def body(i, b):
                    n = i * RING + b
                    has_a, has_b1, has_c = in_range(i, b + 2, RING), in_range(i, b + 1, RING), in_range(i, b - 1, RING)
                    steps.start(n * (A + B1 + B2 + C) + 2 * A + B1 - (C if has_c else 0) - (0 if has_b1 else A))
                    if has_a:
                        norm0 = Norm(0, n + 2, xin[:, (b + 2) % RING], M0_SCALE)
                        x_in[(b + 2) % RING].wait(dve, 32 * (i + (b + 2) // RING) + 32)
                        norm0.stats()
                    if has_b1:
                        turned_at = turn(n + 1, (b + 1) % 2)
                    if has_a:
                        norm0.mean()
                        norm0.scale()
                    if has_b1:
                        rotate(n + 1, turned_at)
                    if has_a:
                        norm0.invert()
                        hT_ps_done.wait(dve, n + 2)
                        h_done.mark(norm0.finish(h, M0_SHIFT))
                    if has_c:
                        norm1, norm2 = Norm(1, n - 1, x1, M0_SCALE2), Norm(2, n - 1, normed, M0_GAIN2)
                    product(n, b % 2)
                    if has_c:
                        y_ps_done.wait(dve, n)
                        gated_at = steps.mark(dve.tensor_tensor(x1[:, :, :], y_ps[:, :, 0:D], two(mod(M0_GATE)), ALU.mult))
                    reduce(n, 0)
                    if has_c:
                        add_x(n - 1, (b - 1) % RING, gated_at)
                        norm1.stats()
                        norm1.mean()
                        norm1.scale()
                    reduce(n, 1)
                    if has_c:
                        norm1.invert()
                        normed_at = steps.mark(norm1.finish(normed, M0_SHIFT2))
                    sums_done.wait(dve, 2 * n + 2)
                    den_at = steps.mark(dve.tensor_scalar(den[:, :, :], nd[:, :, :, D0], EPS_ATT, None, ALU.add))
                    if has_c:
                        steps.wait(normed_at)
                        norm2.stats()
                    steps.wait(den_at)
                    rden_at = steps.mark(dve.reciprocal(rden[:, :, :], den[:, :, :]))
                    if has_c:
                        norm2.mean()
                    steps.wait(rden_at)
                    oT_ps_done.wait(dve, n)
                    o_done.mark(dve.tensor_tensor(o[:, :, :].rearrange("p t (h d) -> p t h d", d=D0), nd[:, :, :, 0:D0],
                                                  rden[:, :, :].unsqueeze(3).to_broadcast([P, 2, H0, D0]), ALU.mult))
                    if has_c:
                        norm2.scale()
                        finish(n - 1, (b - 1) % 2, i * 2 + (b - 1) // 2, norm2)
                    assert steps.n == A * has_a + B1 * has_b1 + B2 + C * has_c, steps.n

                steps.start(0)
                for n in range(2):
                    norm0 = Norm(0, n, xin[:, n], M0_SCALE)
                    x_in[n].wait(dve, 32)
                    norm0.stats()
                    norm0.mean()
                    norm0.scale()
                    norm0.invert()
                    hT_ps_done.wait(dve, n)
                    h_done.mark(norm0.finish(h, M0_SHIFT))
                rotate(0, turn(0, 0))
                all_rounds(dve, RING, body)
                n = PAIRS - 1
                steps.start(PAIRS * (A + B1 + B2 + C) - C + 0)
                norm1, norm2 = Norm(1, n, x1, M0_SCALE2), Norm(2, n, normed, M0_GAIN2)
                y_ps_done.wait(dve, n + 1)
                add_x(n, n % RING, steps.mark(dve.tensor_tensor(x1[:, :, :], y_ps[:, :, 0:D], two(mod(M0_GATE)), ALU.mult)))
                norm1.stats()
                norm1.mean()
                norm1.scale()
                norm1.invert()
                steps.wait(steps.mark(norm1.finish(normed, M0_SHIFT2)))
                norm2.stats()
                norm2.mean()
                norm2.scale()
                finish(n, n % 2, n // 2, norm2)


def layer1_attention(nc, x, wq, wk, wv, wo, mods, ident, fold, out):
    s = Scope(nc)
    x_t, out_t = tiles_of(x), tiles_of(out)
    HEADS, DH = 64, 64
    HALF = P // 2
    TOK = 2 * P
    CHUNKS = HEADS * DH // P
    UNIT = 4
    UNITS = CHUNKS // UNIT
    SCALE = DH ** -0.5
    BATCHES = [7] * 4 + [6] * 6
    assert sum(BATCHES) == HALF
    NB = len(BATCHES)
    W = DH + 1
    PROJ = 2 * NB
    ORDER = [(w, u) for u in range(UNITS) for w in "kq"] + [("v", u) for u in range(UNITS)]
    ROUND = PROJ + len(ORDER)
    V_BY_DVE = [u for u in range(UNITS) if u % 2]
    V_BY_ACT = [u for u in range(UNITS) if u % 2 == 0]
    FOLD_AFTER = len(ORDER) - UNITS + 1

    def evacuates(engine, place):
        if place < PROJ:
            return True
        w, u = ORDER[place - PROJ]
        return (w == "q" or (w == "v" and u in V_BY_ACT)) == (engine == "act")

    def evacuated(engine, g, place):
        of = [evacuates(engine, p) for p in range(ROUND)]
        return g * sum(of) + sum(of[PROJ:]) + sum(of[:place + 1])

    with s.stack:
        sb = s.sb
        consts = sb("l1_mods", [P, 4, D])
        ident_sb, fold_sb = sb("l1_ident", [P, P]), sb("l1_fold", [P, P])
        w_hi = {w: sb(f"l1_w{w}_hi", [P, HEADS * DH], F32R) for w in "qkv"}
        w_lo = {w: sb(f"l1_w{w}_lo", [P, HEADS * DH], F32R) for w in "qkv"}
        wo_sb = sb("l1_wo", [P, CHUNKS, D])
        q = sb("l1_q", [P, P, HEADS])
        v = sb("l1_v", [P, P, W])
        att = sb("l1_att", [P, CHUNKS, P])
        ksum = sb("l1_ksum", [P, UNIT, TOK])
        ks = sb("l1_ks", [P, P])
        den_a, rden_a = sb("l1_den_a", [HALF, 8]), sb("l1_rden_a", [HALF, 8])
        den_b, rden_b = sb("l1_den_b", [P, 2, HALF]), sb("l1_rden_b", [P, 2, HALF])
        eps, eps_att = sb("l1_eps", [P, 1]), sb("l1_eps_att", [P, 1])
        xin, h = sb("l1_x", [P, 2, D]), sb("l1_h", [P, 2, D])
        xres, y = sb("l1_xres", [P, 2, D]), sb("l1_y", [P, 2, D])
        stats, mv = sb("l1_stats", [P, 2, 6]), sb("l1_mean_var", [P, 2, 2])
        std, rstd = sb("l1_std", [P, 2]), sb("l1_rstd", [P, 2])
        hT_hi, hT_lo = sb("l1_hT_hi", [P, 2, 2, HALF], F32R), sb("l1_hT_lo", [P, 2, 2, HALF], F32R)
        ring = s.psum("l1_ring", [P, 3, 2, 512])
        o_ps = s.psum("l1_o_ps", [P, 512])
        misc_ps = s.psum("l1_misc_ps", [P, 512])
        hT_ps, ks_ps = misc_ps[:, 0:TOK], misc_ps[:, TOK:2 * TOK]

        loaded, split_done, ready = s.sem("l1_loaded"), s.sem("l1_split_done"), s.sem("l1_ready")
        dve_steps = s.sem("l1_dve_steps")
        settled, pe_settled = s.sem("l1_settled"), s.sem("l1_pe_settled")
        x_in = Signal(s, "l1_x_in")
        y_stored = [Signal(s, f"l1_y_stored{k}", 16) for k in range(2)]
        unit_done = Signal(s, "l1_unit_done")
        evac = {"act": Signal(s, "l1_act_evac"), "dve": Signal(s, "l1_dve_evac")}
        mv_done, std_done, h_done = Signal(s, "l1_mv_done"), Signal(s, "l1_std_done"), Signal(s, "l1_h_done")
        hT_ps_done, hT_hi_done, hT_done = Signal(s, "l1_hT_ps_done", 1), Signal(s, "l1_hT_hi_done"), Signal(s, "l1_hT_done")
        ks_ps_done, ks_done = Signal(s, "l1_ks_ps_done"), Signal(s, "l1_ks_done")
        v_pool_done, rden_b_done, att_pool_done = Signal(s, "l1_v_pool_done"), Signal(s, "l1_rden_b_done"), Signal(s, "l1_att_pool_done")
        o_ps_done, y_done, xres_done = Signal(s, "l1_o_ps_done"), Signal(s, "l1_y_done", 2), Signal(s, "l1_xres_done")

        LOADS = 8

        def buffer(place):
            return ring[:, place % 3]

        def index(g, place):
            return g * ROUND + place + (ROUND - PROJ)

        def unit_ready(eng, g, place):
            unit_done.wait(eng, index(g, place) + 1)

        def wait_evacuated(eng, by, g, place):
            evac[by].wait(eng, evacuated(by, g, place))

        def place_of(w, u):
            return PROJ + ORDER.index((w, u))

        def rounds(eng, body, last):
            with eng.Fori(0, PAIRS - 1) as g:
                body(g)
            last(PAIRS - 1)

        def pieces(place):
            ps = buffer(place).rearrange("p a b -> p (a b)").rearrange("p (c t) -> p c t", t=TOK)
            for par in range(2):
                for ab in range(2):
                    yield par, ab, ps[HALF * par:HALF * par + HALF, :, P * ab:P * ab + P]

        def half(ab):
            return slice(HALF * ab, HALF * ab + HALF)

        def v_piece(u, par, ab):
            first = 32 * par + UNIT * u
            return v[half(ab), :, first:first + UNIT].rearrange("p t c -> p c t")

        def batch(k):
            return sum(BATCHES[:k]), BATCHES[k]

        def products(place, ab, m):
            return buffer(place)[half(ab), ab, 0:m * W].rearrange("p (t j) -> p t j", j=W)

        with nc.Block() as block:

            @block.sync
            def _(sp):
                sp.dma_start(q[:, 0:HALF, :].rearrange("p a b -> p (a b)"), wq).then_inc(loaded, 16)
                sp.dma_start(q[:, HALF:P, :].rearrange("p a b -> p (a b)"), wk).then_inc(loaded, 16)
                sp.dma_start(att[:, :, :].rearrange("p a b -> p (a b)"), wv).then_inc(loaded, 16)
                sp.dma_start(consts[:, :, :], mods[M1_SHIFT:M1_BIAS + 1].rearrange("m p d -> p m d")).then_inc(loaded, 16)
                sp.dma_start(ident_sb[:, :], ident).then_inc(loaded, 16)
                sp.dma_start(fold_sb[:, :], fold).then_inc(loaded, 16)
                for par in range(2):
                    sp.dma_start(wo_sb[half(par), :, :],
                                 wo.rearrange("(i c q) e -> q i c e", i=HEADS, q=2)[par]).then_inc(loaded, 16)

                def load(g):
                    for t in range(2):
                        x_in.mark(sp.dma_start(xin[:, t, :], x_t[g * 2 + t]), 16)

                for k in range(2):
                    y_stored[k].give_ahead(sp)

                def store(g):
                    for t in range(2):
                        y_done.wait(sp, 2 * g + t + 1)
                        y_stored[t].mark(sp.dma_start(out_t[g * 2 + t], y[:, t, :]), 16)

                load(0)

                def body(g):
                    xres_done.wait(sp, g + 1)
                    load(g + 1)
                    store(g)

                rounds(sp, body, store)
                for k in range(2):
                    y_stored[k].wait(sp, PAIRS * 16)

            @block.gpsimd
            def _(pool):
                pool.memset(eps[:, :], EPS_LN)
                pool.memset(eps_att[:, :], EPS_ATT).then_inc(ready, 1)
                y_done.give_ahead(pool)
                hT_ps_done.give_ahead(pool)
                pool.wait_ge(loaded, LOADS * 16)

                def scale_v(g):
                    ks_done.wait(pool, g + 2)
                    for u in V_BY_ACT:
                        wait_evacuated(pool, "act", g, place_of("v", u))
                        part = v[:, :, 0:DH].rearrange("p t (q c) -> p t q c", q=2)[:, :, :, UNIT * u:UNIT * u + UNIT]
                        last = pool.tensor_tensor(part, part, ks[:, :].unsqueeze(2).unsqueeze(3).to_broadcast([P, P, 2, UNIT]), ALU.mult)
                    v_pool_done.mark(last)

                def residual(g):
                    x_in.wait(pool, 32 * g + 32)
                    h_done.wait(pool, g + 1)
                    y_done.wait(pool, 2 * g)
                    xres_done.mark(pool.tensor_tensor(
                        xres[:, :, :], xin[:, :, :], consts[:, 3, :].unsqueeze(1).to_broadcast([P, 2, D]), ALU.add))

                def scale_att(g, sub):
                    for k in range(NB):
                        t0, m = batch(k)
                        rden_b_done.wait(pool, NB * (2 * g + sub) + k + 1)
                        part = att[:, :, HALF + t0:HALF + t0 + m].rearrange("p c t -> p t c")
                        last = pool.tensor_tensor(
                            part, part, rden_b[:, sub, t0:t0 + m].unsqueeze(2).to_broadcast([P, m, CHUNKS]), ALU.mult)
                    att_pool_done.mark(last)

                def body(g):
                    residual(g)
                    scale_att(g, 0)
                    scale_att(g, 1)

                def loop(g):
                    body(g)
                    scale_v(g)

                scale_v(-1)
                rounds(pool, loop, body)

            @block.scalar
            def _(act):
                act.wait_ge(ready, 1)
                act.wait_ge(split_done, 2)

                def prepare(g):
                    mv_done.wait(act, g + 1)
                    std_done.mark(act.activation(std[:, :], mv[:, :, 1], ACT.Sqrt, bias=eps[:, 0:1]))
                    hT_ps_done.wait(act, g + 1)
                    hT_hi_done.mark(act.copy(hT_hi[:, :, :, :].rearrange("p a s t -> p s a t"),
                                             hT_ps.rearrange("p (s a t) -> p s a t", s=2, a=2)))

                def project(g):
                    for n, (w, u) in enumerate(ORDER):
                        place = PROJ + n
                        if w == "q":
                            unit_ready(act, g, place)
                            for par, ab, ps in pieces(place):
                                dst = q[half(ab), :, 2 * UNIT * u + par:2 * UNIT * (u + 1):2].rearrange("p t c -> p c t")
                                last = act.activation(dst, ps, ACT.Relu, scale=SCALE)
                            evac["act"].mark(last)
                        elif w == "v":
                            if u in V_BY_ACT:
                                unit_ready(act, g, place)
                                for par, ab, ps in pieces(place):
                                    last = act.copy(v_piece(u, par, ab), ps)
                                evac["act"].mark(last)
                            if u == V_BY_ACT[0]:
                                ks_ps_done.wait(act, g + 2)
                                for ab in range(2):
                                    src = ks_ps[half(ab), P * ab:P * ab + P]
                                    act.copy(v[half(ab), :, DH], src)
                                    last = act.copy(ks[half(ab), :], src)
                                ks_done.mark(last)

                def attend(g, sub):
                    for k in range(NB):
                        t0, m = batch(k)
                        place = NB * sub + k
                        unit_ready(act, g, place)
                        ps = products(place, 1, m)
                        for par in range(2):
                            act.activation(den_b[half(par), sub, t0:t0 + m], ps[:, :, DH], ACT.Identity,
                                           bias=eps_att[half(1), 0:1])
                            last = act.copy(att[half(par), :, HALF + t0:HALF + t0 + m].rearrange("p c t -> p t c"),
                                            ps[:, :, CHUNKS * par:CHUNKS * par + CHUNKS])
                        evac["act"].mark(last)

                prepare(0)
                project(-1)

                def body(g):
                    attend(g, 0)
                    prepare(g + 1)
                    attend(g, 1)
                    project(g)

                def last(g):
                    attend(g, 0)
                    attend(g, 1)

                rounds(act, body, last)

            @block.tensor
            def _(pe):
                pe.wait_ge(loaded, LOADS * 16)
                pe.wait_ge(split_done, 2)

                def acquire(g, place):
                    if isinstance(g, int) and g == -1 and place - 3 < PROJ:
                        return
                    if place >= 3:
                        user = place - 3
                    else:
                        user = max(p for p in range(ROUND) if p % 3 == place)
                        g = g - 1
                    for by in evac:
                        if evacuates(by, user):
                            wait_evacuated(pe, by, g, user)

                def turn(g):
                    h_done.wait(pe, g + 1)
                    if not isinstance(g, int) or g:
                        hT_done.wait(pe, g)
                    for t in range(2):
                        last = pe.transpose(hT_ps[:, t * P:t * P + P], h[:, t, :], ident_sb[:, :])
                    hT_ps_done.mark(last)

                def project(g):
                    hT_done.wait(pe, g + 2)
                    hi, lo = (a[:, :, :, :].rearrange("p a s t -> p (a s t)") for a in (hT_hi, hT_lo))
                    for n, (w, u) in enumerate(ORDER):
                        if n == FOLD_AFTER:
                            wait_evacuated(pe, "dve", g, place_of("k", UNITS - 1))
                            for k in range(UNIT):
                                last = pe.matmul(ks_ps, fold_sb[:, :], ksum[:, k, :], start=k == 0, stop=k == UNIT - 1)
                            ks_ps_done.mark(last)
                        place = PROJ + n
                        acquire(g, place)
                        ps = buffer(place).rearrange("p a b -> p (a b)").rearrange("p (c t) -> p c t", t=TOK)
                        for c in range(UNIT):
                            cols = slice((UNIT * u + c) * P, (UNIT * u + c) * P + P)
                            pe.matmul(ps[:, c], w_hi[w][:, cols], hi, start=True, stop=False)
                            pe.matmul(ps[:, c], w_hi[w][:, cols], lo, start=False, stop=False)
                            last = pe.matmul(ps[:, c], w_lo[w][:, cols], hi, start=False, stop=True)
                        unit_done.mark(last)

                def attend(g, sub):
                    if sub == 0:
                        v_pool_done.wait(pe, g + 1)
                        wait_evacuated(pe, "dve", g - 1, place_of("v", V_BY_DVE[-1]))
                    for k in range(NB):
                        t0, m = batch(k)
                        place = NB * sub + k
                        acquire(g, place)
                        settle(pe, pe_settled)
                        for t in range(m):
                            tok = HALF * sub + t0 + t
                            for ab in range(2):
                                last = pe.matmul(products(place, ab, m)[:, t], q[half(ab), tok, :], v[half(ab), tok, :],
                                                 start=True, stop=True)
                        unit_done.mark(last)

                def output(g, sub):
                    wait_evacuated(pe, "dve", g, NB * sub + NB - 1)
                    att_pool_done.wait(pe, 2 * g + sub + 1)
                    y_done.wait(pe, 2 * g + sub)
                    for c in range(CHUNKS):
                        last = pe.matmul(o_ps[:, 0:D], att[:, c, :], wo_sb[:, c, :], start=c == 0, stop=c == CHUNKS - 1)
                    o_ps_done.mark(last)

                turn(0)
                project(-1)

                def body(g):
                    attend(g, 0)
                    output(g, 0)
                    turn(g + 1)
                    attend(g, 1)
                    project(g)
                    output(g, 1)

                def last(g):
                    for sub in range(2):
                        attend(g, sub)
                        output(g, sub)

                rounds(pe, body, last)

            @block.vector
            def _(dve):
                dve.wait_ge(loaded, LOADS * 16)
                for w, src in (("q", q[:, 0:HALF, :]), ("k", q[:, HALF:P, :]), ("v", att[:, :, :])):
                    src = src.rearrange("p a b -> p (a b)")
                    last = dve.tensor_copy(w_hi[w][:, :], src)
                last.then_inc(split_done, 1)
                dve.wait_ge(split_done, 1)
                for w, src in (("q", q[:, 0:HALF, :]), ("k", q[:, HALF:P, :]), ("v", att[:, :, :])):
                    src = src.rearrange("p a b -> p (a b)")
                    last = dve.tensor_tensor(w_lo[w][:, :], src, w_hi[w][:, :].bitcast(F32), ALU.subtract)
                last.then_inc(split_done, 1)
                link = Chain(dve, dve_steps, 0)
                step = link.then

                def mod(k):
                    return consts[:, k, :].unsqueeze(1).to_broadcast([P, 2, D])

                def prepare(g):
                    x_in.wait(dve, 32 * g + 32)
                    for t in range(2):
                        last = dve.bn_stats(stats[:, t, :], xin[:, t, :])
                    step(last)
                    settle(dve, settled)
                    for t in range(2):
                        last = dve.bn_aggr(mv[:, t, :], stats[:, t, :])
                    mv_done.mark(last)
                    std_done.wait(dve, g + 1)
                    step(dve.reciprocal(rstd[:, :], std[:, :]))
                    hT_ps_done.wait(dve, g)
                    for t in range(2):
                        last = dve.tensor_scalar(h[:, t, :], xin[:, t, :], mv[:, t, 0:1], rstd[:, t:t + 1],
                                                 ALU.subtract, ALU.mult)
                    step(last)
                    step(dve.tensor_tensor(h[:, :, :], h[:, :, :], mod(1), ALU.mult))
                    h_done.mark(dve.tensor_tensor(h[:, :, :], h[:, :, :], mod(0), ALU.add))

                def rest(g):
                    hT_hi_done.wait(dve, g + 1)
                    hT_done.mark(dve.tensor_tensor(hT_lo[:, :, :, :].rearrange("p a s t -> p s a t"),
                                                   hT_ps.rearrange("p (s a t) -> p s a t", s=2, a=2),
                                                   hT_hi[:, :, :, :].bitcast(F32).rearrange("p a s t -> p s a t"), ALU.subtract))

                def project(g):
                    for n, (w, u) in enumerate(ORDER):
                        place = PROJ + n
                        if w == "k":
                            unit_ready(dve, g, place)
                            ps = buffer(place).rearrange("p a b -> p (a b)")
                            acc = ksum[:, :, :].rearrange("p c t -> p (c t)")
                            if u == 0:
                                last = dve.tensor_scalar(acc, ps, 0.0, None, ALU.max)
                            else:
                                wait_evacuated(dve, "dve", g, place_of("k", u - 1))
                                last = dve.scalar_tensor_tensor(acc, ps, 0.0, acc, ALU.max, ALU.add)
                            evac["dve"].mark(last)
                        elif w == "v" and u in V_BY_DVE:
                            if u == V_BY_DVE[0]:
                                ks_done.wait(dve, g + 2)
                            unit_ready(dve, g, place)
                            for par, ab, ps in pieces(place):
                                last = dve.tensor_tensor(v_piece(u, par, ab), ps,
                                                         ks[half(ab), :].unsqueeze(1).to_broadcast([HALF, UNIT, P]), ALU.mult)
                            evac["dve"].mark(last)

                def attend(g, sub):
                    for k in range(NB):
                        t0, m = batch(k)
                        place = NB * sub + k
                        unit_ready(dve, g, place)
                        ps = products(place, 0, m)
                        step(dve.tensor_scalar(den_a[:, 0:m], ps[:, :, DH], EPS_ATT, None, ALU.add))
                        step(dve.reciprocal(rden_a[:, 0:m], den_a[:, 0:m]))
                        for par in range(2):
                            last = dve.tensor_tensor(
                                att[half(par), :, t0:t0 + m].rearrange("p c t -> p t c"),
                                ps[:, :, CHUNKS * par:CHUNKS * par + CHUNKS],
                                rden_a[:, 0:m].unsqueeze(2).to_broadcast([HALF, m, CHUNKS]), ALU.mult)
                        evac["dve"].mark(last)
                        wait_evacuated(dve, "act", g, place)
                        rden_b_done.mark(dve.reciprocal(rden_b[:, sub, t0:t0 + m], den_b[:, sub, t0:t0 + m]))

                def residual(g, sub):
                    o_ps_done.wait(dve, 2 * g + sub + 1)
                    xres_done.wait(dve, g + 1)
                    y_stored[sub].wait(dve, 16 * g)
                    step(dve.tensor_tensor(y[:, sub, :], o_ps[:, 0:D], consts[:, 2, :], ALU.mult))
                    y_done.mark(dve.tensor_tensor(y[:, sub, :], y[:, sub, :], xres[:, sub, :], ALU.add))

                sizes = dict(prepare=4, rest=0, project=0, attend=2 * NB, residual=1)

                def stage(fn, at, *args):
                    link.base, link.n = at, 0
                    fn(*args)
                    assert link.n == sizes[fn.__name__], (fn.__name__, link.n)
                    return at + link.n

                head = stage(prepare, 0, 0)
                stage(rest, head, 0)
                head = stage(project, head, -1)
                per_round = sizes["prepare"] + sizes["project"] + 2 * (sizes["attend"] + sizes["residual"])

                def body(g):
                    at = stage(attend, head + g * per_round, g, 0)
                    at = stage(prepare, at, g + 1)
                    at = stage(residual, at, g, 0)
                    stage(rest, at, g + 1)
                    at = stage(attend, at, g, 1)
                    at = stage(project, at, g)
                    stage(residual, at, g, 1)

                def last(g):
                    at = head + g * per_round
                    for sub in range(2):
                        at = stage(attend, at, g, sub)
                        at = stage(residual, at, g, sub)

                rounds(dve, body, last)


def layer1_ffn(nc, x, in_w, in_b, out_w, out_b, ln1_g, ln1_b, wg, w1, b1, w2, b2, mods, ident, upto, same_batch,
               batch_before, other_position, tile_mask, falling, y1_dram, y1T_dram, out):
    s = Scope(nc)
    x_t, out_t = tiles_of(x), tiles_of(out)
    NH, DH = 4, 32
    E, FF = 8, 512
    FC = FF // P
    CAP = B * L // E
    SCALE = DH ** -0.5
    W = DH + 1
    RING = 4
    BLOCK = P // E
    with s.stack:
        sb = s.sb
        consts = sb("f_mods", [P, 4, D])
        rows = sb("f_rows", [P, 4, D])
        in_w_sb, in_b_sb, out_w_sb = sb("f_in_w", [P, 3 * D]), sb("f_in_b", [P, 2]), sb("f_out_w", [P, D])
        wg_sb, ident_sb = sb("f_wg", [P, E]), sb("f_ident", [P, P])
        upto_sb, same_sb, before_sb = sb("f_upto", [P, P]), sb("f_same", [P, P]), sb("f_before", [P, P])
        other_sb = sb("f_other", [P, P])
        eps, power = sb("f_eps", [P, 2]), sb("f_power", [P, 2])
        logits = sb("f_logits", [P, TILES, E])
        w12 = sb("f_w12", [P, E, D])
        bias = sb("f_bias", [P, TILES, D])
        coef = sb("f_coef", [P, TILES, E])

        with ExitStack() as part:
            def sb1(name, shape, dt=F32):
                return part.enter_context(nc.sbuf_tensor(name, shape, dt))

            def ps1(name, shape):
                return part.enter_context(nc.psum_tensor(name, shape, F32))

            xin, h = sb1("fa_x", [P, RING, 2, D]), sb1("fa_h", [P, 2, D])
            h_biased = sb1("fa_h_biased", [P, RING, 2, D])
            stats, mv = sb1("fa_stats", [P, 2, 2, 6]), sb1("fa_mean_var", [P, 2, 2, 2])
            scaled = sb1("fa_scaled", [P, 2, 2, D])
            shifted, rstd = sb1("fa_shifted", [P, 2, 2]), sb1("fa_rstd", [P, 2, 2])
            hT, kT = sb1("fa_hT", [P, 2, P]), sb1("fa_kT", [P, 2, P])
            qT = sb1("fa_qT", [P, NH, 2, P])
            v1 = sb1("fa_v1", [P, RING, 2, NH, W])
            ident_r, other_r = sb1("fa_ident_r", [P, P], F32R), sb1("fa_other_r", [P, P], F32R)
            score, top = sb1("fa_score", [P, NH, 2, P]), sb1("fa_top", [P, NH, 2])
            prob, probT = sb1("fa_prob", [P, NH, 2, P]), sb1("fa_probT", [P, NH, 2, P])
            rden, o, oT = sb1("fa_rden", [P, 2, NH]), sb1("fa_o", [P, 2, D]), sb1("fa_oT", [P, 2, P])
            z, y1, y1T = sb1("fa_z", [P, 2, D]), sb1("fa_y1", [P, 2, D]), sb1("fa_y1T", [P, 2, P])
            s_ps, probT_ps = ps1("fa_s_ps", [P, 2, 512]), ps1("fa_probT_ps", [P, 2, 512])
            t_ps, qk_ps = ps1("fa_t_ps", [P, 2, 2, P]), ps1("fa_qk_ps", [P, 2, 2 * P])
            r1_ps, r2_ps = ps1("fa_r1_ps", [P, 2, 2, D]), ps1("fa_r2_ps", [P, 512])
            s_of, probT_of = (a[:, :, :].rearrange("p b (h t k) -> p (b h) t k", h=2, t=2) for a in (s_ps, probT_ps))
            hT_ps, oT_ps, y1T_ps = t_ps[:, 0], t_ps[:, 1], t_ps[:, 1]
            v_ps, mha_ps = r1_ps[:, 0], r1_ps[:, 1]
            o_ps = r2_ps[:, 0:2 * NH * W].rearrange("p (t h d) -> p t h d", t=2, h=NH)
            logit_ps = r2_ps[:, 2 * NH * W:2 * NH * W + 2 * E].rearrange("p (t e) -> p t e", t=2)

            def sig(name):
                return Signal(s, "fa_" + name)

            loaded, ready, rounded = s.sem("fa_loaded"), s.sem("fa_ready"), s.sem("fa_rounded")
            dve_steps, pool_steps, settled = s.sem("fa_dve_steps"), s.sem("fa_pool_steps"), s.sem("fa_settled")
            x_in = [sig(f"x_in{k}") for k in range(RING)]
            mv_done, rstd_done = [sig(f"mv_done{k}") for k in range(2)], [sig(f"rstd_done{k}") for k in range(2)]
            h_done, h_biased_done, hT_ps_done, hT_done = sig("h_done"), sig("h_biased_done"), sig("hT_ps_done"), sig("hT_done")
            qk_ps_done, v_ps_done, qk_done, v_done = sig("qk_ps_done"), sig("v_ps_done"), sig("qk_done"), sig("v_done")
            s_ps_done, shifted_done, prob_done = sig("s_ps_done"), sig("shifted_done"), sig("prob_done")
            probT_ps_done, probT_done, o_ps_done, o_done = sig("probT_ps_done"), sig("probT_done"), sig("o_ps_done"), sig("o_done")
            oT_ps_done, oT_done, mha_ps_done, z_done = sig("oT_ps_done"), sig("oT_done"), sig("mha_ps_done"), sig("z_done")
            y1_done, y1T_ps_done, y1T_done = sig("y1_done"), sig("y1T_ps_done"), sig("y1T_done")
            logit_ps_done, logit_done = sig("logit_ps_done"), sig("logit_done")
            y1_stored, y1T_stored = sig("y1_stored"), sig("y1T_stored")
            LOADS = 15

            def rounds(eng, body):
                def with_stages(i, b):
                    body(i, b, [x for x, ahead in zip("ASOZTR", (2, 1, 0, -1, -2, -3)) if in_range(i, b + ahead, RING)])

                all_rounds(eng, RING, with_stages, 3)

            with nc.Block() as block:

                @block.sync
                def _(sp):
                    def load(n, slot):
                        for t in range(2):
                            x_in[slot].mark(sp.dma_start(xin[:, slot, t, :], x_t[n * 2 + t]), 16)

                    load(0, 0)
                    for dst, src in ((consts[:, :, :], mods[M1_SHIFT2:M1_BIAS2 + 1].rearrange("m p d -> p m d")),
                                     (in_w_sb[:, :], in_w), (out_w_sb[:, :], out_w), (wg_sb[:, :], wg),
                                     (in_b_sb[:, 0:1], in_b[0:D].rearrange("(p a) -> p a", a=1)),
                                     (in_b_sb[:, 1:2], in_b[D:2 * D].rearrange("(p a) -> p a", a=1)),
                                     (ident_sb[:, :], ident), (upto_sb[:, :], upto), (same_sb[:, :], same_batch),
                                     (before_sb[:, :], batch_before), (other_sb[:, :], other_position),
                                     (rows[:, 0, :], in_b[2 * D:3 * D].rearrange("(a d) -> a d", a=1).to_broadcast([P, D])),
                                     (rows[:, 1, :], out_b.rearrange("(a d) -> a d", a=1).to_broadcast([P, D])),
                                     (rows[:, 2, :], ln1_g.rearrange("(a d) -> a d", a=1).to_broadcast([P, D])),
                                     (rows[:, 3, :], ln1_b.rearrange("(a d) -> a d", a=1).to_broadcast([P, D]))):
                        sp.dma_start(dst, src).then_inc(loaded, 16)

                    def body(i, b, stages):
                        n = i * RING + b
                        if in_range(i, b + 3, RING) and not (isinstance(n, int) and n == -3):
                            h_done.wait(sp, n)
                            load(n + 3, (b + 3) % RING)
                        if "Z" in stages:
                            y1_done.wait(sp, n)
                            y1_stored.mark(sp.dma_start(y1_dram[n - 1], y1[:, :, :]), 16)
                        if "T" in stages:
                            y1T_done.wait(sp, n - 1)
                            y1T_stored.mark(sp.dma_start(y1T_dram[n - 2], y1T[:, :, :]), 16)

                    rounds(sp, body)
                    y1_stored.wait(sp, PAIRS * 16)
                    y1T_stored.wait(sp, PAIRS * 16)

                @block.gpsimd
                def _(pool):
                    pool.memset(eps[:, :], EPS_LN)
                    pool.memset(power[:, :], -0.5)
                    pool.memset(qT[:, :, :, :], 0.0)
                    pool.memset(v1[:, :, :, :, :], 1.0).then_inc(ready, 1)
                    pool.wait_ge(ready, 1)
                    pool.wait_ge(loaded, LOADS * 16)
                    steps = Steps(pool, pool_steps)

                    def root(k, n):
                        mv_done[k].wait(pool, n + 1)
                        steps.wait(steps.mark(pool.tensor_tensor(shifted[:, k, :], mv[:, k, :, 1], eps[:, :], ALU.add)))
                        rstd_done[k].mark(pool.tensor_tensor(rstd[:, k, :], shifted[:, k, :], power[:, :], ALU.pow))

                    def body(i, b, stages):
                        n = i * RING + b
                        steps.start(pairs_done(n + 2) + pairs_done(n - 1) if isinstance(n, int) else n * 2 + 1)
                        if "A" in stages:
                            root(0, n + 2)
                            h_done.wait(pool, n + 3)
                            z_done.wait(pool, n - 1)
                            h_biased_done.mark(pool.tensor_tensor(h_biased[:, (b + 2) % RING], h[:, :, :], two(rows[:, 1, :]), ALU.add))
                        if "Z" in stages:
                            root(1, n - 1)

                    rounds(pool, body)

                @block.scalar
                def _(act):
                    act.wait_ge(loaded, LOADS * 16)
                    act.wait_ge(ready, 1)

                    def body(i, b, stages):
                        n = i * RING + b
                        if "O" in stages:
                            probT_ps_done.wait(act, n + 1)
                            o_ps_done.wait(act, n)
                            probT_done.mark(act.copy(probT[:, :, :, :].rearrange("p (b h) t k -> p b (h t k)", h=2), probT_ps[:, :, :]))
                        if "Z" in stages:
                            oT_ps_done.wait(act, n)
                            mha_ps_done.wait(act, n - 1)
                            oT_done.mark(act.copy(oT[:, :, :], oT_ps))
                        if "A" in stages:
                            hT_ps_done.wait(act, n + 3)
                            v_ps_done.wait(act, n + 2)
                            hT_done.mark(act.copy(hT[:, :, :], hT_ps))
                        if "S" in stages:
                            shifted_done.wait(act, n + 2)
                            probT_ps_done.wait(act, n + 1)
                            prob_done.mark(act.activation(prob[:, :, :, :], score[:, :, :, :], ACT.Exp, scale=SCALE))
                        if "A" in stages:
                            qk_ps_done.wait(act, n + 3)
                            s_ps_done.wait(act, n + 2)
                            for hd in range(NH):
                                of = slice(DH * hd, DH * hd + DH)
                                act.activation(qT[of, hd].rearrange("p t k -> p (t k)"), qk_ps[of, 0, :], ACT.Identity,
                                               bias=in_b_sb[of, 0:1])
                            last = act.activation(kT[:, :, :].rearrange("p t k -> p (t k)"), qk_ps[:, 1, :], ACT.Identity,
                                                  bias=in_b_sb[:, 1:2])
                            qk_done.mark(last)
                        if "T" in stages:
                            y1T_ps_done.wait(act, n - 1)
                            logit_ps_done.wait(act, n - 2)
                            y1T_stored.wait(act, (n - 2) * 16)
                            y1T_done.mark(act.copy(y1T[:, :, :], y1T_ps))

                    rounds(act, body)

                @block.tensor
                def _(pe):
                    pe.wait_ge(loaded, LOADS * 16)
                    pe.wait_ge(rounded, 1)

                    def turn(dst, src, done):
                        for t in range(2):
                            last = pe.transpose(dst[:, t, :], src[:, t, :], ident_sb[:, :])
                        done.mark(last)

                    def body(i, b, stages):
                        n = i * RING + b
                        if "O" in stages:
                            prob_done.wait(pe, n + 1)
                            probT_done.wait(pe, n)
                            for t in range(2):
                                for hd in range(NH):
                                    last = pe.transpose(probT_of[:, hd, t, :], prob[:, hd, t, :], ident_sb[:, :])
                            probT_ps_done.mark(last)
                        if "Z" in stages:
                            o_done.wait(pe, n)
                            hT_done.wait(pe, pairs_done(n + 2))
                            y1T_done.wait(pe, n - 2)
                            turn(oT_ps, o, oT_ps_done)
                        if "S" in stages:
                            qk_done.wait(pe, n + 2)
                            shifted_done.wait(pe, n + 1)
                            for k in range(2):
                                pe.matmul(s_ps[:, k, :].rearrange("p (a k) -> p a k", k=P), ident_r[:, :],
                                          other_r[:, :].unsqueeze(1).to_broadcast([P, 4, P]), start=True, stop=False)
                                for hd in (2 * k, 2 * k + 1):
                                    for t in range(2):
                                        last = pe.matmul(s_of[:, hd, t, :], qT[:, hd, t, :], kT[:, t, :],
                                                         start=False, stop=hd % 2 == t == 1)
                            s_ps_done.mark(last)
                        if "R" in stages:
                            y1T_done.wait(pe, n - 2)
                            logit_done.wait(pe, n - 3)
                            o_done.wait(pe, pairs_done(n))
                            for t in range(2):
                                last = pe.matmul(logit_ps[:, t, :], y1T[:, t, :], wg_sb[:, :], start=True, stop=True)
                            logit_ps_done.mark(last)
                        if "A" in stages:
                            h_done.wait(pe, n + 3)
                            hT_done.wait(pe, n + 2)
                            oT_done.wait(pe, n)
                            y1T_done.wait(pe, n - 2)
                            turn(hT_ps, h, hT_ps_done)
                        if "O" in stages:
                            probT_done.wait(pe, n + 1)
                            v_done.wait(pe, n + 1)
                            o_done.wait(pe, n)
                            logit_done.wait(pe, pairs_done(n - 2))
                            for t in range(2):
                                for hd in range(NH):
                                    last = pe.matmul(o_ps[:, t, hd, :], probT[:, hd, t, :], v1[:, b, t, hd, :], start=True, stop=True)
                            o_ps_done.mark(last)
                        if "A" in stages:
                            hT_done.wait(pe, n + 3)
                            qk_done.wait(pe, n + 2)
                            for k in range(2):
                                last = pe.matmul(qk_ps[:, k, :], in_w_sb[:, k * D:(k + 1) * D],
                                                 hT[:, :, :].rearrange("p t k -> p (t k)"), start=True, stop=True)
                            qk_ps_done.mark(last)
                        if "Z" in stages:
                            oT_done.wait(pe, n)
                            z_done.wait(pe, n - 1)
                            v_done.wait(pe, pairs_done(n + 2))
                            for t in range(2):
                                last = pe.matmul(mha_ps[:, t, :], oT[:, t, :], out_w_sb[:, :], start=True, stop=True)
                            mha_ps_done.mark(last)
                        if "T" in stages:
                            y1_done.wait(pe, n - 1)
                            oT_done.wait(pe, pairs_done(n))
                            hT_done.wait(pe, pairs_done(n + 3))
                            y1T_done.wait(pe, n - 2)
                            turn(y1T_ps, y1, y1T_ps_done)
                        if "A" in stages:
                            v_done.wait(pe, n + 2)
                            z_done.wait(pe, n)
                            for t in range(2):
                                last = pe.matmul(v_ps[:, t, :], hT[:, t, :], in_w_sb[:, 2 * D:3 * D], start=True, stop=True)
                            v_ps_done.mark(last)

                    rounds(pe, body)

                @block.vector
                def _(dve):
                    dve.wait_ge(loaded, LOADS * 16)
                    dve.wait_ge(ready, 1)
                    dve.tensor_copy(ident_r[:, :], ident_sb[:, :])
                    dve.tensor_copy(other_r[:, :], other_sb[:, :]).then_inc(rounded, 1)
                    steps = Steps(dve, dve_steps)

                    class Norm:

                        def __init__(self, k, n, src, gain):
                            self.k, self.n, self.src, self.gain = k, n, src, gain

                        def mean(self):
                            for t in range(2):
                                last = dve.bn_stats(stats[:, self.k, t, :], self.src[:, t, :])
                            steps.wait(steps.mark(last))
                            settle(dve, settled)
                            for t in range(2):
                                last = dve.bn_aggr(mv[:, self.k, t, :], stats[:, self.k, t, :])
                            mv_done[self.k].mark(last)

                        def scale(self):
                            mv_done[self.k].wait(dve, self.n + 1)
                            for t in range(2):
                                last = dve.scalar_tensor_tensor(scaled[:, self.k, t, :], self.src[:, t, :],
                                                                mv[:, self.k, t, 0:1], self.gain, ALU.subtract, ALU.mult)
                            self.scaled_at = steps.mark(last)

                        def finish(self, dst, shift):
                            rstd_done[self.k].wait(dve, self.n + 1)
                            steps.wait(self.scaled_at)
                            for t in range(2):
                                last = dve.scalar_tensor_tensor(dst[:, t, :], scaled[:, self.k, t, :], rstd[:, self.k, t:t + 1],
                                                                shift, ALU.mult, ALU.add)
                            return last

                    sizes = dict(A=(2, 2), S=(1, 1), O=(1, 0), Z=(2, -1))

                    def body(i, b, stages):
                        n = i * RING + b
                        if isinstance(n, int):
                            steps.start(sum(size * pairs_done(n + ahead) for size, ahead in sizes.values()))
                        else:
                            steps.start(n * sum(size for size, _ in sizes.values())
                                        + sum(size * ahead for size, ahead in sizes.values()))
                        if "A" in stages:
                            slot = (b + 2) % RING
                            x_in[slot].wait(dve, 32 * (i + (b + 2) // RING) + 32)
                            norm0 = Norm(0, n + 2, xin[:, slot], consts[:, 1, :])
                            norm0.mean()
                            norm0.scale()
                            hT_ps_done.wait(dve, n + 2)
                            h_biased_done.wait(dve, n + 2)
                            h_done.mark(norm0.finish(h, consts[:, 0, :]))
                        if "R" in stages:
                            logit_ps_done.wait(dve, n - 2)
                            logit_done.mark(dve.tensor_copy(logits[:, bass.ds((n - 3) * 2, 2), :], logit_ps))
                        if "S" in stages:
                            s_ps_done.wait(dve, n + 2)
                            top_at = steps.mark(dve.tensor_reduce(top[:, :, :], s_of, AX.X, ALU.max))
                        if "S" in stages:
                            steps.wait(top_at)
                            prob_done.wait(dve, n + 1)
                            shifted_done.mark(dve.tensor_tensor(
                                score[:, :, :, :], s_of, top[:, :, :].unsqueeze(3).to_broadcast([P, NH, 2, P]), ALU.subtract))
                        if "O" in stages:
                            o_ps_done.wait(dve, n + 1)
                            rden_at = steps.mark(dve.reciprocal(rden[:, :, :], o_ps[:, :, :, DH]))
                        if "Z" in stages:
                            mha_ps_done.wait(dve, n)
                            h_biased_done.wait(dve, n)
                            z_done.mark(dve.tensor_tensor(z[:, :, :], mha_ps, h_biased[:, (b - 1) % RING], ALU.add))
                        if "O" in stages:
                            steps.wait(rden_at)
                            oT_ps_done.wait(dve, n)
                            o_done.mark(dve.tensor_tensor(o[:, :, :].rearrange("p t (h d) -> p t h d", h=NH), o_ps[:, :, :, 0:DH],
                                                          rden[:, :, :].unsqueeze(3).to_broadcast([P, 2, NH, DH]), ALU.mult))
                        if "Z" in stages:
                            z_done.wait(dve, n)
                            norm1 = Norm(1, n - 1, z, rows[:, 2, :])
                            norm1.mean()
                            norm1.scale()
                        if "A" in stages:
                            v_ps_done.wait(dve, n + 3)
                            o_ps_done.wait(dve, n - 1)
                            v_done.mark(dve.tensor_tensor(
                                v1[:, slot, :, :, 0:DH], v_ps.rearrange("p t (h d) -> p t h d", h=NH),
                                two(rows[:, 0, :]).rearrange("p t (h d) -> p t h d", h=NH), ALU.add))
                        if "Z" in stages:
                            y1T_ps_done.wait(dve, n - 1)
                            y1_stored.wait(dve, 16 * (n - 1))
                            y1_done.mark(norm1.finish(y1, rows[:, 3, :]))

                    rounds(dve, body)

        with ExitStack() as part:
            def sb2(name, shape, dt=F32):
                return part.enter_context(nc.sbuf_tensor(name, shape, dt))

            def ps2(name, shape):
                return part.enter_context(nc.psum_tensor(name, shape, F32))

            w1_sb, w2_sb = sb2("fb_w1", [P, E, FC, D]), sb2("fb_w2", [P, E, FC, D])
            b1_sb, b2_rows, b12 = sb2("fb_b1", [P, E, FC]), sb2("fb_b2", [P, D]), sb2("fb_b12", [P, D])
            b1_of = sb2("fb_b1_of", [P, E, FC, BLOCK, E])
            mask_sb, falling_sb = sb2("fb_mask", [P, BLOCK]), sb2("fb_falling", [P, E])
            b12_of = sb2("fb_b12_of", [P, BLOCK, D])
            top, ex, total = sb2("fb_top", [P, TILES]), sb2("fb_exp", [P, TILES, E]), sb2("fb_sum", [P, TILES])
            rtotal, gates, gate = sb2("fb_rsum", [P, TILES]), sb2("fb_gates", [P, TILES, E]), sb2("fb_gate", [P, TILES])
            rank, first = sb2("fb_rank", [P, TILES, E]), sb2("fb_first", [P, TILES])
            chosen, of_batch = sb2("fb_chosen", [P, TILES, E]), sb2("fb_of_batch", [P, E])
            tile_counts, running = sb2("fb_tile_counts", [P, TILES, E]), sb2("fb_running", [P, TILES, E])
            zero, place, kept = sb2("fb_zero", [P, TILES]), sb2("fb_place", [P, TILES, E]), sb2("fb_kept", [P, TILES, E])
            coefT = sb2("fb_coefT", [P, TILES // BLOCK, P])
            w_ps, within_ps, tile_ps, before_ps = ps2("fb_w_ps", [P, 2, 512]), ps2("fb_within_ps", [P, 512]), ps2("fb_tile_ps", [P, 512]), ps2("fb_before_ps", [P, 512])
            b_ps, bias_ps = ps2("fb_b_ps", [P, 512]), ps2("fb_bias_ps", [P, 2, 512])
            loaded, ready, dve_steps = s.sem("fb_loaded"), s.sem("fb_ready"), s.sem("fb_dve_steps")
            shifted_done, exp_done, chosen_done, of_batch_done = s.sem("fb_shifted_done"), s.sem("fb_exp_done"), s.sem("fb_chosen_done"), s.sem("fb_of_batch_done")
            counts_done, b1_of_done, w12_ps_done, b12_ps_done = s.sem("fb_counts_done"), s.sem("fb_b1_of_done"), s.sem("fb_w12_ps_done"), s.sem("fb_b12_ps_done")
            b12_of_done, coef_done, coefT_ps_done, coefT_done = s.sem("fb_b12_of_done"), s.sem("fb_coef_done"), s.sem("fb_coefT_ps_done"), s.sem("fb_coefT_done")
            bias_ps_done, bias_done = s.sem("fb_bias_ps_done"), s.sem("fb_bias_done")
            with nc.Block() as block:

                @block.sync
                def _(sp):
                    sp.dma_start(w1_sb[:, :, :, :], w1.rearrange("e (c p) d -> p e c d", p=P)).then_inc(loaded, 16)
                    sp.dma_start(w2_sb[:, :, :, :], w2.rearrange("e (c p) d -> p e c d", p=P)).then_inc(loaded, 16)
                    sp.dma_start(b1_sb[:, :, :].rearrange("p e c -> p (e c)"), b1).then_inc(loaded, 16)
                    sp.dma_start(b2_rows[:, :], b2.unsqueeze(0).to_broadcast([BLOCK, E, D])).then_inc(loaded, 16)
                    sp.dma_start(mask_sb[:, :], tile_mask).then_inc(loaded, 16)
                    sp.dma_start(falling_sb[:, :], falling).then_inc(loaded, 16)

                @block.gpsimd
                def _(pool):
                    pool.memset(zero[:, :], 0.0)
                    pool.memset(b1_of[:, :, :, :, :], 0.0).then_inc(ready, 1)
                    pool.wait_ge(ready, 1)
                    pool.wait_ge(loaded, 6 * 16)
                    for e in range(E):
                        last = pool.tensor_copy(b1_of[:, e, :, :, e], b1_sb[:, e, :].unsqueeze(2).to_broadcast([P, FC, BLOCK]))
                    last.then_inc(b1_of_done, 1)

                @block.scalar
                def _(act):
                    act.wait_ge(shifted_done, 1)
                    act.activation(ex[:, :, :], ex[:, :, :], ACT.Exp).then_inc(exp_done, 1)
                    act.wait_ge(w12_ps_done, 1)
                    act.copy(w12[:, :, :].rearrange("p (a e) d -> p a (e d)", a=2), w_ps[:, :, :])
                    act.wait_ge(coefT_ps_done, 1)
                    act.copy(coefT[:, :, :].rearrange("p a b -> p (a b)"), within_ps[:, :]).then_inc(coefT_done, 1)
                    for k in range(TILES // 4):
                        act.wait_ge(bias_ps_done, k + 1)
                        act.copy(bias[:, 4 * k:4 * k + 4, :].rearrange("p t d -> p (t d)"),
                                 bias_ps[:, k % 2, :]).then_inc(bias_done, 1)

                @block.tensor
                def _(pe):
                    pe.wait_ge(loaded, 6 * 16)
                    for e in range(E):
                        for c in range(FC):
                            last = pe.matmul(w_ps[:, e // 4, (e % 4) * D:(e % 4) * D + D], w1_sb[:, e, c, :], w2_sb[:, e, c, :],
                                             start=c == 0, stop=c == FC - 1)
                    last.then_inc(w12_ps_done, 1)
                    pe.wait_ge(b1_of_done, 1)
                    for e in range(E):
                        for c in range(FC):
                            last = pe.matmul(b_ps[:, 0:D], b1_of[:, e, c].rearrange("p a b -> p (a b)"), w2_sb[:, e, c, :],
                                             start=e == c == 0, stop=(e, c) == (E - 1, FC - 1))
                    last.then_inc(b12_ps_done, 1)
                    pe.wait_ge(chosen_done, 1)
                    flat = chosen[:, :, :].rearrange("p t e -> p (t e)")
                    pe.matmul(within_ps[:, :], upto_sb[:, :], flat, start=True, stop=True)
                    pe.matmul(tile_ps[:, :], same_sb[:, :], flat, start=True, stop=True)
                    pe.wait_ge(of_batch_done, 1)
                    pe.matmul(before_ps[:, 0:E], before_sb[:, :], of_batch[:, :], start=True, stop=True).then_inc(counts_done, 1)
                    pe.wait_ge(coef_done, 1)
                    for k in range(TILES // BLOCK):
                        last = pe.transpose(within_ps[:, k * P:k * P + P],
                                            coef[:, k * BLOCK:(k + 1) * BLOCK, :].rearrange("p t e -> p (t e)"), ident_sb[:, :])
                    last.then_inc(coefT_ps_done, 1)
                    pe.wait_ge(coefT_done, 1)
                    pe.wait_ge(b12_of_done, 1)
                    for j in range(TILES):
                        k = j // 4
                        if j % 4 == 0 and k >= 2:
                            pe.wait_ge(bias_done, k - 1)
                        last = pe.matmul(bias_ps[:, k % 2, (j % 4) * D:(j % 4) * D + D], coefT[:, j // BLOCK, :],
                                         b12_of[:, j % BLOCK, :], start=True, stop=True)
                        if j % 4 == 3:
                            last.then_inc(bias_ps_done, 1)

                @block.vector
                def _(dve):
                    link = Chain(dve, dve_steps, 0)
                    step = link.then

                    def each(a):
                        return a.unsqueeze(2).to_broadcast([P, TILES, E])

                    step(dve.tensor_reduce(top[:, :], logits[:, :, :], AX.X, ALU.max))
                    dve.tensor_tensor(ex[:, :, :], logits[:, :, :], each(top[:, :]), ALU.subtract).then_inc(shifted_done, 1)
                    dve.wait_ge(exp_done, 1)
                    step(dve.tensor_reduce(total[:, :], ex[:, :, :], AX.X, ALU.add))
                    step(dve.reciprocal(rtotal[:, :], total[:, :]))
                    step(dve.tensor_tensor(gates[:, :, :], ex[:, :, :], each(rtotal[:, :]), ALU.mult))
                    step(dve.tensor_reduce(gate[:, :], gates[:, :, :], AX.X, ALU.max))
                    step(dve.tensor_tensor(rank[:, :, :], gates[:, :, :], each(gate[:, :]), ALU.is_equal))
                    dve.wait_ge(loaded, 6 * 16)
                    step(dve.tensor_tensor(rank[:, :, :], rank[:, :, :],
                                           falling_sb[:, :].unsqueeze(1).to_broadcast([P, TILES, E]), ALU.mult))
                    step(dve.tensor_reduce(first[:, :], rank[:, :, :], AX.X, ALU.max))
                    ins = dve.tensor_tensor(chosen[:, :, :], rank[:, :, :], each(first[:, :]), ALU.is_equal)
                    ins.then_inc(chosen_done, 1)
                    dve.wait_ge(chosen_done, 1)
                    dve.tensor_reduce(of_batch[:, :], chosen[:, :, :].rearrange("p t e -> p e t"), AX.X, ALU.add).then_inc(of_batch_done, 1)
                    dve.wait_ge(b12_ps_done, 1)
                    step(dve.tensor_tensor(b12[:, :], b_ps[:, 0:D], b2_rows[:, :], ALU.add))
                    dve.tensor_tensor(b12_of[:, :, :], b12[:, :].unsqueeze(1).to_broadcast([P, BLOCK, D]),
                                      mask_sb[:, :].unsqueeze(2).to_broadcast([P, BLOCK, D]), ALU.mult).then_inc(b12_of_done, 1)
                    dve.wait_ge(counts_done, 1)
                    dve.wait_ge(ready, 1)
                    step(dve.tensor_copy(tile_counts[:, :, :].rearrange("p t e -> p (t e)"), tile_ps[:, :]))
                    for e in range(E):
                        last = dve.tensor_tensor_scan(running[:, :, e], tile_counts[:, :, e], zero[:, :], 0.0, ALU.add, ALU.add)
                    step(last)
                    step(dve.tensor_tensor(running[:, :, :], running[:, :, :], tile_counts[:, :, :], ALU.subtract))
                    step(dve.tensor_tensor(place[:, :, :].rearrange("p t e -> p (t e)"), within_ps[:, :],
                                           running[:, :, :].rearrange("p t e -> p (t e)"), ALU.add))
                    step(dve.tensor_copy(of_batch[:, :], before_ps[:, 0:E]))
                    step(dve.tensor_tensor(place[:, :, :], place[:, :, :], of_batch[:, :].unsqueeze(1).to_broadcast([P, TILES, E]), ALU.add))
                    step(dve.scalar_tensor_tensor(kept[:, :, :].rearrange("p t e -> p (t e)"),
                                                  place[:, :, :].rearrange("p t e -> p (t e)"), float(CAP),
                                                  chosen[:, :, :].rearrange("p t e -> p (t e)"), ALU.is_le, ALU.mult))
                    dve.tensor_tensor(coef[:, :, :], kept[:, :, :], each(gate[:, :]), ALU.mult).then_inc(coef_done, 1)

        with ExitStack() as part:
            def sb3(name, shape, dt=F32):
                return part.enter_context(nc.sbuf_tensor(name, shape, dt))

            RING3 = 4
            HALF_E = E // 2
            xin, y1, y1T = sb3("fc_x", [P, RING3, 2, D]), sb3("fc_y1", [P, RING3, 2, D]), sb3("fc_y1T", [P, RING3, 2, P])
            base, acc, y = sb3("fc_base", [P, 2, 2, D]), sb3("fc_acc", [P, 2, D]), sb3("fc_y", [P, 2, 2, D])
            part_e, part_2, part_1 = sb3("fc_part_e", [P, 2, 2, HALF_E, D]), sb3("fc_part_2", [P, 2, 2, D]), sb3("fc_part_1", [P, 2, 2, D])
            biased, scaled, total_y = sb3("fc_biased", [P, 2, 2, D]), sb3("fc_scaled", [P, 2, D]), sb3("fc_total", [P, 2, D])
            stats, mv = sb3("fc_stats", [P, 2, 6]), sb3("fc_mean_var", [P, 2, 2])
            std, rstd = sb3("fc_std", [P, 2]), sb3("fc_rstd", [P, 2])
            e_ps = part.enter_context(nc.psum_tensor("fc_e_ps", [P, 4, 2, 512], F32))

            def sig(name):
                return Signal(s, "fc_" + name)

            ins_done, y_stored = [sig(f"in{k}") for k in range(RING3)], [sig(f"y_stored{k}") for k in range(2)]
            e_done, added, scaled_done = sig("e_done"), sig("added"), sig("scaled_done")
            base_done, part_done, biased_done, total_done = sig("base_done"), sig("part_done"), sig("biased_done"), sig("total_done")
            mv_done, std_done, y_done = sig("mv_done"), sig("std_done"), sig("y_done")
            dve_steps, pool_steps, settled = s.sem("fc_dve_steps"), s.sem("fc_pool_steps"), s.sem("fc_settled")

            def rounds(eng, body):
                def with_stages(i, b):
                    body(i, b, [x for x, ahead in zip("EN", (0, -1)) if in_range(i, b + ahead, RING3)])

                all_rounds(eng, RING3, with_stages, 1)

            with nc.Block() as block:

                @block.sync
                def _(sp):
                    def load(n, slot):
                        ins_done[slot].mark(sp.dma_start(y1T[:, slot], y1T_dram[n]), 16)
                        ins_done[slot].mark(sp.dma_start(y1[:, slot], y1_dram[n]), 16)
                        for t in range(2):
                            ins_done[slot].mark(sp.dma_start(xin[:, slot, t, :], x_t[n * 2 + t]), 16)

                    def body(i, b, stages):
                        n = i * RING3 + b
                        if in_range(i, b + 2, RING3):
                            added.wait(sp, n - 1)
                            base_done.wait(sp, n - 1)
                            biased_done.wait(sp, n - 1)
                            load(n + 2, (b + 2) % RING3)
                        if "N" in stages:
                            y_done.wait(sp, n)
                            for t in range(2):
                                y_stored[(b - 1) % 2].mark(sp.dma_start(out_t[(n - 1) * 2 + t], y[:, (b - 1) % 2, t, :]), 16)

                    load(0, 0)
                    rounds(sp, body)
                    for k in range(2):
                        y_stored[k].wait(sp, PAIRS // 2 * 32)

                @block.gpsimd
                def _(pool):
                    steps = Steps(pool, pool_steps)

                    def body(i, b, stages):
                        n = i * RING3 + b
                        steps.start(pairs_done(n))
                        if "E" in stages:
                            k = b % 2
                            ins_done[b].wait(pool, 64 * i + 64)
                            added.wait(pool, n - 1)
                            base_done.mark(pool.tensor_tensor(base[:, k], y1[:, b], bias[:, bass.ds(n * 2, 2), :], ALU.add))
                            y_done.wait(pool, n - 1)
                            biased_done.mark(pool.tensor_tensor(biased[:, k], xin[:, b], two(consts[:, 3, :]), ALU.add))
                            scaled_done.wait(pool, n + 1)
                            part_done.wait(pool, n)
                            part_at = steps.mark(pool.tensor_tensor(part_2[:, :, :, :], part_e[:, k, :, 0:2], part_e[:, k, :, 2:4], ALU.add))
                            steps.wait(part_at)
                            total_done.wait(pool, n - 1)
                            part_done.mark(pool.tensor_tensor(part_1[:, k], part_2[:, :, 0], part_2[:, :, 1], ALU.add))

                    rounds(pool, body)

                @block.scalar
                def _(act):
                    def body(i, b, stages):
                        n = i * RING3 + b
                        if "E" in stages:
                            k = b % 2
                            part_done.wait(act, n - 1)
                            for t in range(2):
                                e_done.wait(act, 2 * n + t + 1)
                                for e in range(HALF_E, E):
                                    last = act.activation(part_e[:, k, t, e - HALF_E, :], e_ps[:, 2 * k + t, 1, (e - HALF_E) * D:(e - HALF_E) * D + D],
                                                          ACT.Copy, scale=coef[:, bass.ds(n * 2 + t, 1), e])
                            scaled_done.mark(last)
                        if "N" in stages:
                            mv_done.wait(act, n)
                            std_done.mark(act.activation(std[:, :], mv[:, :, 1], ACT.Sqrt, bias=eps[:, 0:1]))

                    rounds(act, body)

                @block.tensor
                def _(pe):
                    def body(i, b, stages):
                        n = i * RING3 + b
                        if "E" in stages:
                            ins_done[b].wait(pe, 64 * i + 64)
                            scaled_done.wait(pe, n - 1)
                            added.wait(pe, n - 1)
                            for t in range(2):
                                for k in range(2):
                                    last = pe.matmul(e_ps[:, 2 * (b % 2) + t, k, :], y1T[:, b, t, :],
                                                     w12[:, HALF_E * k:HALF_E * k + HALF_E, :].rearrange("p e d -> p (e d)"),
                                                     start=True, stop=True)
                                e_done.mark(last)

                    rounds(pe, body)

                @block.vector
                def _(dve):
                    steps = Steps(dve, dve_steps)
                    SUM, NORM = HALF_E - 1, 3

                    def body(i, b, stages):
                        n = i * RING3 + b
                        steps.start(pairs_done(n) * SUM + pairs_done(n - 1) * NORM)
                        k, before = b % 2, (b - 1) % 2
                        if "N" in stages:
                            added.wait(dve, n)
                            part_done.wait(dve, n)
                            total_done.mark(dve.tensor_tensor(total_y[:, :, :], acc[:, :, :], part_1[:, before], ALU.add))
                        for e in range(HALF_E):
                            if "E" in stages:
                                if e == 0:
                                    base_done.wait(dve, n + 1)
                                    total_done.wait(dve, n)
                                else:
                                    steps.wait(added_at)
                                for t in range(2):
                                    if e == 0:
                                        e_done.wait(dve, 2 * n + t + 1)
                                    last = dve.scalar_tensor_tensor(
                                        acc[:, t, :], e_ps[:, 2 * k + t, 0, e * D:e * D + D],
                                        coef[:, bass.ds(n * 2 + t, 1), e], acc[:, t, :] if e else base[:, k, t, :],
                                        ALU.mult, ALU.add)
                                if e < HALF_E - 1:
                                    added_at = steps.mark(last)
                                else:
                                    added.mark(last)
                            if "N" in stages:
                                if e == 0:
                                    total_done.wait(dve, n)
                                    for t in range(2):
                                        last = dve.bn_stats(stats[:, t, :], total_y[:, t, :])
                                    stats_at = steps.mark(last)
                                elif e == 1:
                                    steps.wait(stats_at)
                                    settle(dve, settled)
                                    for t in range(2):
                                        last = dve.bn_aggr(mv[:, t, :], stats[:, t, :])
                                    mv_done.mark(last)
                                elif e == 2:
                                    mv_done.wait(dve, n)
                                    for t in range(2):
                                        last = dve.scalar_tensor_tensor(scaled[:, t, :], total_y[:, t, :], mv[:, t, 0:1],
                                                                        consts[:, 2, :], ALU.subtract, ALU.mult)
                                    scaled_at = steps.mark(last)
                                else:
                                    std_done.wait(dve, n)
                                    rstd_at = steps.mark(dve.reciprocal(rstd[:, :], std[:, :]))
                                    steps.wait(scaled_at)
                                    steps.wait(rstd_at)
                                    biased_done.wait(dve, n)
                                    y_stored[before].wait(dve, 32 * (i * 2 + (b - 1) // 2))
                                    for t in range(2):
                                        last = dve.scalar_tensor_tensor(y[:, before, t, :], scaled[:, t, :], rstd[:, t:t + 1],
                                                                        biased[:, before, t, :], ALU.mult, ALU.add)
                                    y_done.mark(last)

                    rounds(dve, body)


def adaln_two_layers(nc, x, L0_wqkv, L0_wo, L0_ln_g, L0_ln_b, L0_c, L0_wmod, L1_wq, L1_wk, L1_wv, L1_wo, L1_bo,
                     in_w, in_b, out_w, out_b, ln1_g, ln1_b, ln2_g, ln2_b, wg, w1, b1, w2, b2, L1_c, L1_wmod,
                     ident, upto, same_batch, last_of_batch, batch_before, fold, other_position, cos, sin,
                     tile_mask, falling, out):
    def scratch(name, shape):
        return nc.dram_tensor(name, shape, F32, kind="Internal").ap()

    mods = scratch("mods", (M_COUNT, P, D))
    x1, x2 = scratch("x1", (B, L, D)), scratch("x2", (B, L, D))
    y1, y1T = scratch("y1", (PAIRS, P, 2, D)), scratch("y1T", (PAIRS, D, 2, P))
    modulation(nc, L0_c, L0_wmod, L0_ln_g, L0_ln_b, L1_c, L1_wmod, L1_bo, ln2_g, ln2_b, mods)
    layer0(nc, x, L0_wqkv, L0_wo, mods, ident, upto, last_of_batch, cos, sin, x1)
    layer1_attention(nc, x1, L1_wq, L1_wk, L1_wv, L1_wo, mods, ident, fold, x2)
    layer1_ffn(nc, x2, in_w, in_b, out_w, out_b, ln1_g, ln1_b, wg, w1, b1, w2, b2, mods, ident, upto, same_batch,
               batch_before, other_position, tile_mask, falling, y1, y1T, out)




def kernel(**inputs):
    import numpy as _np
    import concourse.bacc as _bacc
    from concourse import mybir as _mybir
    from concourse.bass_utils import run_bass_kernel_spmd as _run

    a = {name: _np.asarray(value) for name, value in inputs.items()}
    experts, hidden = a["L1_ffn_b1"].shape
    cos, sin = rope_tables()
    arrays = {
        "x": a["L0_attn_x"],
        "L0_wqkv": _np.concatenate([a["L0_attn_wq"], a["L0_attn_wk"], a["L0_attn_wv"]], axis=1),
        "L0_wo": a["L0_attn_wo"],
        "L0_ln_g": a["L0_ffn_ln_g"],
        "L0_ln_b": a["L0_ffn_ln_b"],
        "L0_c": a["L0_c"].T,
        "L0_wmod": a["L0_wmod"],
        "L1_wq": a["L1_attn_Wq"],
        "L1_wk": a["L1_attn_Wk"],
        "L1_wv": a["L1_attn_Wv"],
        "L1_wo": a["L1_attn_Wo"],
        "L1_bo": a["L1_attn_bo"],
        "in_w": a["L1_ffn_in_proj_w"].T,
        "in_b": a["L1_ffn_in_proj_b"],
        "out_w": a["L1_ffn_out_proj_w"].T,
        "out_b": a["L1_ffn_out_proj_b"],
        "ln1_g": a["L1_ffn_ln1_g"],
        "ln1_b": a["L1_ffn_ln1_b"],
        "ln2_g": a["L1_ffn_ln2_g"],
        "ln2_b": a["L1_ffn_ln2_b"],
        "wg": a["L1_ffn_wg"],
        "w1": a["L1_ffn_w1"].transpose(0, 2, 1),
        "b1": a["L1_ffn_b1"].reshape(experts, hidden // P, P).transpose(2, 0, 1).reshape(P, -1),
        "w2": a["L1_ffn_w2"],
        "b2": a["L1_ffn_b2"],
        "L1_c": a["L1_c"].T,
        "L1_wmod": a["L1_wmod"],
        "ident": IDENT,
        "upto": UPTO,
        "same_batch": SAME_BATCH,
        "last_of_batch": LAST_OF_BATCH,
        "batch_before": BATCH_BEFORE,
        "fold": FOLD,
        "other_position": OTHER_POSITION,
        "cos": cos,
        "sin": sin,
        "tile_mask": (_np.arange(P)[:, None] // experts == _np.arange(P // experts)[None, :]).astype(_np.float32),
        "falling": _np.tile(_np.arange(experts, 0, -1).astype(_np.float32), (P, 1)),
    }
    arrays = {name: _np.ascontiguousarray(value) for name, value in arrays.items()}
    nc = _bacc.Bacc("TRN2", target_bir_lowering=False, num_devices=1)
    args = {name: nc.dram_tensor(name, value.shape, _mybir.dt.from_np(value.dtype), kind="ExternalInput").ap()
            for name, value in arrays.items()}
    out = nc.dram_tensor("out", (B, L, D), F32, kind="ExternalOutput").ap()
    adaln_two_layers(nc, out=out, **args)
    r = _run(nc, [arrays], core_ids=[0])
    return r.results[0]["out"]
```

```python
from contextlib import ExitStack

import numpy as np

import concourse.bass as bass
from concourse import mybir

F32 = mybir.dt.float32
F32R = mybir.dt.float32r
ALU = mybir.AluOpType
ACT = mybir.ActivationFunctionType
AX = mybir.AxisListType

P = 128
B, L, D = 8, 1024, 128
SEG = P // B
TILES = B * L // P
PAIRS = TILES // 2
EPS_LN = 1e-5
EPS_ATT = 1e-6

H0, D0 = 16, 8
V0 = D0 + 1
HEADS_OF_BANK = (6, 5, 5)

(M0_SHIFT, M0_SCALE, M0_GATE, M0_SHIFT2, M0_SCALE2, M0_GAIN2, M0_BIAS2, M1_SHIFT, M1_SCALE, M1_GATE,
 M1_BIAS, M1_SHIFT2, M1_SCALE2, M1_GAIN2, M1_BIAS2, M_COUNT) = range(16)

_row = np.arange(P)
_batch, _pos = _row // SEG, _row % SEG
_same = _batch[:, None] == _batch[None, :]
IDENT = np.eye(P, dtype=np.float32)
UPTO = (_same & (_pos[:, None] <= _pos[None, :])).astype(np.float32)
SAME_BATCH = _same.astype(np.float32)
LAST_OF_BATCH = (_same & (_pos[:, None] == SEG - 1)).astype(np.float32)
BATCH_BEFORE = (_batch[:, None] < _batch[None, :]).astype(np.float32)
FOLD = (_row[:, None] % 64 == _row[None, :] % 64).astype(np.float32)
OTHER_POSITION = np.where(_pos[:, None] == _pos[None, :], 0.0, -1e30).astype(np.float32)


def rope_tables():
    inv = (1.0 / np.float32(10000.0) ** (np.arange(0, D0, 2, dtype=np.float32) / np.float32(D0))).astype(np.float32)
    at = (np.arange(TILES)[None, :] * SEG + _pos[:, None]).astype(np.float32)
    angle = (at[:, :, None] * inv[None, None, :]).astype(np.float32)
    cos, sin = np.cos(angle).astype(np.float32), np.sin(angle).astype(np.float32)
    return np.repeat(cos, 2, axis=2), np.stack([-sin, sin], axis=3).reshape(P, TILES, D0)


def tiles_of(x):
    return x.rearrange("l (j n) d -> j l n d", n=SEG)


class Scope:

    def __init__(self, nc):
        self.nc, self.stack = nc, ExitStack()

    def sb(self, name, shape, dt=F32):
        return self.stack.enter_context(self.nc.sbuf_tensor(name, shape, dt))

    def psum(self, name, shape, dt=F32):
        return self.stack.enter_context(self.nc.psum_tensor(name, shape, dt))

    def sem(self, name):
        return self.stack.enter_context(self.nc.semaphore(name))


class Signal:

    def __init__(self, scope, name, ahead=0):
        self.sem, self.ahead = scope.sem(name), ahead

    def give_ahead(self, engine):
        engine.sem_inc(self.sem, self.ahead)

    def mark(self, instruction, by=1):
        instruction.then_inc(self.sem, by)

    def wait(self, engine, count):
        if not isinstance(count, int) or count + self.ahead > 0:
            engine.wait_ge(self.sem, count + self.ahead)


def in_range(i, b, ring):
    return not isinstance(i, int) or 0 <= i * ring + b < PAIRS


def pairs_done(n):
    return min(max(n, 0), PAIRS) if isinstance(n, int) else n


def two(row):
    return row.unsqueeze(1).to_broadcast([P, 2, D])


def all_rounds(eng, ring, body, more=0):
    for n in range(-more, ring):
        body(n // ring, n % ring)
    with eng.Fori(1, PAIRS // ring - 1) as i:
        for b in range(ring):
            body(i, b)
    for n in range(PAIRS - ring, PAIRS + more):
        body(n // ring, n % ring)


class Steps:

    def __init__(self, engine, sem):
        self.engine, self.sem, self.base, self.n = engine, sem, 0, 0

    def start(self, base):
        self.base, self.n = base, 0

    def mark(self, instruction):
        self.n += 1
        instruction.then_inc(self.sem, 1)
        return self.base + self.n

    def wait(self, count):
        self.engine.wait_ge(self.sem, count)


class Chain:

    def __init__(self, engine, sem):
        self.engine, self.sem, self.base, self.n = engine, sem, 0, 0

    def start(self, base):
        self.base, self.n = base, 0

    def then(self, instruction):
        self.n += 1
        instruction.then_inc(self.sem, 1)
        self.engine.wait_ge(self.sem, self.base + self.n)


def settle(engine, settled):
    engine.sem_inc(settled, 1)


def modulation(nc, L0_c, L0_wmod, L0_ln_g, L0_ln_b, L1_c, L1_wmod, L1_bo, L1_ln2_g, L1_ln2_b, mods, next_inputs):
    s = Scope(nc)
    with s.stack:
        cT = s.sb("mod_cT", [P, 2, B])
        wmod = s.sb("mod_w", [P, 2, 6 * D])
        rows = s.sb("mod_rows", [P, 5, D])
        cneg = s.sb("mod_exp", [P, 2, B])
        den = s.sb("mod_den", [P, 2, B])
        rden = s.sb("mod_rden", [P, 2, B])
        silu = s.sb("mod_silu", [P, 2, B])
        silu_rows = s.sb("mod_silu_rows", [P, 2, P])
        size = s.sb("mod_size", [P, 2, 2, D])
        sign = s.sb("mod_sign", [P, 2, 2, D])
        gate = s.sb("mod_gate", [P, 2, 2, D])
        tile = s.sb("mod_tiles", [P, M_COUNT, D])
        mod_ps = s.psum("mod_ps", [P, 4, 512])
        loaded, exp_done, silu_done, mod_done = s.sem("mod_loaded"), s.sem("mod_exp_done"), s.sem("mod_silu_done"), s.sem("mod_done")
        steps, tiles_done, stored = s.sem("mod_steps"), s.sem("mod_tiles_done"), s.sem("mod_stored")
        with nc.Block() as block:

            @block.sync
            def _(sp):
                for layer, (c, w) in enumerate(((L0_c, L0_wmod), (L1_c, L1_wmod))):
                    sp.dma_start(cT[:, layer, :], c).then_inc(loaded, 16)
                    sp.dma_start(wmod[:, layer, :], w).then_inc(loaded, 16)
                for n, row in enumerate((L0_ln_g, L0_ln_b, L1_bo, L1_ln2_g, L1_ln2_b)):
                    sp.dma_start(rows[:, n, :], row.rearrange("(a d) -> a d", a=1).to_broadcast([P, D])).then_inc(loaded, 16)
                next_inputs.start(sp)
                sp.wait_ge(tiles_done, 1)
                sp.dma_start(mods.rearrange("m p d -> p m d"), tile[:, 0:M_COUNT, :]).then_inc(stored, 16)
                sp.wait_ge(stored, 16)

            @block.scalar
            def _(act):
                act.wait_ge(loaded, 9 * 16)
                act.activation(cneg[:, :, :], cT[:, :, :], ACT.Exp, scale=-1.0).then_inc(exp_done, 1)

            @block.tensor
            def _(pe):
                pe.wait_ge(silu_done, 1)
                for layer in range(2):
                    for half, width in ((0, 512), (1, 256)):
                        last = pe.matmul(mod_ps[:, 2 * layer + half, 0:width], silu_rows[:, layer, :],
                                         wmod[:, layer, 512 * half:512 * half + width], start=True, stop=True)
                last.then_inc(mod_done, 1)

            @block.vector
            def _(dve):
                link = Chain(dve, steps)
                dve.wait_ge(exp_done, 1)
                link.then(dve.tensor_scalar(den[:, :, :], cneg[:, :, :], 1.0, None, ALU.add))
                link.then(dve.reciprocal(rden[:, :, :], den[:, :, :]))
                link.then(dve.tensor_tensor(silu[:, :, :], cT[:, :, :], rden[:, :, :], ALU.mult))
                for layer in range(2):
                    last = dve.tensor_copy(silu_rows[:, layer, :].rearrange("p (l n) -> p l n", n=SEG),
                                           silu[:, layer, :].unsqueeze(2).to_broadcast([P, B, SEG]))
                last.then_inc(silu_done, 1)
                dve.wait_ge(mod_done, 1)

                def part(layer, k):
                    return mod_ps[:, 2 * layer + k // 4, (k % 4) * D:(k % 4) * D + D]

                for layer, (shift, scale, shift2, scale2) in enumerate(
                        ((M0_SHIFT, M0_SCALE, M0_SHIFT2, M0_SCALE2), (M1_SHIFT, M1_SCALE, M1_SHIFT2, M1_SCALE2))):
                    dve.tensor_copy(tile[:, shift, :], part(layer, 0))
                    dve.tensor_scalar(tile[:, scale, :], part(layer, 1), 1.0, None, ALU.add)
                    dve.tensor_copy(tile[:, shift2, :], part(layer, 3))
                    dve.tensor_scalar(tile[:, scale2, :], part(layer, 4), 1.0, None, ALU.add)
                    for g, k in enumerate((2, 5)):
                        last = dve.tensor_scalar(sign[:, layer, g, :], part(layer, k), 0.0, 2.0, ALU.is_ge, ALU.mult)
                link.then(last)
                link.then(dve.tensor_scalar(sign[:, :, :, :], sign[:, :, :, :], -1.0, None, ALU.add))
                for layer in range(2):
                    for g, k in enumerate((2, 5)):
                        last = dve.tensor_tensor(size[:, layer, g, :], sign[:, layer, g, :], part(layer, k), ALU.mult)
                link.then(last)
                link.then(dve.scalar_tensor_tensor(gate[:, :, :, :], size[:, :, :, :], 0.25, sign[:, :, :, :], ALU.max, ALU.mult))
                dve.tensor_copy(tile[:, M0_GATE, :], gate[:, 0, 0, :])
                dve.tensor_copy(tile[:, M1_GATE, :], gate[:, 1, 0, :])
                dve.tensor_tensor(tile[:, M0_GAIN2, :], gate[:, 0, 1, :], rows[:, 0, :], ALU.mult)
                dve.tensor_tensor(tile[:, M0_BIAS2, :], gate[:, 0, 1, :], rows[:, 1, :], ALU.mult)
                dve.tensor_tensor(tile[:, M1_BIAS, :], gate[:, 1, 0, :], rows[:, 2, :], ALU.mult)
                dve.tensor_tensor(tile[:, M1_GAIN2, :], gate[:, 1, 1, :], rows[:, 3, :], ALU.mult)
                dve.tensor_tensor(tile[:, M1_BIAS2, :], gate[:, 1, 1, :], rows[:, 4, :],
                                  ALU.mult).then_inc(tiles_done, 1)


class Layer0Inputs:

    RING = 4
    AHEAD = 3
    LOADS = 7

    def __init__(self, scope, x, wqkv, wo, ident, upto, last_of_batch, cos2, sin2):
        sb = scope.sb
        self.x_t = tiles_of(x)
        self.xin = sb("l0_x", [P, self.RING, 2, D])
        self.wqkv, self.wo = sb("l0_wqkv", [P, 3 * D]), sb("l0_wo", [P, D])
        self.ident, self.upto, self.last = sb("l0_ident", [P, P]), sb("l0_upto", [P, P]), sb("l0_last", [P, P])
        self.cos, self.sin = sb("l0_cos", [P, TILES, D0]), sb("l0_sin", [P, TILES, D0])
        self.constants = ((self.wqkv, wqkv), (self.wo, wo), (self.ident, ident), (self.upto, upto),
                          (self.last, last_of_batch), (self.cos, cos2), (self.sin, sin2))
        assert len(self.constants) == self.LOADS
        self.loaded = scope.sem("l0_loaded")
        self.x_in = [Signal(scope, f"l0_x_in{k}") for k in range(self.RING)]

    def load_x(self, sp, n, slot):
        for t in range(2):
            self.x_in[slot].mark(sp.dma_start(self.xin[:, slot, t, :], self.x_t[n * 2 + t]), 16)

    def start(self, sp):
        for n in range(self.AHEAD):
            self.load_x(sp, n, n)
        for dst, src in self.constants:
            sp.dma_start(dst[tuple(slice(None) for _ in dst.shape)], src).then_inc(self.loaded, 16)


def layer0(nc, inputs, mods, next_w, next_wo, w_hi, w_lo, next_wo_sb, out):
    s = Scope(nc)
    out_t = tiles_of(out)
    RING, xin, x_in, loaded = inputs.RING, inputs.xin, inputs.x_in, inputs.loaded
    wqkv_sb, wo_sb, ident_sb, upto_sb, last_sb = inputs.wqkv, inputs.wo, inputs.ident, inputs.upto, inputs.last
    cos_sb, sin_sb = inputs.cos, inputs.sin
    with s.stack:
        sb = s.sb
        consts = sb("l0_mods", [P, 7, D])
        eps = sb("l0_eps", [P, 1])
        x1, biased, y = sb("l0_x1", [P, 2, D]), sb("l0_biased", [P, 2, D]), sb("l0_y", [P, 2, 2, D])
        scaled, normed = sb("l0_scaled", [P, 3, 2, D]), sb("l0_normed", [P, 2, D])
        stats, mv = sb("l0_stats", [P, 3, 2, 6]), sb("l0_mean_var", [P, 3, 2, 2])
        std, rstd = sb("l0_std", [P, 3, 2]), sb("l0_rstd", [P, 3, 2])
        h, hT = sb("l0_h", [P, 2, D]), sb("l0_hT", [P, 2, P])
        raw, swapped = sb("l0_raw", [P, 2, 2, 2 * D]), sb("l0_swapped", [P, 2, 2, 2 * D])
        straight, turned = sb("l0_straight", [P, 2, 2 * D]), sb("l0_turned", [P, 2, 2 * D])
        rotated = sb("l0_rotated", [P, 2, 2 * D])
        qk = sb("l0_qk", [P, 2, 2, 2 * D])
        v1 = sb("l0_v1", [P, 2, 2, H0, V0])
        kv = sb("l0_kv", [P, 2, 2, H0, D0, V0])
        cum = sb("l0_cum", [P, 2, H0, D0, V0])
        prod = sb("l0_prod", [P, 2, H0, D0, V0])
        nd = sb("l0_numden", [P, 2, H0, V0])
        den, rden = sb("l0_den", [P, 2, H0]), sb("l0_rden", [P, 2, H0])
        o, oT = sb("l0_o", [P, 2, D]), sb("l0_oT", [P, 2, P])
        PART = next_w.shape[1] // PAIRS
        staged = sb("l0_staged", [P, PART])
        hT_ps, oT_ps, y_ps = s.psum("l0_hT_ps", [P, 2, 256]), s.psum("l0_oT_ps", [P, 2, 256]), s.psum("l0_y_ps", [P, 2, 256])
        proj_ps, cum_ps = s.psum("l0_proj_ps", [P, 2, 512]), s.psum("l0_cum_ps", [P, 3, 512])

        ready, settled = s.sem("l0_ready"), s.sem("l0_settled")
        staged_in, hi_done, lo_done, next_wo_in = (Signal(s, "l0_staged_in"), Signal(s, "l0_hi_done"),
                                                   Signal(s, "l0_lo_done"), Signal(s, "l0_next_wo_in"))
        y_stored = [Signal(s, f"l0_y_stored{k}", 32) for k in range(2)]
        dve_steps = s.sem("l0_dve_steps")
        mv_done = [Signal(s, f"l0_mv_done{k}") for k in range(3)]
        std_done = [Signal(s, f"l0_std_done{k}") for k in range(3)]
        h_done, hT_ps_done, hT_done = Signal(s, "l0_h_done"), Signal(s, "l0_hT_ps_done", 1), Signal(s, "l0_hT_done", 1)
        proj_done, raw_done = Signal(s, "l0_proj_done", 1), Signal(s, "l0_raw_done", 1)
        straight_done, rotated_done, qk_done = Signal(s, "l0_straight_done"), Signal(s, "l0_rotated_done", 1), Signal(s, "l0_qk_done", 1)
        kv_done, cum_ps_done, cum_done = Signal(s, "l0_kv_done", 2), Signal(s, "l0_cum_ps_done", 6), Signal(s, "l0_cum_done", 3)
        prod_done = [Signal(s, f"l0_prod_done{t}", 1) for t in range(2)]
        sums_done = Signal(s, "l0_sums_done", 2)
        o_done, oT_ps_done, oT_done = Signal(s, "l0_o_done"), Signal(s, "l0_oT_ps_done", 1), Signal(s, "l0_oT_done", 1)
        y_ps_done, x1_done, biased_done, y_done = (Signal(s, "l0_y_ps_done", 1), Signal(s, "l0_x1_done", 2),
                                                   Signal(s, "l0_biased_done"), Signal(s, "l0_y_done", 1))

        LOADS = inputs.LOADS + 1
        BANKS = len(HEADS_OF_BANK)
        first = [sum(HEADS_OF_BANK[:k]) for k in range(BANKS)]

        def bank(k):
            return slice(first[k], first[k] + HEADS_OF_BANK[k]), HEADS_OF_BANK[k] * D0 * V0

        def products(t, par):
            flat = "p h d m -> p (h d) m"
            return (prod[:, t].rearrange(flat), cum[:, t].rearrange(flat), qk[:, par, t, 0:D].unsqueeze(2).to_broadcast([P, D, V0]))

        with nc.Block() as block:

            @block.sync
            def _(sp):
                sp.dma_start(consts[:, :, :], mods[0:7].rearrange("m p d -> p m d")).then_inc(loaded, 16)
                for k in range(2):
                    y_stored[k].give_ahead(sp)

                def store(n, par):
                    y_done.wait(sp, n + 1)
                    for t in range(2):
                        y_stored[par].mark(sp.dma_start(out_t[n * 2 + t], y[:, par, t, :]), 16)

                for half in range(2):
                    next_wo_in.mark(sp.dma_start(
                        next_wo_sb[half * P // 2:(half + 1) * P // 2, :, :],
                        next_wo.rearrange("(i c q) e -> q i c e", i=P // 2, q=2)[half]), 16)

                def body(i, b):
                    n = i * RING + b
                    if in_range(i, b + 3, RING):
                        x1_done.wait(sp, n)
                        inputs.load_x(sp, n + 3, (b + 3) % RING)
                    lo_done.wait(sp, n)
                    staged_in.mark(sp.dma_start(staged[:, :], next_w[:, bass.ds(n * PART, PART)]), 16)
                    if in_range(i, b - 1, RING):
                        store(n - 1, (b - 1) % 2)

                all_rounds(sp, RING, body)
                store(PAIRS - 1, (PAIRS - 1) % 2)
                next_wo_in.wait(sp, 32)
                for k in range(2):
                    y_stored[k].wait(sp, PAIRS // 2 * 32)

            @block.gpsimd
            def _(pool):
                pool.memset(eps[:, :], EPS_LN)
                pool.memset(v1[:, :, :, :, :], 1.0)
                pool.memset(cum[:, 1], 0.0).then_inc(ready, 1)
                qk_done.give_ahead(pool)
                cum_ps_done.give_ahead(pool)
                rotated_done.give_ahead(pool)
                sums_done.give_ahead(pool)
                y_done.give_ahead(pool)
                pool.wait_ge(loaded, LOADS * 16)

                def rotate(n, par):
                    raw_done.wait(pool, n + 1)
                    rotated_done.wait(pool, n)
                    straight_done.mark(pool.tensor_tensor(
                        straight[:, :, :].rearrange("p t (g d) -> p t g d", d=D0),
                        raw[:, par].rearrange("p t (g d) -> p t g d", d=D0),
                        cos_sb[:, bass.ds(n * 2, 2), :].unsqueeze(2).to_broadcast([P, 2, 2 * H0, D0]), ALU.mult))

                def multiply(n, par, tiles=range(2)):
                    qk_done.wait(pool, n + 1)
                    cum_ps_done.wait(pool, 6 * (n - 1))
                    for t in tiles:
                        k = qk[:, par, t, D:2 * D].rearrange("p (h d) -> p h d", d=D0)
                        kv_done.mark(pool.tensor_tensor(
                            kv[:, par, t], k.unsqueeze(3).to_broadcast([P, H0, D0, V0]),
                            v1[:, par, t].unsqueeze(2).to_broadcast([P, H0, D0, V0]), ALU.mult))

                def attend(n, par):
                    cum_done.wait(pool, 6 * n + 6)
                    sums_done.wait(pool, 2 * n)
                    dst, sums, q = products(1, par)
                    prod_done[1].mark(pool.tensor_tensor(dst, sums, q, ALU.mult))

                def bias(n):
                    x1_done.wait(pool, n + 1)
                    y_done.wait(pool, n)
                    biased_done.mark(pool.tensor_tensor(
                        biased[:, :, :], x1[:, :, :], consts[:, M0_BIAS2, :].unsqueeze(1).to_broadcast([P, 2, D]), ALU.add))

                rotate(0, 0)
                multiply(0, 0)

                def body(i, b):
                    n = i * RING + b
                    if in_range(i, b + 1, RING):
                        rotate(n + 1, (b + 1) % 2)
                        multiply(n + 1, (b + 1) % 2, [0])
                    attend(n, b % 2)
                    if in_range(i, b + 1, RING):
                        multiply(n + 1, (b + 1) % 2, [1])
                    if in_range(i, b - 1, RING):
                        bias(n - 1)
                    hi_done.wait(pool, n + 1)
                    part = bass.ds(n * PART, PART)
                    lo_done.mark(pool.tensor_tensor(w_lo[:, part], staged[:, :], w_hi[:, part].bitcast(F32), ALU.subtract))

                all_rounds(pool, RING, body)
                bias(PAIRS - 1)

            @block.scalar
            def _(act):
                act.wait_ge(ready, 1)
                kv_done.give_ahead(act)
                y_ps_done.give_ahead(act)
                for t in range(2):
                    prod_done[t].give_ahead(act)

                def root(k, n):
                    mv_done[k].wait(act, n + 1)
                    std_done[k].mark(act.activation(std[:, k, :], mv[:, k, :, 1], ACT.Sqrt, bias=eps[:, 0:1]))

                def turn(n):
                    hT_ps_done.wait(act, n + 1)
                    proj_done.wait(act, n)
                    hT_done.mark(act.copy(hT[:, :, :], hT_ps[:, :, 0:P]))

                def evacuate(par):
                    act.copy(raw[:, par], proj_ps[:, :, 0:2 * D])
                    src, dst = (a.rearrange("p t (f e) -> p t f e", e=2) for a in (proj_ps[:, :, 0:2 * D], swapped[:, par]))
                    for e in range(2):
                        act.copy(dst[:, :, :, e], src[:, :, :, 1 - e])
                    raw_done.mark(act.copy(v1[:, par, :, :, 0:D0],
                                           proj_ps[:, :, 2 * D:3 * D].rearrange("p t (h d) -> p t h d", d=D0)))

                def project(n, par):
                    proj_done.wait(act, n + 1)
                    rotated_done.wait(act, n - 1)
                    kv_done.wait(act, 2 * (n - 1))
                    evacuate(par)

                def rectify(n, par):
                    rotated_done.wait(act, n + 1)
                    for t in range(2):
                        prod_done[t].wait(act, n - 1)
                    qk_done.mark(act.activation(qk[:, par, :, :], rotated[:, :, :], ACT.Relu))

                def sums(n, t):
                    prod_done[t].wait(act, n)
                    for k in range(BANKS):
                        heads, width = bank(k)
                        cum_ps_done.wait(act, 6 * n + 3 * t + k + 1)
                        cum_done.mark(act.copy(cum[:, t, heads].rearrange("p h d m -> p (h d m)"), cum_ps[:, k, 0:width]))

                def attended(n):
                    oT_ps_done.wait(act, n + 1)
                    y_ps_done.wait(act, n)
                    oT_done.mark(act.copy(oT[:, :, :], oT_ps[:, :, 0:P]))

                for n in range(2):
                    root(0, n)
                    turn(n)
                    if n == 0:
                        proj_done.wait(act, 1)
                        evacuate(0)
                rotated_done.wait(act, 1)
                qk_done.mark(act.activation(qk[:, 0, :, :], rotated[:, :, :], ACT.Relu))
                project(1, 1)

                def body(i, b):
                    n = i * RING + b
                    sums(n, 0)
                    if in_range(i, b - 1, RING):
                        attended(n - 1)
                    if in_range(i, b + 2, RING):
                        root(0, n + 2)
                    if in_range(i, b + 1, RING):
                        rectify(n + 1, (b + 1) % 2)
                    sums(n, 1)
                    if in_range(i, b + 2, RING):
                        turn(n + 2)
                    if in_range(i, b - 1, RING):
                        root(1, n - 1)
                    if in_range(i, b + 2, RING):
                        project(n + 2, b % 2)
                    if in_range(i, b - 1, RING):
                        root(2, n - 1)
                    staged_in.wait(act, 16 * (n + 1))
                    hi_done.mark(act.copy(w_hi[:, bass.ds(n * PART, PART)], staged[:, :]))

                all_rounds(act, RING, body)
                attended(PAIRS - 1)
                root(1, PAIRS - 1)
                root(2, PAIRS - 1)

            @block.tensor
            def _(pe):
                pe.wait_ge(loaded, LOADS * 16)
                pe.wait_ge(ready, 1)
                cum_done.give_ahead(pe)
                raw_done.give_ahead(pe)
                x1_done.give_ahead(pe)
                oT_ps_done.give_ahead(pe)
                proj_done.give_ahead(pe)
                hT_done.give_ahead(pe)
                oT_done.give_ahead(pe)

                def turn(n):
                    h_done.wait(pe, n + 1)
                    hT_done.wait(pe, n)
                    for t in range(2):
                        last = pe.transpose(hT_ps[:, t, 0:P], h[:, t, :], ident_sb[:, :])
                    hT_ps_done.mark(last)

                def project(n):
                    hT_done.wait(pe, n + 1)
                    raw_done.wait(pe, n)
                    for t in range(2):
                        last = pe.matmul(proj_ps[:, t, 0:3 * D], hT[:, t, :], wqkv_sb[:, :], start=True, stop=True)
                    proj_done.mark(last)

                def sums(n, t, par):
                    kv_done.wait(pe, 2 * n + t + 1)
                    for k in range(BANKS):
                        heads, width = bank(k)
                        cum_done.wait(pe, 6 * n + 3 * t + k - 3 + 1)
                        pe.matmul(cum_ps[:, k, 0:width], upto_sb[:, :],
                                  kv[:, par, t, heads].rearrange("p h d m -> p (h d m)"), start=True, stop=False)
                        cum_ps_done.mark(pe.matmul(
                            cum_ps[:, k, 0:width], last_sb[:, :],
                            cum[:, 1 - t, heads].rearrange("p h d m -> p (h d m)"), start=False, stop=True))

                def attended(n):
                    o_done.wait(pe, n + 1)
                    oT_done.wait(pe, n)
                    for t in range(2):
                        last = pe.transpose(oT_ps[:, t, 0:P], o[:, t, :], ident_sb[:, :])
                    oT_ps_done.mark(last)

                def output(n):
                    oT_done.wait(pe, n + 1)
                    x1_done.wait(pe, n)
                    for t in range(2):
                        last = pe.matmul(y_ps[:, t, 0:D], oT[:, t, :], wo_sb[:, :], start=True, stop=True)
                    y_ps_done.mark(last)

                for n in range(2):
                    turn(n)
                    project(n)

                def body(i, b):
                    n = i * RING + b
                    sums(n, 0, b % 2)
                    if in_range(i, b - 1, RING):
                        attended(n - 1)
                    sums(n, 1, b % 2)
                    if in_range(i, b - 1, RING):
                        output(n - 1)
                    if in_range(i, b + 2, RING):
                        turn(n + 2)
                        project(n + 2)

                all_rounds(pe, RING, body)
                attended(PAIRS - 1)
                output(PAIRS - 1)

            @block.vector
            def _(dve):
                dve.wait_ge(loaded, LOADS * 16)
                hT_ps_done.give_ahead(dve)
                steps = Steps(dve, dve_steps)

                def mod(k):
                    return consts[:, k, :]

                class Norm:

                    def __init__(self, k, n, src, gain):
                        self.k, self.n, self.src, self.gain = k, n, src, gain

                    def stats(self):
                        for t in range(2):
                            last = dve.bn_stats(stats[:, self.k, t, :], self.src[:, t, :])
                        self.had = steps.mark(last)

                    def mean(self):
                        steps.wait(self.had)
                        settle(dve, settled)
                        for t in range(2):
                            last = dve.bn_aggr(mv[:, self.k, t, :], stats[:, self.k, t, :])
                        mv_done[self.k].mark(last)

                    def scale(self):
                        mv_done[self.k].wait(dve, self.n + 1)
                        for t in range(2):
                            last = dve.scalar_tensor_tensor(scaled[:, self.k, t, :], self.src[:, t, :], mv[:, self.k, t, 0:1],
                                                            mod(self.gain), ALU.subtract, ALU.mult)
                        self.had = steps.mark(last)

                    def invert(self):
                        std_done[self.k].wait(dve, self.n + 1)
                        self.had = steps.mark(dve.reciprocal(rstd[:, self.k, :], std[:, self.k, :]))

                    def finish(self, dst, shift):
                        steps.wait(self.had)
                        for t in range(2):
                            last = dve.scalar_tensor_tensor(dst[:, t, :], scaled[:, self.k, t, :], rstd[:, self.k, t:t + 1],
                                                            mod(shift) if isinstance(shift, int) else shift[:, t, :],
                                                            ALU.mult, ALU.add)
                        return last

                def add_x(n, slot, had):
                    steps.wait(had)
                    x1_done.mark(dve.tensor_tensor(x1[:, :, :], x1[:, :, :], xin[:, slot], ALU.add))
                    x1_done.wait(dve, n + 1)

                def finish(n, par, uses, norm):
                    norm.invert()
                    biased_done.wait(dve, n + 1)
                    y_stored[par].wait(dve, 32 * uses)
                    y_done.mark(norm.finish(y[:, par], biased))

                def turn(n, par):
                    raw_done.wait(dve, n + 1)
                    last = dve.tensor_tensor(
                        turned[:, :, :].rearrange("p t (g d) -> p t g d", d=D0), swapped[:, par].rearrange("p t (g d) -> p t g d", d=D0),
                        sin_sb[:, bass.ds(n * 2, 2), :].unsqueeze(2).to_broadcast([P, 2, 2 * H0, D0]), ALU.mult)
                    return steps.mark(last)

                def rotate(n, had):
                    steps.wait(had)
                    straight_done.wait(dve, n + 1)
                    qk_done.wait(dve, n)
                    rotated_done.mark(dve.tensor_tensor(rotated[:, :, :], straight[:, :, :], turned[:, :, :], ALU.add))

                def product(n, par):
                    cum_done.wait(dve, 6 * n + 3)
                    dst, sums, q = products(0, par)
                    prod_done[0].mark(dve.tensor_tensor(dst, sums, q, ALU.mult))

                def reduce(n, t):
                    prod_done[t].wait(dve, n + 1)
                    sums_done.mark(dve.tensor_reduce(nd[:, t], prod[:, t].rearrange("p h d m -> p h m d"), AX.X, ALU.add))

                A, B1, B2, C = 3, 1, 2, 8

                def body(i, b):
                    n = i * RING + b
                    has_a, has_b1, has_c = in_range(i, b + 2, RING), in_range(i, b + 1, RING), in_range(i, b - 1, RING)
                    steps.start(n * (A + B1 + B2 + C) + 2 * A + B1 - (C if has_c else 0) - (0 if has_b1 else A))
                    if has_a:
                        norm0 = Norm(0, n + 2, xin[:, (b + 2) % RING], M0_SCALE)
                        x_in[(b + 2) % RING].wait(dve, 32 * (i + (b + 2) // RING) + 32)
                        norm0.stats()
                    if has_b1:
                        turned_at = turn(n + 1, (b + 1) % 2)
                    if has_a:
                        norm0.mean()
                        norm0.scale()
                    if has_b1:
                        rotate(n + 1, turned_at)
                    if has_a:
                        norm0.invert()
                        hT_ps_done.wait(dve, n + 2)
                        h_done.mark(norm0.finish(h, M0_SHIFT))
                    if has_c:
                        norm1, norm2 = Norm(1, n - 1, x1, M0_SCALE2), Norm(2, n - 1, normed, M0_GAIN2)
                    product(n, b % 2)
                    if has_c:
                        y_ps_done.wait(dve, n)
                        gated_at = steps.mark(dve.tensor_tensor(x1[:, :, :], y_ps[:, :, 0:D], two(mod(M0_GATE)), ALU.mult))
                    reduce(n, 0)
                    if has_c:
                        add_x(n - 1, (b - 1) % RING, gated_at)
                        norm1.stats()
                        norm1.mean()
                        norm1.scale()
                    reduce(n, 1)
                    if has_c:
                        norm1.invert()
                        normed_at = steps.mark(norm1.finish(normed, M0_SHIFT2))
                    sums_done.wait(dve, 2 * n + 2)
                    den_at = steps.mark(dve.tensor_scalar(den[:, :, :], nd[:, :, :, D0], EPS_ATT, None, ALU.add))
                    if has_c:
                        steps.wait(normed_at)
                        norm2.stats()
                    steps.wait(den_at)
                    rden_at = steps.mark(dve.reciprocal(rden[:, :, :], den[:, :, :]))
                    if has_c:
                        norm2.mean()
                    steps.wait(rden_at)
                    oT_ps_done.wait(dve, n)
                    o_done.mark(dve.tensor_tensor(o[:, :, :].rearrange("p t (h d) -> p t h d", d=D0), nd[:, :, :, 0:D0],
                                                  rden[:, :, :].unsqueeze(3).to_broadcast([P, 2, H0, D0]), ALU.mult))
                    if has_c:
                        norm2.scale()
                        finish(n - 1, (b - 1) % 2, i * 2 + (b - 1) // 2, norm2)
                    assert steps.n == A * has_a + B1 * has_b1 + B2 + C * has_c, steps.n

                steps.start(0)
                for n in range(2):
                    norm0 = Norm(0, n, xin[:, n], M0_SCALE)
                    x_in[n].wait(dve, 32)
                    norm0.stats()
                    norm0.mean()
                    norm0.scale()
                    norm0.invert()
                    hT_ps_done.wait(dve, n)
                    h_done.mark(norm0.finish(h, M0_SHIFT))
                rotate(0, turn(0, 0))
                all_rounds(dve, RING, body)
                n = PAIRS - 1
                steps.start(PAIRS * (A + B1 + B2 + C) - C)
                norm1, norm2 = Norm(1, n, x1, M0_SCALE2), Norm(2, n, normed, M0_GAIN2)
                y_ps_done.wait(dve, n + 1)
                add_x(n, n % RING, steps.mark(dve.tensor_tensor(x1[:, :, :], y_ps[:, :, 0:D], two(mod(M0_GATE)), ALU.mult)))
                norm1.stats()
                norm1.mean()
                norm1.scale()
                norm1.invert()
                steps.wait(steps.mark(norm1.finish(normed, M0_SHIFT2)))
                norm2.stats()
                norm2.mean()
                norm2.scale()
                finish(n, n % 2, n // 2, norm2)


def layer1_attention(nc, x, w_hi, w_lo, wo_sb, mods, ident, fold, out):
    s = Scope(nc)
    x_t, out_t = tiles_of(x), tiles_of(out)
    HEADS, DH = 64, 64
    HALF = P // 2
    TOK = 2 * P
    CHUNKS = HEADS * DH // P
    UNIT = 4
    UNITS = CHUNKS // UNIT
    SCALE = DH ** -0.5
    BATCHES = [7] * 4 + [6] * 6
    assert sum(BATCHES) == HALF
    NB = len(BATCHES)
    W = DH + 1
    PLAN = []
    for sub, k_after in enumerate(((2, 6, NB - 1, NB - 1), (1, 3, 5, 7))):
        for k in range(NB):
            PLAN.append(("att", sub * NB + k))
            PLAN += [("k", 4 * sub + n) for n, at in enumerate(k_after) if at == k]
    PLAN += [("q", 0), ("q", 1)]
    for u in range(2, UNITS):
        PLAN += [("v", u - 2), ("q", u)]
    PLAN += [("v", UNITS - 2), ("v", UNITS - 1)]
    ROUND = len(PLAN)
    assert [u for w, u in PLAN if w == "k"] == list(range(UNITS))

    def runs(g, place):
        if not isinstance(g, int) or 0 <= g < PAIRS - 1:
            return True
        return (PLAN[place][0] == "att") == (g >= 0)

    def evacuates(engine, place):
        w = PLAN[place][0]
        return w == "att" or (w == "q") == (engine == "act")

    def units_to(g, place, of=lambda p: True):
        head = sum(of(p) for p in range(ROUND) if runs(-1, p))
        here = sum(of(p) for p in range(place + 1) if runs(g, p))
        if isinstance(g, int) and g == -1:
            return here
        return g * sum(of(p) for p in range(ROUND)) + head + here

    with s.stack:
        sb = s.sb
        consts = sb("l1_mods", [P, 4, D])
        ident_sb, fold_sb = sb("l1_ident", [P, P]), sb("l1_fold", [P, P])
        q = sb("l1_q", [P, P, HEADS])
        v = sb("l1_v", [P, P, W])
        att = sb("l1_att", [P, CHUNKS, P])
        ksum = sb("l1_ksum", [P, UNIT, TOK])
        ksum_all = sb("l1_ksum_all", [P, TOK])
        ks = sb("l1_ks", [P, P])
        den_a, rden_a = sb("l1_den_a", [HALF, 8]), sb("l1_rden_a", [HALF, 8])
        den_b, rden_b = sb("l1_den_b", [P, 2, HALF]), sb("l1_rden_b", [P, 2, HALF])
        eps, eps_att = sb("l1_eps", [P, 1]), sb("l1_eps_att", [P, 1])
        xin, h = sb("l1_x", [P, 2, D]), sb("l1_h", [P, 2, D])
        xres, y = sb("l1_xres", [P, 2, D]), sb("l1_y", [P, D])
        stats, mv = sb("l1_stats", [P, 2, 6]), sb("l1_mean_var", [P, 2, 2])
        std, rstd = sb("l1_std", [P, 2]), sb("l1_rstd", [P, 2])
        hT_hi, hT_lo = sb("l1_hT_hi", [P, 2, 2, HALF], F32R), sb("l1_hT_lo", [P, 2, 2, HALF], F32R)
        ring = s.psum("l1_ring", [P, 3, 2, 512])
        o_ps = s.psum("l1_o_ps", [P, 512])
        misc_ps = s.psum("l1_misc_ps", [P, 512])
        hT_ps, ks_ps = misc_ps[:, 0:TOK], misc_ps[:, TOK:2 * TOK]

        loaded, ready = s.sem("l1_loaded"), s.sem("l1_ready")
        dve_steps = s.sem("l1_dve_steps")
        settled, pe_settled = s.sem("l1_settled"), s.sem("l1_pe_settled")
        x_in = Signal(s, "l1_x_in")
        y_stored = Signal(s, "l1_y_stored", 16)
        unit_done = Signal(s, "l1_unit_done")
        evac = {"act": Signal(s, "l1_act_evac"), "dve": Signal(s, "l1_dve_evac")}
        mv_done, std_done, h_done = Signal(s, "l1_mv_done"), Signal(s, "l1_std_done"), Signal(s, "l1_h_done")
        hT_ps_done, hT_hi_done, hT_done = Signal(s, "l1_hT_ps_done", 1), Signal(s, "l1_hT_hi_done"), Signal(s, "l1_hT_done")
        ks_ps_done, ks_done = Signal(s, "l1_ks_ps_done"), Signal(s, "l1_ks_done")
        rden_b_done, att_pool_done = Signal(s, "l1_rden_b_done"), Signal(s, "l1_att_pool_done")
        o_ps_done, y_done, xres_done = Signal(s, "l1_o_ps_done"), Signal(s, "l1_y_done", 2), Signal(s, "l1_xres_done")
        xres_in, ksum_done = Signal(s, "l1_xres_in"), Signal(s, "l1_ksum_done")

        LOADS = 3

        def buffer(place):
            return ring[:, place % 3]

        def unit_ready(eng, g, place):
            unit_done.wait(eng, units_to(g, place))

        def wait_evacuated(eng, by, g, place):
            evac[by].wait(eng, units_to(g, place, lambda p: evacuates(by, p)))

        def place_of(w, u):
            return PLAN.index((w, u))

        def plan(g):
            return [(place, w, u) for place, (w, u) in enumerate(PLAN) if runs(g, place)]

        def rounds(eng, body, last):
            with eng.Fori(0, PAIRS - 1) as g:
                body(g)
            last(PAIRS - 1)

        def pieces(place):
            ps = buffer(place).rearrange("p a b -> p (a b)").rearrange("p (c t) -> p c t", t=TOK)
            for par in range(2):
                for ab in range(2):
                    yield par, ab, ps[HALF * par:HALF * par + HALF, :, P * ab:P * ab + P]

        def half(ab):
            return slice(HALF * ab, HALF * ab + HALF)

        def v_piece(u, par, ab):
            first = 32 * par + UNIT * u
            return v[half(ab), :, first:first + UNIT].rearrange("p t c -> p c t")

        def batch(k):
            return sum(BATCHES[:k]), BATCHES[k]

        def products(place, ab, m):
            return buffer(place)[half(ab), ab, 0:m * W].rearrange("p (t j) -> p t j", j=W)

        with nc.Block() as block:

            @block.sync
            def _(sp):
                sp.dma_start(consts[:, :, :], mods[M1_SHIFT:M1_BIAS + 1].rearrange("m p d -> p m d")).then_inc(loaded, 16)
                sp.dma_start(ident_sb[:, :], ident).then_inc(loaded, 16)
                sp.dma_start(fold_sb[:, :], fold).then_inc(loaded, 16)

                def load(dst, done, g):
                    for t in range(2):
                        done.mark(sp.dma_start(dst[:, t, :], x_t[g * 2 + t]), 16)

                def store(g):
                    for t in range(2):
                        y_done.wait(sp, 2 * g + t + 1)
                        y_stored.mark(sp.dma_start(out_t[g * 2 + t], y[:, :]), 16)

                load(xin, x_in, 0)
                load(xres, xres_in, 0)
                h_done.wait(sp, 1)
                load(xin, x_in, 1)

                def body(g, more=True):
                    if more:
                        h_done.wait(sp, g + 2)
                        load(xin, x_in, g + 2)
                    store(g)
                    load(xres, xres_in, g + 1)

                with sp.Fori(0, PAIRS - 2) as g:
                    body(g)
                body(PAIRS - 2, False)
                store(PAIRS - 1)
                y_stored.wait(sp, TILES * 16)

            @block.gpsimd
            def _(pool):
                pool.memset(eps[:, :], EPS_LN)
                pool.memset(eps_att[:, :], EPS_ATT).then_inc(ready, 1)
                y_done.give_ahead(pool)
                y_stored.give_ahead(pool)
                hT_ps_done.give_ahead(pool)
                pool.wait_ge(loaded, LOADS * 16)

                def residual(g):
                    xres_in.wait(pool, 32 * g + 32)
                    xres_done.mark(pool.tensor_tensor(
                        xres[:, :, :], xres[:, :, :], consts[:, 3, :].unsqueeze(1).to_broadcast([P, 2, D]), ALU.add))

                def scale_att(g, sub):
                    for k in range(NB):
                        t0, m = batch(k)
                        rden_b_done.wait(pool, NB * (2 * g + sub) + k + 1)
                        part = att[:, :, HALF + t0:HALF + t0 + m].rearrange("p c t -> p t c")
                        last = pool.tensor_tensor(
                            part, part, rden_b[:, sub, t0:t0 + m].unsqueeze(2).to_broadcast([P, m, CHUNKS]), ALU.mult)
                    att_pool_done.mark(last)

                def body(g):
                    residual(g)
                    scale_att(g, 0)
                    scale_att(g, 1)

                rounds(pool, body, body)

            @block.scalar
            def _(act):
                act.wait_ge(ready, 1)

                def root(g):
                    mv_done.wait(act, g + 1)
                    std_done.mark(act.activation(std[:, :], mv[:, :, 1], ACT.Sqrt, bias=eps[:, 0:1]))

                def turn(g):
                    hT_ps_done.wait(act, g + 1)
                    hT_hi_done.mark(act.copy(hT_hi[:, :, :, :].rearrange("p a s t -> p s a t"),
                                             hT_ps.rearrange("p (s a t) -> p s a t", s=2, a=2)))

                def attend(g, place, u):
                    sub, k = divmod(u, NB)
                    t0, m = batch(k)
                    unit_ready(act, g, place)
                    ps = products(place, 1, m)
                    for par in range(2):
                        act.activation(den_b[half(par), sub, t0:t0 + m], ps[:, :, DH], ACT.Identity,
                                       bias=eps_att[half(1), 0:1])
                        last = act.copy(att[half(par), :, HALF + t0:HALF + t0 + m].rearrange("p c t -> p t c"),
                                        ps[:, :, CHUNKS * par:CHUNKS * par + CHUNKS])
                    evac["act"].mark(last)

                def queries(g, place, u):
                    unit_ready(act, g, place)
                    for par, ab, ps in pieces(place):
                        dst = q[half(ab), :, 2 * UNIT * u + par:2 * UNIT * (u + 1):2].rearrange("p t c -> p c t")
                        last = act.activation(dst, ps, ACT.Relu, scale=SCALE)
                    evac["act"].mark(last)

                def key_sums(g):
                    ks_ps_done.wait(act, g + 2)
                    for ab in range(2):
                        src = ks_ps[half(ab), P * ab:P * ab + P]
                        act.copy(v[half(ab), :, DH], src)
                        last = act.copy(ks[half(ab), :], src)
                    ks_done.mark(last)

                def body(g, more=True):
                    for place, w, u in plan(g):
                        if w == "att":
                            attend(g, place, u)
                            if u == NB - 1 and more:
                                root(g + 2)
                        elif w == "q":
                            queries(g, place, u)
                            if u == 0:
                                key_sums(g)
                    if more:
                        turn(g + 2)

                root(0)
                turn(0)
                root(1)
                for place, w, u in plan(-1):
                    if w == "q":
                        queries(-1, place, u)
                        if u == 0:
                            key_sums(-1)
                turn(1)
                with act.Fori(0, PAIRS - 2) as g:
                    body(g)
                body(PAIRS - 2, False)
                body(PAIRS - 1, False)

            @block.tensor
            def _(pe):
                pe.wait_ge(loaded, LOADS * 16)

                def acquire(g, place):
                    users = [p for p in range(place) if p % 3 == place % 3 and runs(g, p)]
                    if not users:
                        if isinstance(g, int) and g == -1:
                            return
                        g = g - 1
                        users = [p for p in range(ROUND) if p % 3 == place % 3 and runs(g, p)]
                    for by in evac:
                        if evacuates(by, users[-1]):
                            wait_evacuated(pe, by, g, users[-1])

                def turn(g):
                    h_done.wait(pe, g + 1)
                    if not isinstance(g, int) or g:
                        hT_done.wait(pe, g)
                    for t in range(2):
                        last = pe.transpose(hT_ps[:, t * P:t * P + P], h[:, t, :], ident_sb[:, :])
                    hT_ps_done.mark(last)

                def project(g, place, w, u):
                    hi, lo = (a[:, :, :, :].rearrange("p a s t -> p (a s t)") for a in (hT_hi, hT_lo))
                    if u == 0:
                        hT_done.wait(pe, g + 2)
                    acquire(g, place)
                    ps = buffer(place).rearrange("p a b -> p (a b)").rearrange("p (c t) -> p c t", t=TOK)
                    for c in range(UNIT):
                        first = ("qkv".index(w) * CHUNKS + UNIT * u + c) * P
                        cols = slice(first, first + P)
                        pe.matmul(ps[:, c], w_hi[:, cols], hi, start=True, stop=False)
                        pe.matmul(ps[:, c], w_hi[:, cols], lo, start=False, stop=False)
                        last = pe.matmul(ps[:, c], w_lo[:, cols], hi, start=False, stop=True)
                    unit_done.mark(last)

                def key_sums(g):
                    ksum_done.wait(pe, g + 2)
                    ks_ps_done.mark(pe.matmul(ks_ps, fold_sb[:, :], ksum_all[:, :], start=True, stop=True))

                def attend(g, place, u):
                    sub, k = divmod(u, NB)
                    t0, m = batch(k)
                    if u == 0:
                        wait_evacuated(pe, "act", g - 1, place_of("q", UNITS - 1))
                        wait_evacuated(pe, "dve", g - 1, place_of("v", UNITS - 1))
                    acquire(g, place)
                    settle(pe, pe_settled)
                    for t in range(m):
                        tok = HALF * sub + t0 + t
                        for ab in range(2):
                            last = pe.matmul(products(place, ab, m)[:, t], q[half(ab), tok, :], v[half(ab), tok, :],
                                             start=True, stop=True)
                    unit_done.mark(last)

                def output(g, sub):
                    wait_evacuated(pe, "dve", g, place_of("att", NB * sub + NB - 1))
                    att_pool_done.wait(pe, 2 * g + sub + 1)
                    y_done.wait(pe, 2 * g + sub)
                    for c in range(CHUNKS):
                        last = pe.matmul(o_ps[:, 0:D], att[:, c, :], wo_sb[:, c, :], start=c == 0, stop=c == CHUNKS - 1)
                    o_ps_done.mark(last)

                def body(g, more=True):
                    units = plan(g)
                    for n, (place, w, u) in enumerate(units):
                        if w == "att":
                            attend(g, place, u)
                        else:
                            project(g, place, w, u)
                            if (w, u) == ("q", 0):
                                key_sums(g)
                        if n + 1 < len(units) and units[n + 1][1:] == ("att", NB):
                            output(g, 0)
                    if more:
                        turn(g + 2)
                    output(g, 1)

                turn(0)
                for place, w, u in plan(-1):
                    project(-1, place, w, u)
                    if (w, u) == ("q", 0):
                        key_sums(-1)
                turn(1)
                with pe.Fori(0, PAIRS - 2) as g:
                    body(g)
                body(PAIRS - 2, False)
                body(PAIRS - 1, False)

            @block.vector
            def _(dve):
                dve.wait_ge(loaded, LOADS * 16)
                link = Chain(dve, dve_steps)
                step = link.then

                def mod(k):
                    return consts[:, k, :].unsqueeze(1).to_broadcast([P, 2, D])

                def prepare(g):
                    x_in.wait(dve, 32 * g + 32)
                    for t in range(2):
                        last = dve.bn_stats(stats[:, t, :], xin[:, t, :])
                    step(last)
                    settle(dve, settled)
                    for t in range(2):
                        last = dve.bn_aggr(mv[:, t, :], stats[:, t, :])
                    mv_done.mark(last)
                    std_done.wait(dve, g + 1)
                    step(dve.reciprocal(rstd[:, :], std[:, :]))
                    hT_ps_done.wait(dve, g)
                    for t in range(2):
                        last = dve.tensor_scalar(h[:, t, :], xin[:, t, :], mv[:, t, 0:1], rstd[:, t:t + 1],
                                                 ALU.subtract, ALU.mult)
                    step(last)
                    step(dve.tensor_tensor(h[:, :, :], h[:, :, :], mod(1), ALU.mult))
                    h_done.mark(dve.tensor_tensor(h[:, :, :], h[:, :, :], mod(0), ALU.add))

                def rest(g):
                    hT_hi_done.wait(dve, g + 1)
                    hT_done.mark(dve.tensor_tensor(hT_lo[:, :, :, :].rearrange("p a s t -> p s a t"),
                                                   hT_ps.rearrange("p (s a t) -> p s a t", s=2, a=2),
                                                   hT_hi[:, :, :, :].bitcast(F32).rearrange("p a s t -> p s a t"), ALU.subtract))

                def keys(g, place, u):
                    unit_ready(dve, g, place)
                    ps = buffer(place).rearrange("p a b -> p (a b)")
                    acc = ksum[:, :, :].rearrange("p c t -> p (c t)")
                    if u == 0:
                        ksum_done.wait(dve, g + 1)
                        last = dve.tensor_scalar(acc, ps, 0.0, None, ALU.max)
                    else:
                        wait_evacuated(dve, "dve", g, place_of("k", u - 1))
                        last = dve.scalar_tensor_tensor(acc, ps, 0.0, acc, ALU.max, ALU.add)
                    evac["dve"].mark(last)
                    if u == UNITS - 1:
                        wait_evacuated(dve, "dve", g, place)
                        ks_ps_done.wait(dve, g + 1)
                        ksum_done.mark(dve.tensor_reduce(ksum_all[:, :], ksum[:, :, :].rearrange("p c t -> p t c"), AX.X, ALU.add))

                def values(g, place, u):
                    if u == 0:
                        ks_done.wait(dve, g + 2)
                    unit_ready(dve, g, place)
                    for par, ab, ps in pieces(place):
                        last = dve.tensor_tensor(v_piece(u, par, ab), ps,
                                                 ks[half(ab), :].unsqueeze(1).to_broadcast([HALF, UNIT, P]), ALU.mult)
                    evac["dve"].mark(last)

                def attend(g, place, u):
                    sub, k = divmod(u, NB)
                    t0, m = batch(k)
                    unit_ready(dve, g, place)
                    ps = products(place, 0, m)
                    step(dve.tensor_scalar(den_a[:, 0:m], ps[:, :, DH], EPS_ATT, None, ALU.add))
                    step(dve.reciprocal(rden_a[:, 0:m], den_a[:, 0:m]))
                    for par in range(2):
                        last = dve.tensor_tensor(
                            att[half(par), :, t0:t0 + m].rearrange("p c t -> p t c"),
                            ps[:, :, CHUNKS * par:CHUNKS * par + CHUNKS],
                            rden_a[:, 0:m].unsqueeze(2).to_broadcast([HALF, m, CHUNKS]), ALU.mult)
                    evac["dve"].mark(last)
                    wait_evacuated(dve, "act", g, place)
                    rden_b_done.mark(dve.reciprocal(rden_b[:, sub, t0:t0 + m], den_b[:, sub, t0:t0 + m]))

                def residual(g, sub):
                    o_ps_done.wait(dve, 2 * g + sub + 1)
                    xres_done.wait(dve, g + 1)
                    y_stored.wait(dve, 16 * (2 * g + sub))
                    step(dve.tensor_tensor(y[:, :], o_ps[:, 0:D], consts[:, 2, :], ALU.mult))
                    y_done.mark(dve.tensor_tensor(y[:, :], y[:, :], xres[:, sub, :], ALU.add))

                sizes = dict(prepare=4, attend=2, residual=1)

                def stage(fn, at, *args):
                    link.start(at)
                    fn(*args)
                    assert link.n == sizes[fn.__name__], (fn.__name__, link.n)
                    return at + link.n

                per_round = sizes["prepare"] + 2 * (NB * sizes["attend"] + sizes["residual"])

                def body(g, more=True, skipped=0):
                    at = 2 * sizes["prepare"] + g * per_round - skipped
                    for place, w, u in plan(g):
                        if w == "att":
                            at = stage(attend, at, g, place, u)
                            if u == NB - 1 and more:
                                at = stage(prepare, at, g + 2)
                            if u == NB:
                                at = stage(residual, at, g, 0)
                        elif w == "k":
                            keys(g, place, u)
                        elif w == "v":
                            values(g, place, u)
                    if more:
                        rest(g + 2)
                    stage(residual, at, g, 1)

                stage(prepare, 0, 0)
                rest(0)
                stage(prepare, sizes["prepare"], 1)
                for place, w, u in plan(-1):
                    if w == "k":
                        keys(-1, place, u)
                    elif w == "v":
                        values(-1, place, u)
                rest(1)
                with dve.Fori(0, PAIRS - 2) as g:
                    body(g)
                body(PAIRS - 2, False)
                body(PAIRS - 1, False, sizes["prepare"])


def layer1_ffn(nc, x, in_w, in_b, out_w, out_b, ln1_g, ln1_b, wg, w1, b1, w2, b2, mods, ident, upto, same_batch,
               batch_before, other_position, tile_mask, falling, y1_dram, y1T_dram, out):
    s = Scope(nc)
    x_t, out_t = tiles_of(x), tiles_of(out)
    NH, DH = 4, 32
    E, FF = 8, 512
    FC = FF // P
    CAP = B * L // E
    SCALE = DH ** -0.5
    W = DH + 1
    RING = 4
    BLOCK = P // E
    with s.stack:
        sb = s.sb
        consts = sb("f_mods", [P, 4, D])
        rows = sb("f_rows", [P, 4, D])
        in_w_sb, in_b_sb, out_w_sb = sb("f_in_w", [P, 3 * D]), sb("f_in_b", [P, 2]), sb("f_out_w", [P, D])
        wg_sb, ident_sb = sb("f_wg", [P, E]), sb("f_ident", [P, P])
        upto_sb, same_sb, before_sb = sb("f_upto", [P, P]), sb("f_same", [P, P]), sb("f_before", [P, P])
        other_sb = sb("f_other", [P, P])
        eps, power = sb("f_eps", [P, 2]), sb("f_power", [P, 2])
        logits = sb("f_logits", [P, TILES, E])
        w12 = sb("f_w12", [P, E, D])
        bias = sb("f_bias", [P, TILES, D])
        coef = sb("f_coef", [P, TILES, E])
        w1_sb, w2_sb = sb("f_w1", [P, E, FC, D]), sb("f_w2", [P, E, FC, D])
        b1_sb, b2_rows = sb("f_b1", [P, E, FC]), sb("f_b2", [P, D])
        mask_sb, falling_sb = sb("f_mask", [P, BLOCK]), sb("f_falling", [P, E])
        experts_loaded = s.sem("f_experts_loaded")

        with ExitStack() as part:
            def sb1(name, shape, dt=F32):
                return part.enter_context(nc.sbuf_tensor(name, shape, dt))

            def ps1(name, shape):
                return part.enter_context(nc.psum_tensor(name, shape, F32))

            xin, h = sb1("fa_x", [P, RING, 2, D]), sb1("fa_h", [P, 2, D])
            h_biased = sb1("fa_h_biased", [P, RING, 2, D])
            stats, mv = sb1("fa_stats", [P, 2, 2, 6]), sb1("fa_mean_var", [P, 2, 2, 2])
            scaled = sb1("fa_scaled", [P, 2, 2, D])
            shifted, rstd = sb1("fa_shifted", [P, 2, 2]), sb1("fa_rstd", [P, 2, 2])
            hT, kT = sb1("fa_hT", [P, 2, P]), sb1("fa_kT", [P, 2, P])
            qT = sb1("fa_qT", [P, NH, 2, P])
            v1 = sb1("fa_v1", [P, RING, 2, NH, W])
            ident_r, other_r = sb1("fa_ident_r", [P, P], F32R), sb1("fa_other_r", [P, P], F32R)
            score, top = sb1("fa_score", [P, NH, 2, P]), sb1("fa_top", [P, NH, 2])
            prob, probT = sb1("fa_prob", [P, NH, 2, P]), sb1("fa_probT", [P, NH, 2, P])
            rden, o, oT = sb1("fa_rden", [P, 2, NH]), sb1("fa_o", [P, 2, D]), sb1("fa_oT", [P, 2, P])
            z, y1, y1T = sb1("fa_z", [P, 2, D]), sb1("fa_y1", [P, 2, D]), sb1("fa_y1T", [P, 2, P])
            s_ps, probT_ps = ps1("fa_s_ps", [P, 2, 512]), ps1("fa_probT_ps", [P, 2, 512])
            t_ps, qk_ps = ps1("fa_t_ps", [P, 2, 2, P]), ps1("fa_qk_ps", [P, 2, 2 * P])
            r1_ps, r2_ps = ps1("fa_r1_ps", [P, 2, 2, D]), ps1("fa_r2_ps", [P, 512])
            s_of, probT_of = (a[:, :, :].rearrange("p b (h t k) -> p (b h) t k", h=2, t=2) for a in (s_ps, probT_ps))
            hT_ps, oT_ps, y1T_ps = t_ps[:, 0], t_ps[:, 1], t_ps[:, 1]
            v_ps, mha_ps = r1_ps[:, 0], r1_ps[:, 1]
            o_ps = r2_ps[:, 0:2 * NH * W].rearrange("p (t h d) -> p t h d", t=2, h=NH)
            logit_ps = r2_ps[:, 2 * NH * W:2 * NH * W + 2 * E].rearrange("p (t e) -> p t e", t=2)

            def sig(name):
                return Signal(s, "fa_" + name)

            loaded, ready, rounded = s.sem("fa_loaded"), s.sem("fa_ready"), s.sem("fa_rounded")
            dve_steps, pool_steps, settled = s.sem("fa_dve_steps"), s.sem("fa_pool_steps"), s.sem("fa_settled")
            x_in = [sig(f"x_in{k}") for k in range(RING)]
            mv_done, rstd_done = [sig(f"mv_done{k}") for k in range(2)], [sig(f"rstd_done{k}") for k in range(2)]
            h_done, h_biased_done, hT_ps_done, hT_done = sig("h_done"), sig("h_biased_done"), sig("hT_ps_done"), sig("hT_done")
            qk_ps_done, v_ps_done, qk_done, v_done = sig("qk_ps_done"), sig("v_ps_done"), sig("qk_done"), sig("v_done")
            s_ps_done, shifted_done, prob_done = sig("s_ps_done"), sig("shifted_done"), sig("prob_done")
            probT_ps_done, probT_done, o_ps_done, o_done = sig("probT_ps_done"), sig("probT_done"), sig("o_ps_done"), sig("o_done")
            oT_ps_done, oT_done, mha_ps_done, z_done = sig("oT_ps_done"), sig("oT_done"), sig("mha_ps_done"), sig("z_done")
            z_scaled_done = sig("z_scaled_done")
            y1_done, y1T_ps_done, y1T_done = sig("y1_done"), sig("y1T_ps_done"), sig("y1T_done")
            logit_ps_done, logit_done = sig("logit_ps_done"), sig("logit_done")
            y1_stored, y1T_stored = sig("y1_stored"), sig("y1T_stored")
            LOADS = 15

            def rounds(eng, body):
                def with_stages(i, b):
                    body(i, b, [x for x, ahead in zip("ASOZTR", (2, 1, 0, -1, -2, -3)) if in_range(i, b + ahead, RING)])

                all_rounds(eng, RING, with_stages, 3)

            with nc.Block() as block:

                @block.sync
                def _(sp):
                    def load(n, slot):
                        for t in range(2):
                            x_in[slot].mark(sp.dma_start(xin[:, slot, t, :], x_t[n * 2 + t]), 16)

                    load(0, 0)
                    for dst, src in ((consts[:, :, :], mods[M1_SHIFT2:M1_BIAS2 + 1].rearrange("m p d -> p m d")),
                                     (in_w_sb[:, :], in_w), (out_w_sb[:, :], out_w), (wg_sb[:, :], wg),
                                     (in_b_sb[:, 0:1], in_b[0:D].rearrange("(p a) -> p a", a=1)),
                                     (in_b_sb[:, 1:2], in_b[D:2 * D].rearrange("(p a) -> p a", a=1)),
                                     (ident_sb[:, :], ident), (upto_sb[:, :], upto), (same_sb[:, :], same_batch),
                                     (before_sb[:, :], batch_before), (other_sb[:, :], other_position),
                                     (rows[:, 0, :], in_b[2 * D:3 * D].rearrange("(a d) -> a d", a=1).to_broadcast([P, D])),
                                     (rows[:, 1, :], out_b.rearrange("(a d) -> a d", a=1).to_broadcast([P, D])),
                                     (rows[:, 2, :], ln1_g.rearrange("(a d) -> a d", a=1).to_broadcast([P, D])),
                                     (rows[:, 3, :], ln1_b.rearrange("(a d) -> a d", a=1).to_broadcast([P, D]))):
                        sp.dma_start(dst, src).then_inc(loaded, 16)

                    for dst, src in ((w1_sb[:, :, :, :], w1.rearrange("e (c p) d -> p e c d", p=P)),
                                     (w2_sb[:, :, :, :], w2.rearrange("e (c p) d -> p e c d", p=P)),
                                     (b1_sb[:, :, :].rearrange("p e c -> p (e c)"), b1),
                                     (b2_rows[:, :], b2.unsqueeze(0).to_broadcast([BLOCK, E, D])),
                                     (mask_sb[:, :], tile_mask), (falling_sb[:, :], falling)):
                        sp.dma_start(dst, src).then_inc(experts_loaded, 16)

                    def body(i, b, stages):
                        n = i * RING + b
                        if in_range(i, b + 3, RING) and not (isinstance(n, int) and n == -3):
                            h_done.wait(sp, n)
                            load(n + 3, (b + 3) % RING)
                        if "T" in stages:
                            y1_done.wait(sp, n - 1)
                            y1_stored.mark(sp.dma_start(y1_dram[n - 2], y1[:, :, :]), 16)
                            y1T_done.wait(sp, n - 1)
                            y1T_stored.mark(sp.dma_start(y1T_dram[n - 2], y1T[:, :, :]), 16)

                    rounds(sp, body)
                    y1_stored.wait(sp, PAIRS * 16)
                    y1T_stored.wait(sp, PAIRS * 16)

                @block.gpsimd
                def _(pool):
                    pool.memset(eps[:, :], EPS_LN)
                    pool.memset(power[:, :], -0.5)
                    pool.memset(qT[:, :, :, :], 0.0)
                    pool.memset(v1[:, :, :, :, :], 1.0).then_inc(ready, 1)
                    pool.wait_ge(ready, 1)
                    pool.wait_ge(loaded, LOADS * 16)
                    steps = Steps(pool, pool_steps)

                    def root(k, n):
                        mv_done[k].wait(pool, n + 1)
                        steps.wait(steps.mark(pool.tensor_tensor(shifted[:, k, :], mv[:, k, :, 1], eps[:, :], ALU.add)))
                        rstd_done[k].mark(pool.tensor_tensor(rstd[:, k, :], shifted[:, k, :], power[:, :], ALU.pow))

                    def body(i, b, stages):
                        n = i * RING + b
                        steps.start(pairs_done(n + 2) + pairs_done(n - 1) if isinstance(n, int) else n * 2 + 1)
                        if "A" in stages:
                            root(0, n + 2)
                            h_done.wait(pool, n + 3)
                            z_done.wait(pool, n - 1)
                            h_biased_done.mark(pool.tensor_tensor(h_biased[:, (b + 2) % RING], h[:, :, :], two(rows[:, 1, :]), ALU.add))
                        if "Z" in stages:
                            root(1, n - 1)

                    rounds(pool, body)

                @block.scalar
                def _(act):
                    act.wait_ge(loaded, LOADS * 16)
                    act.wait_ge(ready, 1)

                    def body(i, b, stages):
                        n = i * RING + b
                        if "O" in stages:
                            probT_ps_done.wait(act, n + 1)
                            o_ps_done.wait(act, n)
                            probT_done.mark(act.copy(probT[:, :, :, :].rearrange("p (b h) t k -> p b (h t k)", h=2), probT_ps[:, :, :]))
                        if "Z" in stages:
                            oT_ps_done.wait(act, n)
                            mha_ps_done.wait(act, n - 1)
                            oT_done.mark(act.copy(oT[:, :, :], oT_ps))
                        if "A" in stages:
                            hT_ps_done.wait(act, n + 3)
                            v_ps_done.wait(act, n + 2)
                            hT_done.mark(act.copy(hT[:, :, :], hT_ps))
                        if "S" in stages:
                            shifted_done.wait(act, n + 2)
                            probT_ps_done.wait(act, n + 1)
                            prob_done.mark(act.activation(prob[:, :, :, :], score[:, :, :, :], ACT.Exp, scale=SCALE))
                        if "A" in stages:
                            qk_ps_done.wait(act, n + 3)
                            s_ps_done.wait(act, n + 2)
                            for hd in range(NH):
                                of = slice(DH * hd, DH * hd + DH)
                                act.activation(qT[of, hd].rearrange("p t k -> p (t k)"), qk_ps[of, 0, :], ACT.Identity,
                                               bias=in_b_sb[of, 0:1])
                            last = act.activation(kT[:, :, :].rearrange("p t k -> p (t k)"), qk_ps[:, 1, :], ACT.Identity,
                                                  bias=in_b_sb[:, 1:2])
                            qk_done.mark(last)
                        if "T" in stages:
                            y1T_ps_done.wait(act, n - 1)
                            logit_ps_done.wait(act, n - 2)
                            y1T_stored.wait(act, (n - 2) * 16)
                            y1T_done.mark(act.copy(y1T[:, :, :], y1T_ps))

                    rounds(act, body)

                @block.tensor
                def _(pe):
                    pe.wait_ge(loaded, LOADS * 16)
                    pe.wait_ge(rounded, 1)

                    def turn(dst, src, done):
                        for t in range(2):
                            last = pe.transpose(dst[:, t, :], src[:, t, :], ident_sb[:, :])
                        done.mark(last)

                    def body(i, b, stages):
                        n = i * RING + b
                        if "O" in stages:
                            prob_done.wait(pe, n + 1)
                            probT_done.wait(pe, n)
                            for t in range(2):
                                for hd in range(NH):
                                    last = pe.transpose(probT_of[:, hd, t, :], prob[:, hd, t, :], ident_sb[:, :])
                            probT_ps_done.mark(last)
                        if "Z" in stages:
                            o_done.wait(pe, n)
                            hT_done.wait(pe, pairs_done(n + 2))
                            y1T_done.wait(pe, n - 2)
                            turn(oT_ps, o, oT_ps_done)
                        if "S" in stages:
                            qk_done.wait(pe, n + 2)
                            shifted_done.wait(pe, n + 1)
                            for k in range(2):
                                pe.matmul(s_ps[:, k, :].rearrange("p (a k) -> p a k", k=P), ident_r[:, :],
                                          other_r[:, :].unsqueeze(1).to_broadcast([P, 4, P]), start=True, stop=False)
                                for hd in (2 * k, 2 * k + 1):
                                    for t in range(2):
                                        last = pe.matmul(s_of[:, hd, t, :], qT[:, hd, t, :], kT[:, t, :],
                                                         start=False, stop=hd % 2 == t == 1)
                            s_ps_done.mark(last)
                        if "R" in stages:
                            y1T_done.wait(pe, n - 2)
                            logit_done.wait(pe, n - 3)
                            o_done.wait(pe, pairs_done(n))
                            for t in range(2):
                                last = pe.matmul(logit_ps[:, t, :], y1T[:, t, :], wg_sb[:, :], start=True, stop=True)
                            logit_ps_done.mark(last)
                        if "A" in stages:
                            h_done.wait(pe, n + 3)
                            hT_done.wait(pe, n + 2)
                            oT_done.wait(pe, n)
                            y1T_done.wait(pe, n - 2)
                            turn(hT_ps, h, hT_ps_done)
                        if "O" in stages:
                            probT_done.wait(pe, n + 1)
                            v_done.wait(pe, n + 1)
                            o_done.wait(pe, n)
                            logit_done.wait(pe, pairs_done(n - 2))
                            for t in range(2):
                                for hd in range(NH):
                                    last = pe.matmul(o_ps[:, t, hd, :], probT[:, hd, t, :], v1[:, b, t, hd, :], start=True, stop=True)
                            o_ps_done.mark(last)
                        if "Z" in stages:
                            oT_done.wait(pe, n)
                            z_done.wait(pe, n - 1)
                            v_done.wait(pe, pairs_done(n + 2))
                            for t in range(2):
                                last = pe.matmul(mha_ps[:, t, :], oT[:, t, :], out_w_sb[:, :], start=True, stop=True)
                            mha_ps_done.mark(last)
                        if "A" in stages:
                            hT_done.wait(pe, n + 3)
                            qk_done.wait(pe, n + 2)
                            for k in range(2):
                                last = pe.matmul(qk_ps[:, k, :], in_w_sb[:, k * D:(k + 1) * D],
                                                 hT[:, :, :].rearrange("p t k -> p (t k)"), start=True, stop=True)
                            qk_ps_done.mark(last)
                        if "T" in stages:
                            y1_done.wait(pe, n - 1)
                            oT_done.wait(pe, pairs_done(n))
                            hT_done.wait(pe, pairs_done(n + 3))
                            y1T_done.wait(pe, n - 2)
                            turn(y1T_ps, y1, y1T_ps_done)
                        if "A" in stages:
                            v_done.wait(pe, n + 2)
                            z_done.wait(pe, n)
                            for t in range(2):
                                last = pe.matmul(v_ps[:, t, :], hT[:, t, :], in_w_sb[:, 2 * D:3 * D], start=True, stop=True)
                            v_ps_done.mark(last)

                    rounds(pe, body)

                @block.vector
                def _(dve):
                    dve.wait_ge(loaded, LOADS * 16)
                    dve.wait_ge(ready, 1)
                    dve.tensor_copy(ident_r[:, :], ident_sb[:, :])
                    dve.tensor_copy(other_r[:, :], other_sb[:, :]).then_inc(rounded, 1)
                    steps = Steps(dve, dve_steps)

                    class Norm:

                        def __init__(self, k, n, src, gain):
                            self.k, self.n, self.src, self.gain = k, n, src, gain

                        def mean(self):
                            for t in range(2):
                                last = dve.bn_stats(stats[:, self.k, t, :], self.src[:, t, :])
                            steps.wait(steps.mark(last))
                            settle(dve, settled)
                            for t in range(2):
                                last = dve.bn_aggr(mv[:, self.k, t, :], stats[:, self.k, t, :])
                            mv_done[self.k].mark(last)

                        def scale(self):
                            mv_done[self.k].wait(dve, self.n + 1)
                            for t in range(2):
                                last = dve.scalar_tensor_tensor(scaled[:, self.k, t, :], self.src[:, t, :],
                                                                mv[:, self.k, t, 0:1], self.gain, ALU.subtract, ALU.mult)
                            return last

                        def finish(self, dst, shift):
                            rstd_done[self.k].wait(dve, self.n + 1)
                            for t in range(2):
                                last = dve.scalar_tensor_tensor(dst[:, t, :], scaled[:, self.k, t, :], rstd[:, self.k, t:t + 1],
                                                                shift, ALU.mult, ALU.add)
                            return last

                    sizes = dict(A=(2, 2), S=(1, 1), O=(1, 0), Z=(1, -1))

                    def body(i, b, stages):
                        n = i * RING + b
                        if isinstance(n, int):
                            steps.start(sum(size * pairs_done(n + ahead) for size, ahead in sizes.values()))
                        else:
                            steps.start(n * sum(size for size, _ in sizes.values())
                                        + sum(size * ahead for size, ahead in sizes.values()))
                        if "A" in stages:
                            slot = (b + 2) % RING
                            x_in[slot].wait(dve, 32 * (i + (b + 2) // RING) + 32)
                            norm0 = Norm(0, n + 2, xin[:, slot], consts[:, 1, :])
                            norm0.mean()
                            scaled_at = steps.mark(norm0.scale())
                        if "T" in stages:
                            norm1 = Norm(1, n - 2, z, rows[:, 2, :])
                            z_scaled_done.wait(dve, n - 1)
                            y1T_ps_done.wait(dve, n - 2)
                            y1_stored.wait(dve, 16 * (n - 2))
                            y1_done.mark(norm1.finish(y1, rows[:, 3, :]))
                        if "A" in stages:
                            steps.wait(scaled_at)
                            hT_ps_done.wait(dve, n + 2)
                            h_biased_done.wait(dve, n + 2)
                            h_done.mark(norm0.finish(h, consts[:, 0, :]))
                        if "R" in stages:
                            logit_ps_done.wait(dve, n - 2)
                            logit_done.mark(dve.tensor_copy(logits[:, bass.ds((n - 3) * 2, 2), :], logit_ps))
                        if "S" in stages:
                            s_ps_done.wait(dve, n + 2)
                            top_at = steps.mark(dve.tensor_reduce(top[:, :, :], s_of, AX.X, ALU.max))
                        if "S" in stages:
                            steps.wait(top_at)
                            prob_done.wait(dve, n + 1)
                            shifted_done.mark(dve.tensor_tensor(
                                score[:, :, :, :], s_of, top[:, :, :].unsqueeze(3).to_broadcast([P, NH, 2, P]), ALU.subtract))
                        if "O" in stages:
                            o_ps_done.wait(dve, n + 1)
                            rden_at = steps.mark(dve.reciprocal(rden[:, :, :], o_ps[:, :, :, DH]))
                        if "Z" in stages:
                            mha_ps_done.wait(dve, n)
                            h_biased_done.wait(dve, n)
                            z_done.mark(dve.tensor_tensor(z[:, :, :], mha_ps, h_biased[:, (b - 1) % RING], ALU.add))
                        if "O" in stages:
                            steps.wait(rden_at)
                            oT_ps_done.wait(dve, n)
                            o_done.mark(dve.tensor_tensor(o[:, :, :].rearrange("p t (h d) -> p t h d", h=NH), o_ps[:, :, :, 0:DH],
                                                          rden[:, :, :].unsqueeze(3).to_broadcast([P, 2, NH, DH]), ALU.mult))
                        if "Z" in stages:
                            z_done.wait(dve, n)
                            norm1 = Norm(1, n - 1, z, rows[:, 2, :])
                            norm1.mean()
                            y1_done.wait(dve, n - 1)
                            z_scaled_done.mark(norm1.scale())
                        if "A" in stages:
                            v_ps_done.wait(dve, n + 3)
                            o_ps_done.wait(dve, n - 1)
                            v_done.mark(dve.tensor_tensor(
                                v1[:, slot, :, :, 0:DH], v_ps.rearrange("p t (h d) -> p t h d", h=NH),
                                two(rows[:, 0, :]).rearrange("p t (h d) -> p t h d", h=NH), ALU.add))

                    rounds(dve, body)

        RING3 = 4
        xin, y1, y1T = s.sb("fc_x", [P, RING3, 2, D]), s.sb("fc_y1", [P, RING3, 2, D]), s.sb("fc_y1T", [P, RING3, 2, P])
        ins_done = [Signal(s, f"fc_in{k}") for k in range(RING3)]

        def load_pair(sp, n, slot):
            ins_done[slot].mark(sp.dma_start(y1T[:, slot], y1T_dram[n]), 16)
            ins_done[slot].mark(sp.dma_start(y1[:, slot], y1_dram[n]), 16)
            for t in range(2):
                ins_done[slot].mark(sp.dma_start(xin[:, slot, t, :], x_t[n * 2 + t]), 16)

        with ExitStack() as part:
            def sb2(name, shape, dt=F32):
                return part.enter_context(nc.sbuf_tensor(name, shape, dt))

            def ps2(name, shape):
                return part.enter_context(nc.psum_tensor(name, shape, F32))

            b12 = sb2("fb_b12", [P, D])
            b1_of = sb2("fb_b1_of", [P, E, FC, BLOCK, E])
            b12_of = sb2("fb_b12_of", [P, BLOCK, D])
            top, ex, total = sb2("fb_top", [P, TILES]), sb2("fb_exp", [P, TILES, E]), sb2("fb_sum", [P, TILES])
            rtotal, gates, gate = sb2("fb_rsum", [P, TILES]), sb2("fb_gates", [P, TILES, E]), sb2("fb_gate", [P, TILES])
            rank, first = sb2("fb_rank", [P, TILES, E]), sb2("fb_first", [P, TILES])
            chosen, of_batch = sb2("fb_chosen", [P, TILES, E]), sb2("fb_of_batch", [P, E])
            tile_counts, running = sb2("fb_tile_counts", [P, TILES, E]), sb2("fb_running", [P, TILES, E])
            zero, place, kept = sb2("fb_zero", [P, TILES]), sb2("fb_place", [P, TILES, E]), sb2("fb_kept", [P, TILES, E])
            coefT = sb2("fb_coefT", [P, TILES // BLOCK, P])
            w_ps, within_ps, tile_ps, before_ps = ps2("fb_w_ps", [P, 2, 512]), ps2("fb_within_ps", [P, 512]), ps2("fb_tile_ps", [P, 512]), ps2("fb_before_ps", [P, 512])
            b_ps, bias_ps = ps2("fb_b_ps", [P, 512]), ps2("fb_bias_ps", [P, 2, 512])
            ready, dve_steps = s.sem("fb_ready"), s.sem("fb_dve_steps")
            shifted_done, exp_done, chosen_done, of_batch_done = s.sem("fb_shifted_done"), s.sem("fb_exp_done"), s.sem("fb_chosen_done"), s.sem("fb_of_batch_done")
            counts_done, b1_of_done, w12_ps_done, b12_ps_done = s.sem("fb_counts_done"), s.sem("fb_b1_of_done"), s.sem("fb_w12_ps_done"), s.sem("fb_b12_ps_done")
            b12_of_done, coef_done, coefT_ps_done, coefT_done = s.sem("fb_b12_of_done"), s.sem("fb_coef_done"), s.sem("fb_coefT_ps_done"), s.sem("fb_coefT_done")
            bias_ps_done, bias_done = s.sem("fb_bias_ps_done"), s.sem("fb_bias_done")
            with nc.Block() as block:

                @block.sync
                def _(sp):
                    for n in range(2):
                        load_pair(sp, n, n)

                @block.gpsimd
                def _(pool):
                    pool.memset(zero[:, :], 0.0)
                    pool.memset(b1_of[:, :, :, :, :], 0.0).then_inc(ready, 1)
                    pool.wait_ge(ready, 1)
                    pool.wait_ge(experts_loaded, 6 * 16)
                    for e in range(E):
                        last = pool.tensor_copy(b1_of[:, e, :, :, e], b1_sb[:, e, :].unsqueeze(2).to_broadcast([P, FC, BLOCK]))
                    last.then_inc(b1_of_done, 1)

                @block.scalar
                def _(act):
                    act.wait_ge(shifted_done, 1)
                    act.activation(ex[:, :, :], ex[:, :, :], ACT.Exp).then_inc(exp_done, 1)
                    act.wait_ge(w12_ps_done, 1)
                    act.copy(w12[:, :, :].rearrange("p (a e) d -> p a (e d)", a=2), w_ps[:, :, :])
                    act.wait_ge(coefT_ps_done, 1)
                    act.copy(coefT[:, :, :].rearrange("p a b -> p (a b)"), within_ps[:, :]).then_inc(coefT_done, 1)
                    for k in range(TILES // 4):
                        act.wait_ge(bias_ps_done, k + 1)
                        act.copy(bias[:, 4 * k:4 * k + 4, :].rearrange("p t d -> p (t d)"),
                                 bias_ps[:, k % 2, :]).then_inc(bias_done, 1)

                @block.tensor
                def _(pe):
                    pe.wait_ge(experts_loaded, 6 * 16)
                    for e in range(E):
                        for c in range(FC):
                            last = pe.matmul(w_ps[:, e // 4, (e % 4) * D:(e % 4) * D + D], w1_sb[:, e, c, :], w2_sb[:, e, c, :],
                                             start=c == 0, stop=c == FC - 1)
                    last.then_inc(w12_ps_done, 1)
                    pe.wait_ge(chosen_done, 1)
                    flat = chosen[:, :, :].rearrange("p t e -> p (t e)")
                    pe.matmul(within_ps[:, :], upto_sb[:, :], flat, start=True, stop=True)
                    pe.matmul(tile_ps[:, :], same_sb[:, :], flat, start=True, stop=True)
                    pe.wait_ge(of_batch_done, 1)
                    pe.matmul(before_ps[:, 0:E], before_sb[:, :], of_batch[:, :], start=True, stop=True).then_inc(counts_done, 1)
                    pe.wait_ge(b1_of_done, 1)
                    for e in range(E):
                        for c in range(FC):
                            last = pe.matmul(b_ps[:, 0:D], b1_of[:, e, c].rearrange("p a b -> p (a b)"), w2_sb[:, e, c, :],
                                             start=e == c == 0, stop=(e, c) == (E - 1, FC - 1))
                    last.then_inc(b12_ps_done, 1)
                    pe.wait_ge(coef_done, 1)
                    for k in range(TILES // BLOCK):
                        last = pe.transpose(within_ps[:, k * P:k * P + P],
                                            coef[:, k * BLOCK:(k + 1) * BLOCK, :].rearrange("p t e -> p (t e)"), ident_sb[:, :])
                    last.then_inc(coefT_ps_done, 1)
                    pe.wait_ge(coefT_done, 1)
                    pe.wait_ge(b12_of_done, 1)
                    for k in range(TILES // 4):
                        if k >= 2:
                            pe.wait_ge(bias_done, k - 1)
                        j = 4 * k
                        pe.matmul(bias_ps[:, k % 2, :], coefT[:, j // BLOCK, :],
                                  b12_of[:, j % BLOCK:j % BLOCK + 4, :].rearrange("p t d -> p (t d)"),
                                  start=True, stop=True).then_inc(bias_ps_done, 1)

                @block.vector
                def _(dve):
                    link = Chain(dve, dve_steps)
                    step = link.then

                    def each(a):
                        return a.unsqueeze(2).to_broadcast([P, TILES, E])

                    step(dve.tensor_reduce(top[:, :], logits[:, :, :], AX.X, ALU.max))
                    dve.tensor_tensor(ex[:, :, :], logits[:, :, :], each(top[:, :]), ALU.subtract).then_inc(shifted_done, 1)
                    dve.wait_ge(exp_done, 1)
                    step(dve.tensor_reduce(total[:, :], ex[:, :, :], AX.X, ALU.add))
                    step(dve.reciprocal(rtotal[:, :], total[:, :]))
                    step(dve.tensor_tensor(gates[:, :, :], ex[:, :, :], each(rtotal[:, :]), ALU.mult))
                    step(dve.tensor_reduce(gate[:, :], gates[:, :, :], AX.X, ALU.max))
                    step(dve.tensor_tensor(rank[:, :, :], gates[:, :, :], each(gate[:, :]), ALU.is_equal))
                    dve.wait_ge(experts_loaded, 6 * 16)
                    step(dve.tensor_tensor(rank[:, :, :], rank[:, :, :],
                                           falling_sb[:, :].unsqueeze(1).to_broadcast([P, TILES, E]), ALU.mult))
                    step(dve.tensor_reduce(first[:, :], rank[:, :, :], AX.X, ALU.max))
                    ins = dve.tensor_tensor(chosen[:, :, :], rank[:, :, :], each(first[:, :]), ALU.is_equal)
                    ins.then_inc(chosen_done, 1)
                    dve.wait_ge(chosen_done, 1)
                    dve.tensor_reduce(of_batch[:, :], chosen[:, :, :].rearrange("p t e -> p e t"), AX.X, ALU.add).then_inc(of_batch_done, 1)
                    dve.wait_ge(counts_done, 1)
                    dve.wait_ge(ready, 1)
                    step(dve.tensor_copy(tile_counts[:, :, :].rearrange("p t e -> p (t e)"), tile_ps[:, :]))
                    for e in range(E):
                        last = dve.tensor_tensor_scan(running[:, :, e], tile_counts[:, :, e], zero[:, :], 0.0, ALU.add, ALU.add)
                    step(last)
                    step(dve.tensor_tensor(running[:, :, :], running[:, :, :], tile_counts[:, :, :], ALU.subtract))
                    step(dve.tensor_tensor(place[:, :, :].rearrange("p t e -> p (t e)"), within_ps[:, :],
                                           running[:, :, :].rearrange("p t e -> p (t e)"), ALU.add))
                    step(dve.tensor_copy(of_batch[:, :], before_ps[:, 0:E]))
                    step(dve.tensor_tensor(place[:, :, :], place[:, :, :], of_batch[:, :].unsqueeze(1).to_broadcast([P, TILES, E]), ALU.add))
                    step(dve.scalar_tensor_tensor(kept[:, :, :].rearrange("p t e -> p (t e)"),
                                                  place[:, :, :].rearrange("p t e -> p (t e)"), float(CAP),
                                                  chosen[:, :, :].rearrange("p t e -> p (t e)"), ALU.is_le, ALU.mult))
                    dve.tensor_tensor(coef[:, :, :], kept[:, :, :], each(gate[:, :]), ALU.mult).then_inc(coef_done, 1)
                    dve.wait_ge(b12_ps_done, 1)
                    step(dve.tensor_tensor(b12[:, :], b_ps[:, 0:D], b2_rows[:, :], ALU.add))
                    dve.tensor_tensor(b12_of[:, :, :], b12[:, :].unsqueeze(1).to_broadcast([P, BLOCK, D]),
                                      mask_sb[:, :].unsqueeze(2).to_broadcast([P, BLOCK, D]), ALU.mult).then_inc(b12_of_done, 1)

        with ExitStack() as part:
            def sb3(name, shape, dt=F32):
                return part.enter_context(nc.sbuf_tensor(name, shape, dt))

            HALF_E = E // 2
            base, acc, y = sb3("fc_base", [P, 2, 2, D]), sb3("fc_acc", [P, 2, 2, D]), sb3("fc_y", [P, 2, 2, D])
            part_e, part_2, part_1 = sb3("fc_part_e", [P, 2, 2, HALF_E, D]), sb3("fc_part_2", [P, 2, 2, D]), sb3("fc_part_1", [P, 2, 2, D])
            biased, scaled, total_y = sb3("fc_biased", [P, 2, 2, D]), sb3("fc_scaled", [P, 2, D]), sb3("fc_total", [P, 2, D])
            stats, mv = sb3("fc_stats", [P, 2, 6]), sb3("fc_mean_var", [P, 2, 2])
            std, rstd = sb3("fc_std", [P, 2]), sb3("fc_rstd", [P, 2])
            e_ps = part.enter_context(nc.psum_tensor("fc_e_ps", [P, 4, 2, 512], F32))

            def sig(name):
                return Signal(s, "fc_" + name)

            y_stored = [sig(f"y_stored{k}") for k in range(2)]
            e_done, added, scaled_done = sig("e_done"), sig("added"), sig("scaled_done")
            base_done, part_done, biased_done, total_done = sig("base_done"), sig("part_done"), sig("biased_done"), sig("total_done")
            mv_done, std_done, y_done = sig("mv_done"), sig("std_done"), sig("y_done")
            dve_steps, pool_steps, settled = s.sem("fc_dve_steps"), s.sem("fc_pool_steps"), s.sem("fc_settled")

            def rounds(eng, body):
                def with_stages(i, b):
                    body(i, b, [x for x, ahead in zip("EN", (0, -1)) if in_range(i, b + ahead, RING3)])

                all_rounds(eng, RING3, with_stages, 1)

            with nc.Block() as block:

                @block.sync
                def _(sp):
                    def body(i, b, stages):
                        n = i * RING3 + b
                        if in_range(i, b + 3, RING3):
                            added.wait(sp, n)
                            base_done.wait(sp, n)
                            biased_done.wait(sp, n)
                            load_pair(sp, n + 3, (b + 3) % RING3)
                        if "N" in stages:
                            y_done.wait(sp, n)
                            for t in range(2):
                                y_stored[(b - 1) % 2].mark(sp.dma_start(out_t[(n - 1) * 2 + t], y[:, (b - 1) % 2, t, :]), 16)

                    rounds(sp, body)
                    for k in range(2):
                        y_stored[k].wait(sp, PAIRS // 2 * 32)

                @block.gpsimd
                def _(pool):
                    steps = Steps(pool, pool_steps)

                    def body(i, b, stages):
                        n = i * RING3 + b
                        steps.start(pairs_done(n))
                        if "E" in stages:
                            k = b % 2
                            ins_done[b].wait(pool, 64 * i + 64)
                            added.wait(pool, n - 1)
                            base_done.mark(pool.tensor_tensor(base[:, k], y1[:, b], bias[:, bass.ds(n * 2, 2), :], ALU.add))
                            y_done.wait(pool, n - 1)
                            biased_done.mark(pool.tensor_tensor(biased[:, k], xin[:, b], two(consts[:, 3, :]), ALU.add))
                            scaled_done.wait(pool, n + 1)
                            part_done.wait(pool, n)
                            part_at = steps.mark(pool.tensor_tensor(part_2[:, :, :, :], part_e[:, k, :, 0:2], part_e[:, k, :, 2:4], ALU.add))
                            steps.wait(part_at)
                            total_done.wait(pool, n - 1)
                            part_done.mark(pool.tensor_tensor(part_1[:, k], part_2[:, :, 0], part_2[:, :, 1], ALU.add))

                    rounds(pool, body)

                @block.scalar
                def _(act):
                    def body(i, b, stages):
                        n = i * RING3 + b
                        if "E" in stages:
                            k = b % 2
                            part_done.wait(act, n - 1)
                            for t in range(2):
                                e_done.wait(act, 2 * n + t + 1)
                                for e in range(HALF_E, E):
                                    last = act.activation(part_e[:, k, t, e - HALF_E, :], e_ps[:, 2 * k + t, 1, (e - HALF_E) * D:(e - HALF_E) * D + D],
                                                          ACT.Copy, scale=coef[:, bass.ds(n * 2 + t, 1), e])
                            scaled_done.mark(last)
                        if "N" in stages:
                            mv_done.wait(act, n)
                            std_done.mark(act.activation(std[:, :], mv[:, :, 1], ACT.Sqrt, bias=eps[:, 0:1]))

                    rounds(act, body)

                @block.tensor
                def _(pe):
                    def body(i, b, stages):
                        n = i * RING3 + b
                        if "E" in stages:
                            ins_done[b].wait(pe, 64 * i + 64)
                            scaled_done.wait(pe, n - 1)
                            added.wait(pe, n - 1)
                            for t in range(2):
                                for k in range(2):
                                    last = pe.matmul(e_ps[:, 2 * (b % 2) + t, k, :], y1T[:, b, t, :],
                                                     w12[:, HALF_E * k:HALF_E * k + HALF_E, :].rearrange("p e d -> p (e d)"),
                                                     start=True, stop=True)
                                e_done.mark(last)

                    rounds(pe, body)

                @block.vector
                def _(dve):
                    steps = Steps(dve, dve_steps)
                    SUM, NORM = HALF_E - 1, 3

                    def body(i, b, stages):
                        n = i * RING3 + b
                        steps.start(pairs_done(n) * SUM + pairs_done(n - 1) * NORM)
                        k, before = b % 2, (b - 1) % 2
                        for e in range(HALF_E):
                            if "E" in stages:
                                if e == 0:
                                    base_done.wait(dve, n + 1)
                                    total_done.wait(dve, n - 1)
                                else:
                                    steps.wait(added_at)
                                for t in range(2):
                                    if e == 0:
                                        e_done.wait(dve, 2 * n + t + 1)
                                    last = dve.scalar_tensor_tensor(
                                        acc[:, k, t, :], e_ps[:, 2 * k + t, 0, e * D:e * D + D],
                                        coef[:, bass.ds(n * 2 + t, 1), e], acc[:, k, t, :] if e else base[:, k, t, :],
                                        ALU.mult, ALU.add)
                                if e < HALF_E - 1:
                                    added_at = steps.mark(last)
                                else:
                                    added.mark(last)
                            if "N" in stages:
                                if e == 0:
                                    added.wait(dve, n)
                                    part_done.wait(dve, n)
                                    total_done.mark(dve.tensor_tensor(total_y[:, :, :], acc[:, before], part_1[:, before], ALU.add))
                                elif e == 1:
                                    total_done.wait(dve, n)
                                    for t in range(2):
                                        last = dve.bn_stats(stats[:, t, :], total_y[:, t, :])
                                    stats_at = steps.mark(last)
                                elif e == 2:
                                    steps.wait(stats_at)
                                    settle(dve, settled)
                                    for t in range(2):
                                        last = dve.bn_aggr(mv[:, t, :], stats[:, t, :])
                                    mv_done.mark(last)
                                else:
                                    mv_done.wait(dve, n)
                                    for t in range(2):
                                        last = dve.scalar_tensor_tensor(scaled[:, t, :], total_y[:, t, :], mv[:, t, 0:1],
                                                                        consts[:, 2, :], ALU.subtract, ALU.mult)
                                    scaled_at = steps.mark(last)
                                    std_done.wait(dve, n)
                                    rstd_at = steps.mark(dve.reciprocal(rstd[:, :], std[:, :]))
                                    steps.wait(scaled_at)
                                    steps.wait(rstd_at)
                                    biased_done.wait(dve, n)
                                    y_stored[before].wait(dve, 32 * (i * 2 + (b - 1) // 2))
                                    for t in range(2):
                                        last = dve.scalar_tensor_tensor(y[:, before, t, :], scaled[:, t, :], rstd[:, t:t + 1],
                                                                        biased[:, before, t, :], ALU.mult, ALU.add)
                                    y_done.mark(last)

                    rounds(dve, body)


def adaln_two_layers(nc, x, L0_wqkv, L0_wo, L0_ln_g, L0_ln_b, L0_c, L0_wmod, L1_wqkv, L1_wo, L1_bo,
                     in_w, in_b, out_w, out_b, ln1_g, ln1_b, ln2_g, ln2_b, wg, w1, b1, w2, b2, L1_c, L1_wmod,
                     ident, upto, same_batch, last_of_batch, batch_before, fold, other_position, cos, sin,
                     tile_mask, falling, out):
    def scratch(name, shape):
        return nc.dram_tensor(name, shape, F32, kind="Internal").ap()

    mods = scratch("mods", (M_COUNT, P, D))
    x1, x2 = scratch("x1", (B, L, D)), scratch("x2", (B, L, D))
    y1, y1T = scratch("y1", (PAIRS, P, 2, D)), scratch("y1T", (PAIRS, D, 2, P))
    shared = Scope(nc)
    with shared.stack:
        w_hi, w_lo = (shared.sb(name, list(L1_wqkv.shape), F32R) for name in ("l1_w_hi", "l1_w_lo"))
        wo_sb = shared.sb("l1_wo", [P, L1_wo.shape[0] // P, D])
        early = Scope(nc)
        with early.stack:
            inputs = Layer0Inputs(early, x, L0_wqkv, L0_wo, ident, upto, last_of_batch, cos, sin)
            modulation(nc, L0_c, L0_wmod, L0_ln_g, L0_ln_b, L1_c, L1_wmod, L1_bo, ln2_g, ln2_b, mods, inputs)
            layer0(nc, inputs, mods, L1_wqkv, L1_wo, w_hi, w_lo, wo_sb, x1)
        layer1_attention(nc, x1, w_hi, w_lo, wo_sb, mods, ident, fold, x2)
    layer1_ffn(nc, x2, in_w, in_b, out_w, out_b, ln1_g, ln1_b, wg, w1, b1, w2, b2, mods, ident, upto, same_batch,
               batch_before, other_position, tile_mask, falling, y1, y1T, out)




def kernel(**inputs):
    import numpy as _np
    import concourse.bacc as _bacc
    from concourse import mybir as _mybir
    from concourse.bass_utils import run_bass_kernel_spmd as _run

    a = {name: _np.asarray(value) for name, value in inputs.items()}
    experts, hidden = a["L1_ffn_b1"].shape
    cos, sin = rope_tables()
    arrays = {
        "x": a["L0_attn_x"],
        "L0_wqkv": _np.concatenate([a["L0_attn_wq"], a["L0_attn_wk"], a["L0_attn_wv"]], axis=1),
        "L0_wo": a["L0_attn_wo"],
        "L0_ln_g": a["L0_ffn_ln_g"],
        "L0_ln_b": a["L0_ffn_ln_b"],
        "L0_c": a["L0_c"].T,
        "L0_wmod": a["L0_wmod"],
        "L1_wqkv": _np.concatenate([a["L1_attn_Wq"], a["L1_attn_Wk"], a["L1_attn_Wv"]], axis=1),
        "L1_wo": a["L1_attn_Wo"],
        "L1_bo": a["L1_attn_bo"],
        "in_w": a["L1_ffn_in_proj_w"].T,
        "in_b": a["L1_ffn_in_proj_b"],
        "out_w": a["L1_ffn_out_proj_w"].T,
        "out_b": a["L1_ffn_out_proj_b"],
        "ln1_g": a["L1_ffn_ln1_g"],
        "ln1_b": a["L1_ffn_ln1_b"],
        "ln2_g": a["L1_ffn_ln2_g"],
        "ln2_b": a["L1_ffn_ln2_b"],
        "wg": a["L1_ffn_wg"],
        "w1": a["L1_ffn_w1"].transpose(0, 2, 1),
        "b1": a["L1_ffn_b1"].reshape(experts, hidden // P, P).transpose(2, 0, 1).reshape(P, -1),
        "w2": a["L1_ffn_w2"],
        "b2": a["L1_ffn_b2"],
        "L1_c": a["L1_c"].T,
        "L1_wmod": a["L1_wmod"],
        "ident": IDENT,
        "upto": UPTO,
        "same_batch": SAME_BATCH,
        "last_of_batch": LAST_OF_BATCH,
        "batch_before": BATCH_BEFORE,
        "fold": FOLD,
        "other_position": OTHER_POSITION,
        "cos": cos,
        "sin": sin,
        "tile_mask": (_np.arange(P)[:, None] // experts == _np.arange(P // experts)[None, :]).astype(_np.float32),
        "falling": _np.tile(_np.arange(experts, 0, -1).astype(_np.float32), (P, 1)),
    }
    arrays = {name: _np.ascontiguousarray(value) for name, value in arrays.items()}
    nc = _bacc.Bacc("TRN2", target_bir_lowering=False, num_devices=1)
    args = {name: nc.dram_tensor(name, value.shape, _mybir.dt.from_np(value.dtype), kind="ExternalInput").ap()
            for name, value in arrays.items()}
    out = nc.dram_tensor("out", (B, L, D), F32, kind="ExternalOutput").ap()
    adaln_two_layers(nc, out=out, **args)
    r = _run(nc, [arrays], core_ids=[0])
    return r.results[0]["out"]
```
